# Optimizing a Trainium2 kernel written in Bass

```python
import numpy as np
import jax
import jax.numpy as jnp

def _softmax(x, axis=-1):
    return jax.nn.softmax(x, axis=axis)

def _gelu(x):
    return jax.nn.gelu(x, approximate=True)

def _silu(x):
    return jax.nn.silu(x)

def _sigmoid(x):
    return jax.nn.sigmoid(x)

def _layernorm(x, axis=-1, eps=1e-05):
    m = jnp.mean(x, axis=axis, keepdims=True)
    v = jnp.var(x, axis=axis, keepdims=True)
    return (x - m) / jnp.sqrt(v + eps)

def _scatter_add(tgt, idx, src, axis=0):
    return tgt.at[idx].add(src)

def _segment_sum(src, seg, n):
    return jax.ops.segment_sum(src, seg, n)
kernel_name = 'mk_gnn_resnorm_d4_gnn_r64_8304db'

def setup_inputs(seed: int=0):
    np.random.seed(seed)
    _w = jnp.asarray

    def _rec_inputs():
        import jax
        import jax.numpy as jnp
        _gk = jax.random.key(seed)
        x = -0.000202 + 1 * jax.random.normal(jax.random.fold_in(_gk, 1), (100000, 64), jnp.float32)
        src = jax.random.randint(jax.random.fold_in(_gk, 2), (25000,), 0, 100000, jnp.int32)
        dst = jax.random.randint(jax.random.fold_in(_gk, 3), (25000,), 0, 100000, jnp.int32)
        _o = jnp.argsort(dst, stable=True)
        src = src[_o]
        dst = dst[_o]
        edge_attr_16 = 1.36993e-05 + 0.999972 * jax.random.normal(jax.random.fold_in(_gk, 12), (25000, 16), jnp.float32)
        edge_attr_32 = -9.77346e-05 + 0.999888 * jax.random.normal(jax.random.fold_in(_gk, 13), (25000, 32), jnp.float32)
        edge_attr_4 = jax.random.uniform(jax.random.fold_in(_gk, 14), (25000, 4), jnp.float32, 0.0, 1)
        return (x, src, dst, edge_attr_16, edge_attr_32, edge_attr_4)
    x, src, dst, edge_attr_16, edge_attr_32, edge_attr_4 = _rec_inputs()

    def _L0_gnn_setup():
        import jax, jax.numpy as jnp
        import numpy as np
        N = 100000
        E = 20000
        D_IN = 64
        D_OUT = 64
        D_EDGE = 16
        NEG_SLOPE = 0.01
        key = jax.random.key(seed)
        ks = jax.random.split(key, 8)
        x = jax.random.normal(ks[0], (N, D_IN), dtype=jnp.float32)
        edge_attr = jax.random.normal(ks[1], (E, D_EDGE), dtype=jnp.float32)
        src = jax.random.randint(ks[2], (E,), 0, N, dtype=jnp.int32)
        dst = jax.random.randint(ks[3], (E,), 0, N, dtype=jnp.int32)
        W1 = jax.random.normal(ks[4], (D_OUT, D_IN + D_EDGE), dtype=jnp.float32) * (2.0 / (D_OUT + D_IN + D_EDGE)) ** 0.5
        W2 = jax.random.normal(ks[5], (D_OUT, D_IN), dtype=jnp.float32) * (2.0 / (D_OUT + D_IN)) ** 0.5
        attn = jax.random.normal(ks[6], (D_OUT + D_IN,), dtype=jnp.float32) * (2.0 / (1 + D_OUT + D_IN)) ** 0.5
        bias = jnp.zeros((D_OUT,), dtype=jnp.float32)
        return {'x': x, 'edge_attr': edge_attr, 'src': src, 'dst': dst, 'W1': W1, 'W2': W2, 'attn': attn, 'bias': bias}
    _L0_gnn_all = _L0_gnn_setup()
    _L0_gnn_in = {k: v for k, v in _L0_gnn_all.items() if k in ('W1', 'W2', 'attn', 'bias')}
    del _L0_gnn_all

    def _L1_gnn_setup():
        import jax, jax.numpy as jnp
        import numpy as np
        N, E, D = (100000, 25000, 64)
        L = 3
        EPS = 1e-05

        def _layer_norm(h, g, b):
            mu = jnp.mean(h, axis=-1, keepdims=True)
            var = jnp.var(h, axis=-1, keepdims=True)
            return (h - mu) * jax.lax.rsqrt(var + EPS) * g + b
        key = jax.random.key(seed)
        ks = jax.random.split(key, 8)
        s = 0.05
        return {'x': jax.random.normal(ks[0], (N, D), jnp.float32), 'edge_src': jax.random.randint(ks[1], (E,), 0, N, jnp.int32), 'edge_dst': jax.random.randint(ks[2], (E,), 0, N, jnp.int32), 'w_l': (jax.random.normal(ks[3], (L, D, D)) * s).astype(jnp.float32), 'b_l': jnp.zeros((L, D), jnp.float32), 'w_r': (jax.random.normal(ks[4], (L, D, D)) * s).astype(jnp.float32), 'gamma': jnp.ones((L, D), jnp.float32), 'beta': jnp.zeros((L, D), jnp.float32), 'w_res': (jax.random.normal(ks[5], (D, D)) * s).astype(jnp.float32), 'b_res': jnp.zeros((D,), jnp.float32), 'w_fc': (jax.random.normal(ks[6], (D, D)) * s).astype(jnp.float32), 'b_fc': jnp.zeros((D,), jnp.float32)}
    _L1_gnn_all = _L1_gnn_setup()
    _L1_gnn_in = {k: v for k, v in _L1_gnn_all.items() if k in ('w_l', 'b_l', 'w_r', 'gamma', 'beta', 'w_res', 'b_res', 'w_fc', 'b_fc')}
    del _L1_gnn_all

    def _L2_gnn_setup():
        import jax, jax.numpy as jnp
        import numpy as np
        N_NODES = 50000
        N_EDGES = 12500
        NODE_DIM = 64
        MSG_DIM = 64
        EDGE_DIM = 4
        ROUNDS = 2

        def gru_cell(a, h, W_ih, W_hh, b_ih, b_hh):
            gi = a @ W_ih + b_ih
            gh = h @ W_hh + b_hh
            i_r, i_z, i_n = jnp.split(gi, 3, axis=1)
            h_r, h_z, h_n = jnp.split(gh, 3, axis=1)
            r = jax.nn.sigmoid(i_r + h_r)
            z = jax.nn.sigmoid(i_z + h_z)
            n = jnp.tanh(i_n + r * h_n)
            return (1.0 - z) * n + z * h
        key = jax.random.key(seed)
        ks = jax.random.split(key, 10)
        in_dim = 2 * NODE_DIM + EDGE_DIM
        return {'hv': jax.random.normal(ks[0], (N_NODES, NODE_DIM), dtype=jnp.float32), 'he': jax.random.uniform(ks[1], (N_EDGES, EDGE_DIM), dtype=jnp.float32), 'W_msg': jax.random.normal(ks[2], (ROUNDS, in_dim, MSG_DIM), dtype=jnp.float32) * 0.05, 'b_msg': jax.random.normal(ks[3], (ROUNDS, MSG_DIM), dtype=jnp.float32) * 0.05, 'W_ih': jax.random.normal(ks[4], (ROUNDS, MSG_DIM, 3 * NODE_DIM), dtype=jnp.float32) * 0.05, 'W_hh': jax.random.normal(ks[5], (ROUNDS, NODE_DIM, 3 * NODE_DIM), dtype=jnp.float32) * 0.05, 'b_ih': jax.random.normal(ks[6], (ROUNDS, 3 * NODE_DIM), dtype=jnp.float32) * 0.05, 'b_hh': jax.random.normal(ks[7], (ROUNDS, 3 * NODE_DIM), dtype=jnp.float32) * 0.05, 'src': jax.random.randint(ks[8], (N_EDGES,), 0, N_NODES, dtype=jnp.int64) if jax.config.jax_enable_x64 else jax.random.randint(ks[8], (N_EDGES,), 0, N_NODES).astype(jnp.int32), 'dst': jax.random.randint(ks[9], (N_EDGES,), 0, N_NODES).astype(jnp.int32)}
    _L2_gnn_all = _L2_gnn_setup()
    _L2_gnn_in = {k: v for k, v in _L2_gnn_all.items() if k in ('W_msg', 'b_msg', 'W_ih', 'W_hh', 'b_ih', 'b_hh')}
    del _L2_gnn_all

    def _L3_gnn_setup():
        import jax, jax.numpy as jnp
        import numpy as np
        N_NODES = 100000
        N_EDGES = 25000
        NODE_F = 64
        EDGE_F = 32
        OUT_F = 64
        HIDDEN = 2 * OUT_F
        IN_F = 2 * NODE_F + EDGE_F
        key = jax.random.key(seed)
        ks = jax.random.split(key, 8)
        nodes = jax.random.normal(ks[0], (N_NODES, NODE_F), dtype=jnp.float32)
        edges = jax.random.normal(ks[1], (N_EDGES, EDGE_F), dtype=jnp.float32)
        senders = jax.random.randint(ks[2], (N_EDGES,), 0, N_NODES, dtype=jnp.int32)
        receivers = jax.random.randint(ks[3], (N_EDGES,), 0, N_NODES, dtype=jnp.int32)
        W1 = jax.random.normal(ks[4], (IN_F, HIDDEN), dtype=jnp.float32) / np.sqrt(IN_F)
        b1 = jnp.zeros((HIDDEN,), dtype=jnp.float32)
        W2 = jax.random.normal(ks[5], (HIDDEN, OUT_F), dtype=jnp.float32) / np.sqrt(HIDDEN)
        b2 = jnp.zeros((OUT_F,), dtype=jnp.float32)
        Wn = jax.random.normal(ks[6], (NODE_F, OUT_F), dtype=jnp.float32) / np.sqrt(NODE_F)
        bn = jnp.zeros((OUT_F,), dtype=jnp.float32)
        return {'nodes': nodes, 'edges': edges, 'senders': senders, 'receivers': receivers, 'W1': W1, 'b1': b1, 'W2': W2, 'b2': b2, 'Wn': Wn, 'bn': bn}
    _L3_gnn_all = _L3_gnn_setup()
    _L3_gnn_in = {k: v for k, v in _L3_gnn_all.items() if k in ('W1', 'b1', 'W2', 'b2', 'Wn', 'bn')}
    del _L3_gnn_all
    return {'x': x, 'src': src, 'dst': dst, 'edge_attr_16': edge_attr_16, 'edge_attr_32': edge_attr_32, 'edge_attr_4': edge_attr_4, 'L0_gnn_W1': _L0_gnn_in['W1'], 'L0_gnn_W2': _L0_gnn_in['W2'], 'L0_gnn_attn': _L0_gnn_in['attn'], 'L0_gnn_bias': _L0_gnn_in['bias'], 'L1_gnn_w_l': _L1_gnn_in['w_l'], 'L1_gnn_b_l': _L1_gnn_in['b_l'], 'L1_gnn_w_r': _L1_gnn_in['w_r'], 'L1_gnn_gamma': _L1_gnn_in['gamma'], 'L1_gnn_beta': _L1_gnn_in['beta'], 'L1_gnn_w_res': _L1_gnn_in['w_res'], 'L1_gnn_b_res': _L1_gnn_in['b_res'], 'L1_gnn_w_fc': _L1_gnn_in['w_fc'], 'L1_gnn_b_fc': _L1_gnn_in['b_fc'], 'L2_gnn_W_msg': _L2_gnn_in['W_msg'], 'L2_gnn_b_msg': _L2_gnn_in['b_msg'], 'L2_gnn_W_ih': _L2_gnn_in['W_ih'], 'L2_gnn_W_hh': _L2_gnn_in['W_hh'], 'L2_gnn_b_ih': _L2_gnn_in['b_ih'], 'L2_gnn_b_hh': _L2_gnn_in['b_hh'], 'L3_gnn_W1': _L3_gnn_in['W1'], 'L3_gnn_b1': _L3_gnn_in['b1'], 'L3_gnn_W2': _L3_gnn_in['W2'], 'L3_gnn_b2': _L3_gnn_in['b2'], 'L3_gnn_Wn': _L3_gnn_in['Wn'], 'L3_gnn_bn': _L3_gnn_in['bn']}

def reference(x, src, dst, edge_attr_16, edge_attr_32, edge_attr_4, L0_gnn_W1, L0_gnn_W2, L0_gnn_attn, L0_gnn_bias, L1_gnn_w_l, L1_gnn_b_l, L1_gnn_w_r, L1_gnn_gamma, L1_gnn_beta, L1_gnn_w_res, L1_gnn_b_res, L1_gnn_w_fc, L1_gnn_b_fc, L2_gnn_W_msg, L2_gnn_b_msg, L2_gnn_W_ih, L2_gnn_W_hh, L2_gnn_b_ih, L2_gnn_b_hh, L3_gnn_W1, L3_gnn_b1, L3_gnn_W2, L3_gnn_b2, L3_gnn_Wn, L3_gnn_bn):
    import jax
    import jax.numpy as jnp

    def _L0_gnn_ref(x, edge_attr, src, dst, W1, W2, attn, bias):
        import jax, jax.numpy as jnp
        import numpy as np
        N = 100000
        E = 20000
        D_IN = 64
        D_OUT = 64
        D_EDGE = 16
        NEG_SLOPE = 0.01
        x_t = x @ W2.T
        x_l = x[src]
        x_r = x[dst]
        f_srt = jnp.concatenate([x_l, edge_attr], axis=-1) @ W1.T
        e = jax.nn.leaky_relu(jnp.concatenate([f_srt, x_r], axis=-1), NEG_SLOPE)
        logits = e @ attn
        seg_max = jax.ops.segment_max(logits, dst, num_segments=N)
        seg_max = jnp.where(jnp.isfinite(seg_max), seg_max, 0.0)
        expd = jnp.exp(logits - seg_max[dst])
        denom = jax.ops.segment_sum(expd, dst, num_segments=N)
        alpha = expd / denom[dst]
        msgs = x_t[src] * alpha[:, None]
        h = jax.ops.segment_sum(msgs, dst, num_segments=N)
        return h + bias

    def _L1_gnn_ref(x, edge_src, edge_dst, w_l, b_l, w_r, gamma, beta, w_res, b_res, w_fc, b_fc):
        import jax, jax.numpy as jnp
        import numpy as np
        N, E, D = (100000, 25000, 64)
        L = 3
        EPS = 1e-05

        def _layer_norm(h, g, b):
            mu = jnp.mean(h, axis=-1, keepdims=True)
            var = jnp.var(h, axis=-1, keepdims=True)
            return (h - mu) * jax.lax.rsqrt(var + EPS) * g + b
        n = x.shape[0]
        deg = jax.ops.segment_sum(jnp.ones(edge_dst.shape, x.dtype), edge_dst, num_segments=n)
        inv_deg = jnp.where(deg > 0, 1.0 / jnp.maximum(deg, 1.0), 0.0)[:, None]
        for i in range(L):
            residual = x @ w_res + b_res if i == 0 else x
            agg = jax.ops.segment_sum(x[edge_src], edge_dst, num_segments=n) * inv_deg
            h = agg @ w_l[i] + b_l[i] + x @ w_r[i]
            h = jax.nn.relu(_layer_norm(h, gamma[i], beta[i]))
            x = h + residual
        return x @ w_fc + b_fc

    def _L2_gnn_ref(hv, he, W_msg, b_msg, W_ih, W_hh, b_ih, b_hh, src, dst):
        import jax, jax.numpy as jnp
        import numpy as np
        N_NODES = 50000
        N_EDGES = 12500
        NODE_DIM = 64
        MSG_DIM = 64
        EDGE_DIM = 4
        ROUNDS = 2

        def gru_cell(a, h, W_ih, W_hh, b_ih, b_hh):
            gi = a @ W_ih + b_ih
            gh = h @ W_hh + b_hh
            i_r, i_z, i_n = jnp.split(gi, 3, axis=1)
            h_r, h_z, h_n = jnp.split(gh, 3, axis=1)
            r = jax.nn.sigmoid(i_r + h_r)
            z = jax.nn.sigmoid(i_z + h_z)
            n = jnp.tanh(i_n + r * h_n)
            return (1.0 - z) * n + z * h
        N = hv.shape[0]
        src = src.astype(jnp.int32)
        dst = dst.astype(jnp.int32)
        rounds = W_msg.shape[0]
        for t in range(rounds):
            m_in = jnp.concatenate([hv[src], hv[dst], he], axis=1)
            msg = m_in @ W_msg[t] + b_msg[t]
            a = jax.ops.segment_sum(msg, dst, num_segments=N)
            hv = gru_cell(a, hv, W_ih[t], W_hh[t], b_ih[t], b_hh[t])
        return hv

    def _L3_gnn_ref(nodes, edges, senders, receivers, W1, b1, W2, b2, Wn, bn):
        import jax, jax.numpy as jnp
        import numpy as np
        N_NODES = 100000
        N_EDGES = 25000
        NODE_F = 64
        EDGE_F = 32
        OUT_F = 64
        HIDDEN = 2 * OUT_F
        IN_F = 2 * NODE_F + EDGE_F
        n_nodes = nodes.shape[0]
        sender_features = nodes[senders]
        receiver_features = nodes[receivers]
        concat = jnp.concatenate([sender_features, receiver_features, edges], axis=-1)
        h = jax.nn.relu(concat @ W1 + b1)
        messages = h @ W2 + b2
        aggregated = jax.ops.segment_sum(messages, receivers, num_segments=n_nodes)
        degree = jax.ops.segment_sum(jnp.ones((receivers.shape[0],), dtype=messages.dtype), receivers, num_segments=n_nodes)
        aggregated = aggregated / jnp.maximum(degree, 1.0)[:, None]
        new_nodes = aggregated + (nodes @ Wn + bn)
        return new_nodes
    x = _layernorm(x + _L0_gnn_ref(x, edge_attr_16, src, dst, L0_gnn_W1, L0_gnn_W2, L0_gnn_attn, L0_gnn_bias), axis=-1)
    x = _layernorm(x + _L1_gnn_ref(x, src, dst, L1_gnn_w_l, L1_gnn_b_l, L1_gnn_w_r, L1_gnn_gamma, L1_gnn_beta, L1_gnn_w_res, L1_gnn_b_res, L1_gnn_w_fc, L1_gnn_b_fc), axis=-1)
    x = _layernorm(x + _L2_gnn_ref(x, edge_attr_4, L2_gnn_W_msg, L2_gnn_b_msg, L2_gnn_W_ih, L2_gnn_W_hh, L2_gnn_b_ih, L2_gnn_b_hh, src, dst), axis=-1)
    x = _layernorm(x + _L3_gnn_ref(x, edge_attr_32, src, dst, L3_gnn_W1, L3_gnn_b1, L3_gnn_W2, L3_gnn_b2, L3_gnn_Wn, L3_gnn_bn), axis=-1)
    return x

_drawn_inputs = setup_inputs


def setup_inputs(seed=0):
    import zlib

    import numpy as np

    out = dict(_drawn_inputs(seed))
    spreads = {'L0_gnn_bias': (0.0, 0.1),
     'L1_gnn_b_l': (0.0, 0.1),
     'L1_gnn_gamma': (1.0, 0.2),
     'L1_gnn_beta': (0.0, 0.1),
     'L1_gnn_b_res': (0.0, 0.1),
     'L1_gnn_b_fc': (0.0, 0.1),
     'L3_gnn_b1': (0.0, 0.346),
     'L3_gnn_b2': (0.0, 0.278),
     'L3_gnn_bn': (0.0, 0.1)}
    factors = {'edge_attr_4': 24.072, 'L2_gnn_b_msg': 8.0, 'L2_gnn_b_hh': 4.459, 'edge_attr_16': 2.698}
    for name, (base, spread) in spreads.items():
        noise = np.random.default_rng([zlib.crc32(name.encode()), seed]).standard_normal(out[name].shape)
        drawn = base * np.exp(spread * noise) if base else spread * noise
        out[name] = jnp.asarray(drawn.astype(out[name].dtype))
    for name, factor in factors.items():
        out[name] = (out[name] * factor).astype(out[name].dtype)
    return out
```

```python
from contextlib import ExitStack

import concourse.bass as bass
from concourse import mybir

F32 = mybir.dt.float32
I32 = mybir.dt.int32
ALU = mybir.AluOpType
ACT = mybir.ActivationFunctionType

P = 128
D = 64
H = 2
COLS = 512
TILE = H * COLS
Q = COLS // P
B = 4
EPS = 1e-5
BIG = 1e30
OUTSIDE = 1 << 20


def build(nc, a, out):
    N = a["x"].shape[0]
    E = a["src"].shape[0]
    TM = -(-N // TILE)
    TE = -(-E // TILE)
    SLOTS = TE * TILE
    LAST_E = E - (TE - 1) * TILE
    LAST_P = LAST_E // Q
    assert LAST_E % Q == 0 and LAST_E <= COLS and N < OUTSIDE and N % 8 == 0

    norm = lambda l: [f"{s}{l}" for s in ("centred", "squared", "variance", "logvar", "rstd", "normed")]
    sage = lambda i: norm(1 + i) + [f"relu{i}", f"added{i}"] + (["residual_mm"] if i == 0 else [])
    gru = lambda r: [f"{s}{r}" for s in ("gate_r", "gate_z", "gate_n", "sig_r", "sig_z", "reset", "tanh",
                                         "diff", "scaled", "hidden")]
    save = lambda l: [f"turned_out{l}", f"rows_out{l}"]
    chain = (["turned_in", "x_in"] + norm(0) + sage(0) + sage(1) + sage(2) + norm(4) + gru(0) + gru(1)
             + ["summed"] + norm(5))
    saves = sum((save(l) for l in range(1, 7)), [])
    gather2 = ["turned_in", "turned_dst", "src_in", "x_in", "turned_edge", "edge_in"]
    PHASES = [
        ("main", TM, chain + norm(6) + save(7)),
        ("src", TE, chain + saves),
        ("d0", TE, gather2 + ["same", "hidden_mm", "small_slope", "leaky", "penalty", "logits", "max_before",
                              "new_weight", "max_step", "max_shift", "inv_degree", "decay_exp", "weight_exp",
                              "weighted", "inv_den", "mixed"] + norm(0) + save(1)),
        ("d1", TE, ["turned_in", "mean"] + sage(0) + save(2)),
        ("d2", TE, ["turned_in", "mean"] + sage(1) + save(3)),
        ("d3", TE, ["turned_in", "mean"] + sage(2) + norm(4) + save(4)),
        ("d4", TE, ["turned_in", "turned_edge", "times_degree", "message", "message_in", "reset_sum"] + gru(0)
         + save(5)),
        ("d5", TE, ["turned_in", "turned_edge", "times_degree", "message", "message_in", "reset_sum"] + gru(1)
         + ["summed"] + norm(5) + save(6)),
        ("d6", TE, gather2 + ["hidden_mm", "hidden_relu0", "hidden_relu1", "message", "mean"] + norm(6) + save(7)),
    ]
    tiles_of = {ph: tiles for ph, tiles, _ in PHASES}
    kind = lambda stage: stage.rstrip("0123456789")
    turn, turns, base, count = {}, {}, {}, {}
    for ph, tiles, stages in PHASES:
        for s in stages:
            turn[ph, s] = turns.get((ph, kind(s)), 0)
            turns[ph, kind(s)] = turn[ph, s] + 1
        for k in dict.fromkeys(map(kind, stages)):
            base[ph, k] = count.get(k, 0)
            count[k] = base[ph, k] + turns[ph, k] * tiles
    SCANS = [("d0", 4)] + [(f"d{k}", 1) for k in (1, 2, 3)] + [("d4", 2), ("d5", 2), ("d6", 1)]
    scan_base, n = {}, 0
    for ph, k in SCANS:
        scan_base[ph] = (n, k)
        n += 2 * k * TE

    def slot_uses(ph, b):
        return -(-(tiles_of[ph] - b) // B)

    LOADS = {"main": 1, "d0": 4, "d1": 3, "d2": 3, "d3": 4, "d4": 5, "d5": 6, "d6": 5}
    GATHERS = {"src": 8, "d0": 16, "d1": 8, "d2": 8, "d3": 8, "d4": 8, "d5": 8, "d6": 16}
    STORES = {"main": 1, "src": 6, "d0": 2, "d1": 2, "d2": 2, "d3": 2, "d4": 2, "d5": 2}
    KEEPS = {"d0": 4, "d1": 1, "d2": 1, "d3": 1, "d4": 1, "d5": 1}
    SCATTERS = {"d6": 8}

    def before(table, ph, b):
        v = 0
        for name, _, _ in PHASES:
            if name == ph:
                return v
            v += 16 * table.get(name, 0) * slot_uses(name, b)
        return v

    with ExitStack() as ctx:
        def sb(name, shape, dt=F32):
            return ctx.enter_context(nc.sbuf_tensor(name, shape, dt))

        def dram(name, shape, dt=F32):
            return nc.dram_tensor(name, shape, dt, kind="Internal").ap()

        def sem(name):
            return ctx.enter_context(nc.semaphore(name))

        S = {k: sem(k) for k in count}
        loaded = [sem(f"loaded{b}") for b in range(B)]
        gathered = [sem(f"gathered{b}") for b in range(B)]
        stored = [sem(f"stored{b}") for b in range(B)]
        kept = [sem(f"kept{b}") for b in range(B)]
        scattered = [sem(f"scattered{b}") for b in range(B)]
        carried, scanned = sem("carried"), sem("scanned")
        weights_in, zeroed, consts, prep_pe, prep_dve = (sem(n) for n in (
            "weights_in", "zeroed", "consts", "prep_pe", "prep_dve"))
        pad_filled, pad_put, ids_in, ids_ready, fills, iota_done, id_steps, ident_zero = (
            sem(n) for n in ("pad_filled", "pad_put", "ids_in", "ids_ready", "fills", "iota_done", "id_steps",
                             "ident_zero"))
        map_zero, map_copied, staged, ones_set, passed = (
            sem(n) for n in ("map_zero", "map_copied", "staged", "ones_set", "passed"))
        map_put = [sem(f"map_put{b}") for b in range(B)]
        map_got = [sem(f"map_got{b}") for b in range(B)]

        dst_pad = dram("dst_pad", (P * (TE * 8 + 1),), I32)
        src_pad = dram("src_pad", (SLOTS,), I32)
        node_slot = dram("node_slot", (N, 1), I32)
        table = {l: dram(f"table{l}", (2 * SLOTS, D)) for l in range(1, 7)}
        state = {l: dram(f"state{l}", (TE * P, COLS)) for l in range(1, 7)}
        same_d = dram("same_d", (TE * P, COLS))
        degree_d = dram("degree_d", (TE * P, COLS))
        inv_degree_d = dram("inv_degree_d", (TE * P, COLS))

        def ring(name, cols=COLS, dt=F32):
            return [sb(f"{name}{b}", [P, cols], dt) for b in range(B)]

        rows, rows2, edges, rows_o = ring("rows"), ring("rows2"), ring("edges"), ring("rows_o")
        X, Y, Z, R, W = ring("X"), ring("Y"), ring("Z"), ring("R"), ring("W")
        XS, EF, AG, DN, DC, MSG = ring("XS"), ring("EF"), ring("AG"), ring("DN"), ring("DC"), ring("MSG")
        SAME, DEG = ring("SAME"), ring("DEG")
        MX = ring("MX", COLS + 1)
        IDS = ring("IDS", COLS + 1, I32)
        carry = sb("carry", [P, 1])
        PA = [ctx.enter_context(nc.psum_tensor(f"PA{b}", [P, COLS], F32)) for b in range(B)]
        PB = [ctx.enter_context(nc.psum_tensor(f"PB{b}", [P, COLS], F32)) for b in range(B)]

        NT = 10
        names = (["wr0", "wr1", "wr2", "wfc", "wl0", "wl1", "wl2", "wn", "w1x", "w1e", "w2", "wres"]
                 + [f"{n}{t}" for t in range(2) for n in ("msg_s", "msg_d", "msg_e", "ih_r", "ih_z", "ih_n",
                                                          "hh_r", "hh_z", "hh_n")])
        wraw = sb("wraw", [P, len(names), P])
        wat = {n: wraw[:, i, :] for i, n in enumerate(names)}
        wturned = sb("wturned", [P, NT, P])
        wcentred = sb("wcentred", [P, 9, P])
        wc = {n: wcentred[:, i, :] for i, n in enumerate(names[:8] + ["w2"])}
        w3s, w3d, w3e = sb("w3s", [P, P]), sb("w3d", [P, P]), sb("w3e", [P, P])
        w3o = sb("w3o", [P, D])
        ident, ones_block, mean_block, centre = (sb(n, [P, P]) for n in ("ident", "ones_block", "mean_block", "centre"))
        att_f, att_r = sb("att_f", [P, P]), sb("att_r", [P, P])
        ones = sb("ones", [P, COLS])
        eps = sb("eps", [P, 1])
        cols = ["bias0", "bl0", "bl1", "bl2", "bfc", "zero", "bn", "b3", "g0", "g1", "g2", "be0", "be1", "be2",
                "bres", "att_f", "att_r", "ih_r0", "ih_z0", "ih_n0", "hh_r0", "hh_z0", "hh_n0",
                "ih_r1", "ih_z1", "ih_n1", "hh_r1", "hh_z1", "hh_n1", "b2"]
        bias = sb("bias", [P, 32])
        bcol = {n: bias[:, i:i + 1] for i, n in enumerate(cols)}
        NC = 8
        bcent = sb("bcent", [P, NC])
        b1col = sb("b1col", [P, 1])
        gate_b = sb("gate_b", [P, 4])
        norm_bias = {0: 0, 1: 1, 2: 2, 3: 3, 4: 4, 5: 5, 6: 6, "6d": 7}

        ids = {n: sb(n, [P, TE * 8], I32) for n in
               ("dst_of", "dst_next", "src_of", "src_rows", "dst_row", "put_row", "slot1", "src_map", "dst_map",
                "src_slot", "dst_slot")}
        idf = sb("idf", [P, TE * 8])
        idf2 = sb("idf2", [P, TE * 8])
        fill = sb("fill", [P, 2, TE * 8 + 1], I32)
        zero_map = sb("zero_map", [80, N // 80], I32)
        gi = [sb(f"gi{b}", [P, 16], I32) for b in range(B)]
        gv = [sb(f"gv{b}", [P, 16], I32) for b in range(B)]

        weight_loads = []
        def load_block(name, src, row=0, k=D):
            for h in range(H):
                weight_loads.append((wraw[h * D + row:h * D + row + k, names.index(name), h * D:h * D + src.shape[-1]],
                                     src))
        for i in range(3):
            load_block(f"wr{i}", a["L1_gnn_w_r"][i])
            load_block(f"wl{i}", a["L1_gnn_w_l"][i])
        load_block("wfc", a["L1_gnn_w_fc"])
        load_block("wn", a["L3_gnn_Wn"])
        load_block("w1x", a["L0_gnn_W1"][:, 0:D])
        load_block("w1e", a["L0_gnn_W1"][:, D:])
        load_block("w2", a["L0_gnn_W2"])
        load_block("wres", a["L1_gnn_w_res"])
        for t in range(2):
            m = a["L2_gnn_W_msg"][t]
            load_block(f"msg_s{t}", m[0:D, :])
            load_block(f"msg_d{t}", m[D:2 * D, :])
            load_block(f"msg_e{t}", m[2 * D:, :], 0, 4)
            load_block(f"msg_e{t}", a["L2_gnn_b_msg"][t:t + 1, :], 4, 1)
            for k, g in enumerate("rzn"):
                load_block(f"ih_{g}{t}", a["L2_gnn_W_ih"][t][:, k * D:k * D + D])
                load_block(f"hh_{g}{t}", a["L2_gnn_W_hh"][t][:, k * D:k * D + D])
        w3 = a["L3_gnn_W1"]
        for h in range(H):
            weight_loads += [(w3s[h * D:h * D + D, :], w3[0:D, :]), (w3d[h * D:h * D + D, :], w3[D:2 * D, :]),
                             (w3e[h * D:h * D + 32, :], w3[2 * D:, :])]
        weight_loads.append((w3o[:, :], a["L3_gnn_W2"]))
        column = lambda x: x.rearrange("(f o) -> f o", o=1)
        weight_loads.append((b1col[:, :], column(a["L3_gnn_b1"])))
        vectors = {"bias0": a["L0_gnn_bias"], "bfc": a["L1_gnn_b_fc"], "bres": a["L1_gnn_b_res"],
                   "bn": a["L3_gnn_bn"], "b2": a["L3_gnn_b2"],
                   "att_f": a["L0_gnn_attn"][0:D], "att_r": a["L0_gnn_attn"][D:2 * D]}
        for i in range(3):
            vectors |= {f"bl{i}": a["L1_gnn_b_l"][i], f"g{i}": a["L1_gnn_gamma"][i], f"be{i}": a["L1_gnn_beta"][i]}
        for t in range(2):
            for k, g in enumerate("rzn"):
                vectors |= {f"ih_{g}{t}": a["L2_gnn_b_ih"][t][k * D:k * D + D],
                            f"hh_{g}{t}": a["L2_gnn_b_hh"][t][k * D:k * D + D]}
        for name, vec in vectors.items():
            for h in range(H):
                weight_loads.append((bias[h * D:h * D + D, cols.index(name):cols.index(name) + 1], column(vec)))
        n_weight_dmas = len(weight_loads)

        block = ctx.enter_context(nc.Block())

        def each_batch(eng, ph, body, peel=False):
            full = tiles_of[ph] // B * B
            if peel:
                body(0, B)
            with eng.Fori(B if peel else 0, full - B + 1, B) as t:
                body(t, B)
            if tiles_of[ph] > full:
                body(full, tiles_of[ph] - full)

        def batch_size(ph, t):
            return min(B, tiles_of[ph] - t) if isinstance(t, int) else B

        def wait(eng, ph, stage, t, b):
            k = kind(stage)
            eng.wait_ge(S[k], t * turns[ph, k] + (base[ph, k] + turn[ph, stage] * batch_size(ph, t) + b + 1))

        def wait_before(eng, ph, stage, t, b):
            k = kind(stage)
            v = base[ph, k] + turn[ph, stage] * B + b + 1 - turns[ph, k] * B
            assert v >= 0
            eng.wait_ge(S[k], t * turns[ph, k] + v)

        def wait_phase(eng, ph, stage):
            k = kind(stage)
            eng.wait_ge(S[k], base[ph, k] + turns[ph, k] * tiles_of[ph])

        def settle(eng):
            eng.sem_inc(passed, 1)

        def wait_loaded(eng, ph, t, b, k=None):
            k = LOADS[ph] if k is None else k
            eng.wait_ge(loaded[b], t * (4 * LOADS[ph]) + (before(LOADS, ph, b) + 16 * k))

        def wait_gathered(eng, ph, t, b):
            eng.wait_ge(gathered[b], t * (4 * GATHERS[ph]) + (before(GATHERS, ph, b) + 16 * GATHERS[ph]))

        def wait_stored(eng, ph, t, b, k):
            v = before(STORES, ph, b) + 16 * k
            if not isinstance(t, int) or t * 4 * STORES.get(ph, 0) + v > 0:
                eng.wait_ge(stored[b], t * (4 * STORES.get(ph, 0)) + v)

        def scan_place(ph, t, b, k):
            first, per = scan_base[ph]
            if ph == "d0":
                return first + 4 * (k // 2) * batch_size(ph, t) + 4 * b + 2 * (k % 2)
            return first + 2 * (per * b + k)

        def wait_scans(eng, ph, t, b, k):
            eng.wait_ge(scanned, t * (2 * scan_base[ph][1]) + (scan_place(ph, t, b, k - 1) + 2))

        n_id_loads = 3 * H + 1

        @block.tensor
        def _(pe):
            mm = nc.tensor.matmul

            pe.wait_ge(weights_in, 16 * n_weight_dmas)
            pe.wait_ge(consts, 2)
            for i in range(NT):
                bank = [PA[0], PB[0], PA[1]][i // Q]
                last = nc.tensor.transpose(bank[:, (i % Q) * P:(i % Q + 1) * P], wraw[:, i, :], ident[:, :])
            last.then_inc(prep_pe, 1)
            pe.wait_ge(prep_dve, 1)
            for i in range(8):
                bank = [PB[1], PA[2]][i // Q]
                mm(bank[:, (i % Q) * P:(i % Q + 1) * P], wturned[:, i, :], centre[:, :], start=True, stop=True)
            mm(PB[2][:, 0:P], wat["w2"], centre[:, :], start=True, stop=True)
            mm(PB[2][:, P:P + NC], centre[:, :], bias[:, 0:NC], start=True, stop=True).then_inc(prep_pe, 1)
            pe.wait_ge(prep_dve, 2)

            def turn_in(ph, t, b, src, bank, order, stage):
                for q in range(Q):
                    o = bank[b][:, q * P:(q + 1) * P] if order == "any" else bank[b][:, q::Q]
                    last = nc.tensor.transpose(o, src[b][:, q * P:(q + 1) * P], ident[:, :])
                last.then_inc(S[kind(stage)], 1)

            def turn_out(ph, t, nb, st, order, level, after):
                for b in range(nb):
                    wait(pe, ph, after, t, b)
                    for q in range(Q):
                        i = st[b][:, q * P:(q + 1) * P] if order == "any" else st[b][:, q::Q]
                        last = nc.tensor.transpose(PB[b][:, q * P:(q + 1) * P], i, ident[:, :])
                    last.then_inc(S["turned_out"], 1)

            def variance(ph, t, nb, l):
                for b in range(nb):
                    wait(pe, ph, f"squared{l}", t, b)
                    mm(PB[b][:, :], mean_block[:, :], R[b][:, :], start=True, stop=True)\
                        .then_inc(S["variance"], 1)

            def product(ph, t, nb, bank, pairs, stage, waits):
                for b in range(nb):
                    for w in waits:
                        wait(pe, ph, w, t, b)
                    for k, (w, st) in enumerate(pairs):
                        last = mm(bank[b][:, :], w, st[b][:, :], start=(k == 0), stop=(k == len(pairs) - 1))
                    last.then_inc(S[kind(stage)], 1)

            def norm_of(ph, t, nb, l, pairs, waits):
                product(ph, t, nb, PA, pairs, f"centred{l}", waits)
                variance(ph, t, nb, l)

            def sage_layer(ph, t, nb, i, waits, mean):
                st = X if i == 0 else Y
                pairs = [(wc[f"wr{i}"], st)] + ([(wc[f"wl{i}"], AG)] if mean else [])
                norm_of(ph, t, nb, 1 + i, pairs, waits + (["mean"] if mean else []))
                if i == 0:
                    product(ph, t, nb, PB, [(wat["wres"], X)], "residual_mm", ["logvar1"])

            def gates(ph, t, nb, r, st, waits, msg):
                m = lambda g: [(wat[f"ih_{g}{r}"], MSG)] if msg else []
                more = ["message_in"] if msg else []
                product(ph, t, nb, PA, [(wat[f"hh_r{r}"], st)] + m("r"), f"gate_r{r}", waits + more)
                product(ph, t, nb, PB, [(wat[f"hh_z{r}"], st)] + m("z"), f"gate_z{r}", [])
                for b in range(nb):
                    wait(pe, ph, f"sig_r{r}", t, b)
                    last = mm(PA[b][:, :], wat[f"hh_n{r}"], st[b][:, :], start=True, stop=True)
                    if msg:
                        wait(pe, ph, f"sig_z{r}", t, b)
                        last = mm(PB[b][:, :], wat[f"ih_n{r}"], MSG[b][:, :], start=True, stop=True)
                    last.then_inc(S["gate_n"], 1)

            def chain_pe(ph, order, saving):
                def body(t, nb):
                    for b in range(nb):
                        if ph == "main":
                            wait_loaded(pe, ph, t, b)
                        else:
                            wait_gathered(pe, ph, t, b)
                        turn_in(ph, t, b, rows, PA, order, "turned_in")
                    out_of = lambda l, st, after: turn_out(ph, t, nb, st, order, l, after) if saving else None
                    norm_of(ph, t, nb, 0, [(centre[:, :], X)], ["x_in"])
                    out_of(1, X, "normed0")
                    sage_layer(ph, t, nb, 0, ["normed0"], False)
                    out_of(2, Y, "added0")
                    sage_layer(ph, t, nb, 1, ["added0"], False)
                    out_of(3, Y, "added1")
                    sage_layer(ph, t, nb, 2, ["added1"], False)
                    norm_of(ph, t, nb, 4, [(wc["wfc"], Y), (centre[:, :], X)], ["added2"])
                    out_of(4, X, "normed4")
                    gates(ph, t, nb, 0, X, ["normed4"] + ["rows_out4"] * saving, False)
                    out_of(5, Y, "hidden0")
                    gates(ph, t, nb, 1, Y, ["hidden0"] + ["rows_out5"] * saving, False)
                    norm_of(ph, t, nb, 5, [(centre[:, :], Y)], ["summed"])
                    out_of(6, X, "normed5")
                    if ph == "main":
                        norm_of(ph, t, nb, 6, [(wc["wn"], X)], ["normed5"])
                        turn_out(ph, t, nb, X, order, 7, "normed6")
                each_batch(pe, ph, body)

            chain_pe("main", "any", False)
            chain_pe("src", "any", True)

            level = {"d0": 1, "d4": 5, "d5": 6, "d6": 7}

            def pb_free(ph, t, b):
                wait_before(pe, ph, f"rows_out{level[ph]}", t, b)

            def phase_over(ph, lev):
                wait_phase(pe, ph, f"rows_out{lev}")

            def turn_edge_inputs(ph, t, nb):
                for b in range(nb):
                    wait_gathered(pe, ph, t, b)
                    pb_free(ph, t, b)
                    turn_in(ph, t, b, rows2, PB, "edge", "turned_dst")
                    turn_in(ph, t, b, rows, PA, "edge", "turned_in")
                for b in range(nb):
                    wait(pe, ph, "src_in", t, b)
                    wait_loaded(pe, ph, t, b)
                    turn_in(ph, t, b, edges, PA, "edge", "turned_edge")

            def d0(t, nb):
                turn_edge_inputs("d0", t, nb)
                product("d0", t, nb, PA, [(wturned[:, 8, :], XS), (wturned[:, 9, :], EF)], "hidden_mm", ["edge_in"])
                product("d0", t, nb, PB, [(att_f[:, :], Z), (att_r[:, :], W)], "logits", ["leaky", "x_in"])
                norm_of("d0", t, nb, 0, [(centre[:, :], X), (wc["w2"], AG)], ["mixed"])
                turn_out("d0", t, nb, X, "edge", 1, "normed0")
            phase_over("src", 6)
            each_batch(pe, "d0", d0)

            def turn_src(ph, t, nb):
                for b in range(nb):
                    wait_gathered(pe, ph, t, b)
                    wait_loaded(pe, ph, t, b)
                    turn_in(ph, t, b, rows, PA, "edge", "turned_in")

            def sage_phase(ph, i):
                def body(t, nb):
                    turn_src(ph, t, nb)
                    sage_layer(ph, t, nb, i, [], True)
                    if i == 2:
                        norm_of(ph, t, nb, 4, [(wc["wfc"], Y), (centre[:, :], X)], ["added2"])
                        turn_out(ph, t, nb, X, "edge", 4, "normed4")
                    else:
                        turn_out(ph, t, nb, Y, "edge", 2 + i, f"added{i}")
                each_batch(pe, ph, body)
            for i in range(3):
                sage_phase(f"d{1 + i}", i)

            def gru_phase(ph, r):
                st = X if r == 0 else Y
                def body(t, nb):
                    turn_src(ph, t, nb)
                    for b in range(nb):
                        pb_free(ph, t, b)
                        turn_in(ph, t, b, edges, PB, "edge", "turned_edge")
                    for b in range(nb):
                        wait_scans(pe, ph, t, b, 2)
                    product(ph, t, nb, PA, [(wat[f"msg_s{r}"], AG), (wat[f"msg_d{r}"], W), (wat[f"msg_e{r}"], EF)],
                            "message", ["times_degree"])
                    gates(ph, t, nb, r, st, [], True)
                    if r == 1:
                        norm_of(ph, t, nb, 5, [(centre[:, :], Y)], ["summed"])
                        turn_out(ph, t, nb, X, "edge", 6, "normed5")
                    else:
                        turn_out(ph, t, nb, Y, "edge", 5, "hidden0")
                each_batch(pe, ph, body)
            phase_over("d3", 4)
            pe.wait_ge(ones_set, 1)
            gru_phase("d4", 0)
            phase_over("d4", 5)
            gru_phase("d5", 1)
            phase_over("d5", 6)

            def d6(t, nb):
                turn_edge_inputs("d6", t, nb)
                for b in range(nb):
                    wait(pe, "d6", "x_in", t, b)
                    wait(pe, "d6", "edge_in", t, b)
                    for h, bank in enumerate((PA, PB)):
                        r = slice(h * D, h * D + D)
                        mm(bank[b][:, :], w3s[r, :], XS[b][r, :], start=True, stop=False)
                        mm(bank[b][:, :], w3d[r, :], Y[b][r, :], start=False, stop=False)
                        last = mm(bank[b][:, :], w3e[r, :], EF[b][r, :], start=False, stop=True)
                    last.then_inc(S["hidden_mm"], 1)
                for b in range(nb):
                    wait(pe, "d6", "hidden_relu0", t, b)
                    mm(PA[b][0:D, :], w3o[:, :], Z[b][:, :], start=True, stop=True)
                    wait(pe, "d6", "hidden_relu1", t, b)
                    mm(PA[b][D:P, :], w3o[:, :], W[b][:, :], start=True, stop=True).then_inc(S["message"], 1)
                norm_of("d6", t, nb, 6, [(wc["wn"], X), (centre[:, :], AG)], ["mean"])
                turn_out("d6", t, nb, X, "edge", 7, "normed6")
            each_batch(pe, "d6", d6)

        @block.scalar
        def _(act):
            fn = nc.scalar.activation

            def per_tile(ph, t, nb, stage, waits, op):
                for b in range(nb):
                    for w in waits:
                        wait(act, ph, w, t, b)
                    op(b).then_inc(S[kind(stage)], 1)

            def norm_of(ph, t, nb, l, bias_id=None):
                c = norm_bias[l if bias_id is None else bias_id]
                per_tile(ph, t, nb, f"squared{l}", [f"centred{l}"],
                         lambda b: fn(R[b][:, :], PA[b][:, :], ACT.Square, bias=bcent[:, c:c + 1]))
                per_tile(ph, t, nb, f"logvar{l}", [f"variance{l}"],
                         lambda b: fn(R[b][:, :], PB[b][:, :], ACT.Ln, bias=eps[:, :]))
                per_tile(ph, t, nb, f"rstd{l}", [f"logvar{l}"],
                         lambda b: fn(R[b][:, :], R[b][:, :], ACT.Exp, scale=-0.5))

            def sage_layer(ph, t, nb, i):
                norm_of(ph, t, nb, 1 + i)
                per_tile(ph, t, nb, f"relu{i}", [f"normed{1 + i}"],
                         lambda b: fn(Z[b][:, :], Z[b][:, :], ACT.Relu, bias=bcol[f"be{i}"], scale=bcol[f"g{i}"]))

            def gates(ph, t, nb, r, msg):
                per_tile(ph, t, nb, f"sig_r{r}", [f"gate_r{r}"],
                         lambda b: fn(R[b][:, :], PA[b][:, :], ACT.Sigmoid, bias=gate_b[:, 2 * r:2 * r + 1]))
                per_tile(ph, t, nb, f"sig_z{r}", [f"gate_z{r}"],
                         lambda b: fn(Z[b][:, :], PB[b][:, :], ACT.Sigmoid, bias=gate_b[:, 2 * r + 1:2 * r + 2]))
                per_tile(ph, t, nb, f"tanh{r}", ["reset_sum" if msg else f"reset{r}"],
                         lambda b: fn(R[b][:, :], R[b][:, :], ACT.Tanh, bias=bcol[f"ih_n{r}"]))

            def rows_out(ph, t, nb, level, k):
                for b in range(nb):
                    wait(act, ph, f"turned_out{level}", t, b)
                    if ph == "d6":
                        if not (isinstance(t, int) and t == 0):
                            act.wait_ge(scattered[b], t * (4 * 8))
                    wait_stored(act, ph, t, b, k)
                    fn(rows_o[b][:, :], PB[b][:, :], ACT.Copy).then_inc(S["rows_out"], 1)

            act.wait_ge(prep_dve, 3)

            def log_exp_tables():
                nc.scalar.preload_act_table_set("natural_log_exp_and_others")

            def chain_act(ph, saving):
                def body(t, nb):
                    log_exp_tables()
                    per_tile(ph, t, nb, "x_in", ["turned_in"], lambda b: fn(X[b][:, :], PA[b][:, :], ACT.Copy))
                    norm_of(ph, t, nb, 0)
                    out_of = lambda l: rows_out(ph, t, nb, l, l - 1) if saving else None
                    out_of(1)
                    sage_layer(ph, t, nb, 0)
                    out_of(2)
                    sage_layer(ph, t, nb, 1)
                    out_of(3)
                    sage_layer(ph, t, nb, 2)
                    norm_of(ph, t, nb, 4)
                    out_of(4)
                    gates(ph, t, nb, 0, False)
                    out_of(5)
                    gates(ph, t, nb, 1, False)
                    log_exp_tables()
                    norm_of(ph, t, nb, 5)
                    out_of(6)
                    if ph == "main":
                        norm_of(ph, t, nb, 6)
                        rows_out(ph, t, nb, 7, 0)
                each_batch(act, ph, body)

            chain_act("main", False)
            chain_act("src", True)

            def edge_inputs(ph, t, nb, dst):
                per_tile(ph, t, nb, "src_in", ["turned_in"], lambda b: fn(XS[b][:, :], PA[b][:, :], ACT.Copy))
                for b in range(nb):
                    if ph == "d0" and not (isinstance(t, int) and t == 0):
                        act.wait_ge(kept[b], t * (4 * KEEPS[ph]) + (1 + before(KEEPS, ph, b)))
                    wait(act, ph, "turned_dst", t, b)
                    fn(dst[b][:, :], PB[b][:, :], ACT.Copy).then_inc(S["x_in"], 1)
                per_tile(ph, t, nb, "edge_in", ["turned_edge"], lambda b: fn(EF[b][:, :], PA[b][:, :], ACT.Copy))

            def d0(t, nb):
                log_exp_tables()
                edge_inputs("d0", t, nb, X)
                per_tile("d0", t, nb, "decay_exp", ["max_shift"], lambda b: fn(DC[b][:, :], DC[b][:, :], ACT.Exp))
                per_tile("d0", t, nb, "weight_exp", ["new_weight"], lambda b: fn(R[b][:, :], R[b][:, :], ACT.Exp))
                norm_of("d0", t, nb, 0)
                rows_out("d0", t, nb, 1, 0)
            each_batch(act, "d0", d0)

            def sage_phase(ph, i):
                def body(t, nb):
                    log_exp_tables()
                    sage_layer(ph, t, nb, i)
                    if i == 2:
                        norm_of(ph, t, nb, 4)
                    rows_out(ph, t, nb, 4 if i == 2 else 2 + i, 0)
                each_batch(act, ph, body)
            for i in range(3):
                sage_phase(f"d{1 + i}", i)

            def gru_phase(ph, r):
                def body(t, nb):
                    per_tile(ph, t, nb, "message_in", ["message"], lambda b: fn(MSG[b][:, :], PA[b][:, :], ACT.Copy))
                    gates(ph, t, nb, r, True)
                    if r == 1:
                        log_exp_tables()
                        norm_of(ph, t, nb, 5)
                    rows_out(ph, t, nb, 5 + r, 0)
                each_batch(act, ph, body)
            gru_phase("d4", 0)
            gru_phase("d5", 1)

            def d6(t, nb):
                log_exp_tables()
                edge_inputs("d6", t, nb, Y)
                for h, (bank, hid) in enumerate(((PA, Z), (PB, W))):
                    per_tile("d6", t, nb, f"hidden_relu{h}", ["hidden_mm"],
                             lambda b: fn(hid[b][:, :], bank[b][:, :], ACT.Relu, bias=b1col[:, :]))
                norm_of("d6", t, nb, 6, "6d")
                rows_out("d6", t, nb, 7, 0)
            each_batch(act, "d6", d6, peel=True)

        @block.vector
        def _(dve):
            v = nc.vector

            dve.wait_ge(zeroed, 1)
            v.memset(ones_block[:, :], 0.0).then_inc(consts, 1)
            v.memset(ones[:, :], 1.0)
            v.memset(eps[:, :], EPS)
            dve.wait_ge(consts, 1)
            for h in range(H):
                last = v.memset(ones_block[h * D:h * D + D, h * D:h * D + D], 1.0)
            last.then_inc(id_steps, 1)
            dve.wait_ge(id_steps, 1)
            v.tensor_scalar(mean_block[:, :], ones_block[:, :], 1.0 / D, None, ALU.mult).then_inc(id_steps, 1)
            dve.wait_ge(id_steps, 2)
            dve.wait_ge(zeroed, 2)
            v.tensor_tensor(centre[:, :], ident[:, :], mean_block[:, :], ALU.subtract).then_inc(consts, 1)
            dve.wait_ge(weights_in, 16 * n_weight_dmas)
            v.tensor_scalar(att_f[:, :], ones_block[:, :], bcol["att_f"], None, ALU.mult)
            v.tensor_scalar(att_r[:, :], ones_block[:, :], bcol["att_r"], None, ALU.mult)
            i = cols.index("b3")
            v.tensor_tensor(bias[:, i:i + 1], bcol["bn"], bcol["b2"], ALU.add)
            for r in range(2):
                for k, g in enumerate("rz"):
                    v.tensor_tensor(gate_b[:, 2 * r + k:2 * r + k + 1], bcol[f"ih_{g}{r}"], bcol[f"hh_{g}{r}"], ALU.add)
            dve.wait_ge(prep_pe, 1)
            v.tensor_copy(wturned[:, 0:Q, :], PA[0][:, :].rearrange("p (a b) -> p a b", a=Q))
            v.tensor_copy(wturned[:, 8:NT, :], PA[1][:, 0:2 * P].rearrange("p (a b) -> p a b", a=2))
            v.tensor_copy(wturned[:, Q:7, :], PB[0][:, 0:3 * P].rearrange("p (a b) -> p a b", a=3))
            v.tensor_tensor(wturned[:, 7, :], PB[0][:, 3 * P:4 * P], ident[:, :], ALU.add).then_inc(prep_dve, 1)
            dve.wait_ge(prep_pe, 2)
            v.tensor_copy(wcentred[:, 0:Q, :], PB[1][:, :].rearrange("p (a b) -> p a b", a=Q))
            v.tensor_copy(wcentred[:, Q:8, :], PA[2][:, :].rearrange("p (a b) -> p a b", a=Q))
            v.tensor_copy(wcentred[:, 8, :], PB[2][:, 0:P])
            v.tensor_copy(bcent[:, :], PB[2][:, P:P + NC]).then_inc(prep_dve, 1)
            for b in range(B):
                v.memset(edges[b][:, :], 0.0)
                v.memset(MX[b][:, :], 0.0)
                v.memset(DN[b][:, :], 0.0)
                v.memset(DEG[b][:, :], 0.0)
                v.memset(AG[b][:, :], 0.0)
                last = v.memset(EF[b][:, :], 0.0)
            last.then_inc(prep_dve, 1)

            g = lambda n: ids[n][:, :]
            dve.wait_ge(ids_in, 16 * n_id_loads)
            dve.wait_ge(iota_done, 1)
            v.tensor_tensor(idf[:, :], g("dst_of"), g("dst_next"), ALU.is_equal)
            v.tensor_scalar(g("dst_row"), g("dst_of"), 0.0, None, ALU.max).then_inc(ids_ready, 1)
            dve.wait_ge(ids_ready, 1)
            v.scalar_tensor_tensor(g("put_row"), idf[:, :], float(OUTSIDE), g("dst_of"), ALU.mult, ALU.add)\
                .then_inc(ids_ready, 1)

            def norm_of(ph, t, nb, l, dst, bias_id=None):
                c = norm_bias[l if bias_id is None else bias_id]
                for b in range(nb):
                    wait(dve, ph, f"rstd{l}", t, b)
                    v.scalar_tensor_tensor(dst[b][:, :], PA[b][:, :], bcent[:, c:c + 1], R[b][:, :], ALU.add, ALU.mult)\
                        .then_inc(S["normed"], 1)

            def sage_layer(ph, t, nb, i):
                norm_of(ph, t, nb, 1 + i, Z)
                for b in range(nb):
                    wait(dve, ph, f"relu{i}", t, b)
                    if i == 0:
                        wait(dve, ph, "residual_mm", t, b)
                        op = v.scalar_tensor_tensor(Y[b][:, :], PB[b][:, :], bcol["bres"], Z[b][:, :], ALU.add, ALU.add)
                    else:
                        op = v.tensor_tensor(Y[b][:, :], Y[b][:, :], Z[b][:, :], ALU.add)
                    op.then_inc(S["added"], 1)

            def gates(ph, t, nb, r, msg):
                st = X if r == 0 else Y
                tmp = Y if r == 0 else W
                for b in range(nb):
                    wait(dve, ph, f"gate_n{r}", t, b)
                    v.scalar_tensor_tensor(R[b][:, :], PA[b][:, :], bcol[f"hh_n{r}"], R[b][:, :], ALU.add, ALU.mult)\
                        .then_inc(S["reset"], 1)
                if msg:
                    for b in range(nb):
                        wait(dve, ph, f"reset{r}", t, b)
                        v.tensor_tensor(R[b][:, :], PB[b][:, :], R[b][:, :], ALU.add).then_inc(S["reset_sum"], 1)
                for b in range(nb):
                    wait(dve, ph, f"tanh{r}", t, b)
                    v.tensor_tensor(tmp[b][:, :], st[b][:, :], R[b][:, :], ALU.subtract).then_inc(S["diff"], 1)
                for b in range(nb):
                    wait(dve, ph, f"diff{r}", t, b)
                    v.tensor_tensor(tmp[b][:, :], tmp[b][:, :], Z[b][:, :], ALU.mult).then_inc(S["scaled"], 1)
                for b in range(nb):
                    wait(dve, ph, f"scaled{r}", t, b)
                    v.tensor_tensor(Y[b][:, :], tmp[b][:, :], R[b][:, :], ALU.add).then_inc(S["hidden"], 1)

            def sum_x(ph, t, nb):
                for b in range(nb):
                    wait(dve, ph, "hidden1", t, b)
                    v.tensor_tensor(Y[b][:, :], Y[b][:, :], X[b][:, :], ALU.add).then_inc(S["summed"], 1)

            def chain_dve(ph):
                def body(t, nb):
                    norm_of(ph, t, nb, 0, X)
                    for i in range(3):
                        sage_layer(ph, t, nb, i)
                    norm_of(ph, t, nb, 4, X)
                    gates(ph, t, nb, 0, False)
                    gates(ph, t, nb, 1, False)
                    sum_x(ph, t, nb)
                    norm_of(ph, t, nb, 5, X)
                    if ph == "main":
                        norm_of(ph, t, nb, 6, X)
                each_batch(dve, ph, body)

            chain_dve("main")
            dve.wait_ge(map_copied, 1 + 2 * TE)
            v.tensor_scalar(idf[:, :], g("src_map"), 0.0, None, ALU.is_equal)
            v.tensor_scalar(idf2[:, :], g("slot1"), float(SLOTS), None, ALU.add).then_inc(ids_ready, 1)
            dve.wait_ge(ids_ready, 3)
            v.tensor_tensor(idf2[:, :], idf2[:, :], idf[:, :], ALU.mult).then_inc(ids_ready, 1)
            dve.wait_ge(ids_ready, 4)
            v.scalar_tensor_tensor(g("src_slot"), g("src_map"), -1.0, idf2[:, :], ALU.add, ALU.add)
            v.tensor_scalar(g("dst_slot"), g("dst_map"), -1.0, 0.0, ALU.add, ALU.max).then_inc(ids_ready, 1)
            chain_dve("src")

            def scan(ph, t, b, k, dst, decay, data, op0=ALU.mult, op1=ALU.add, shift=0):
                per = scan_base[ph][1]
                last = COLS - 1 + shift
                for h in range(H):
                    r, other = slice(h * D, h * D + D), slice((1 - h) * D, (1 - h) * D + D)
                    from_ = dst[(b - 1) % B] if h == 0 else dst[b]
                    n = scan_place(ph, t, b, k) + h
                    if not (isinstance(t, int) and t * 2 * per + n == 0):
                        dve.wait_ge(scanned, t * (2 * per) + n)
                    v.tensor_copy(carry[r, :], from_[other, last:last + 1]).then_inc(carried, 1)
                    dve.wait_ge(carried, t * (2 * per) + (n + 1))
                    v.tensor_tensor_scan(dst[b][r, shift:shift + COLS], decay[b][r, :], data(b)[r, :], carry[r, :],
                                         op0, op1).then_inc(scanned, 1)

            def d0(t, nb):
                ph = "d0"
                for b in range(nb):
                    wait_loaded(dve, ph, t, b)
                    if not (isinstance(t, int) and t == 0):
                        dve.wait_ge(kept[b], t * (4 * KEEPS[ph]) + 1)
                    v.tensor_tensor(SAME[b][:, :], IDS[b][:, 0:COLS], IDS[b][:, 1:COLS + 1], ALU.is_equal)\
                        .then_inc(S["same"], 1)
                for b in range(nb):
                    wait(dve, ph, "hidden_mm", t, b)
                    wait(dve, ph, "x_in", t, b)
                    v.tensor_scalar(Z[b][:, :], PA[b][:, :], 0.01, None, ALU.mult).then_inc(S["small_slope"], 1)
                    v.scalar_tensor_tensor(W[b][:, :], X[b][:, :], 0.01, X[b][:, :], ALU.mult, ALU.max)
                    wait(dve, ph, "small_slope", t, b)
                    v.tensor_tensor(Z[b][:, :], PA[b][:, :], Z[b][:, :], ALU.max).then_inc(S["leaky"], 1)
                    wait(dve, ph, "same", t, b)
                    v.tensor_scalar(R[b][:, :], SAME[b][:, :], -1.0, BIG, ALU.add, ALU.mult).then_inc(S["penalty"], 1)
                for b in range(nb):
                    wait(dve, ph, "logits", t, b)
                    wait(dve, ph, "penalty", t, b)
                    scan(ph, t, b, 0, MX, R, lambda b: PB[b], ALU.add, ALU.max, shift=1)
                    wait_scans(dve, ph, t, b, 1)
                    for h in range(H):
                        r, other = slice(h * D, h * D + D), slice((1 - h) * D, (1 - h) * D + D)
                        from_ = MX[(b - 1) % B] if h == 0 else MX[b]
                        last = v.tensor_copy(MX[b][r, 0:1], from_[other, COLS:COLS + 1])
                    last.then_inc(S["max_before"], 1)
                    v.tensor_tensor(R[b][:, :], PB[b][:, :], MX[b][:, 1:COLS + 1], ALU.subtract)\
                        .then_inc(S["new_weight"], 1)
                    wait(dve, ph, "max_before", t, b)
                    v.tensor_tensor(DC[b][:, :], MX[b][:, 0:COLS], MX[b][:, 1:COLS + 1], ALU.subtract)\
                        .then_inc(S["max_step"], 1)
                    wait(dve, ph, "max_step", t, b)
                    v.tensor_scalar(DC[b][:, :], DC[b][:, :], 0.0, None, ALU.min).then_inc(S["max_shift"], 1)
                    scan(ph, t, b, 1, DEG, SAME, lambda b: ones)
                    wait_scans(dve, ph, t, b, 2)
                    v.reciprocal(MSG[b][:, :], DEG[b][:, :]).then_inc(S["inv_degree"], 1)
                for b in range(nb):
                    wait(dve, ph, "decay_exp", t, b)
                    v.tensor_tensor(DC[b][:, :], DC[b][:, :], SAME[b][:, :], ALU.mult)
                    wait(dve, ph, "weight_exp", t, b)
                    v.tensor_tensor(Z[b][:, :], R[b][:, :], XS[b][:, :], ALU.mult).then_inc(S["weighted"], 1)
                    wait(dve, ph, "weighted", t, b)
                    scan(ph, t, b, 2, DN, DC, lambda b: R[b])
                    scan(ph, t, b, 3, AG_n, DC, lambda b: Z[b])
                    wait_scans(dve, ph, t, b, 4)
                    v.reciprocal(W[b][:, :], DN[b][:, :]).then_inc(S["inv_den"], 1)
                    wait(dve, ph, "inv_den", t, b)
                    v.tensor_tensor(AG[b][:, :], AG_n[b][:, :], W[b][:, :], ALU.mult).then_inc(S["mixed"], 1)
                norm_of(ph, t, nb, 0, X)
            AG_n = Y
            each_batch(dve, "d0", d0)

            def gather_scan(ph, t, nb, invert):
                for b in range(nb):
                    wait_loaded(dve, ph, t, b)
                    wait(dve, ph, "turned_in", t, b)
                    scan(ph, t, b, 0, AGS, SAME, lambda b: PA[b])
                    if invert:
                        wait_scans(dve, ph, t, b, 1)
                        v.tensor_tensor(AG[b][:, :], AGS[b][:, :], DEG[b][:, :], ALU.mult).then_inc(S["mean"], 1)
            AGS = DN

            def sage_phase(ph, i):
                def body(t, nb):
                    gather_scan(ph, t, nb, True)
                    sage_layer(ph, t, nb, i)
                    if i == 2:
                        norm_of(ph, t, nb, 4, X)
                each_batch(dve, ph, body)
            for i in range(3):
                sage_phase(f"d{1 + i}", i)

            def gru_phase(ph, r):
                st = X if r == 0 else Y
                def body(t, nb):
                    for b in range(nb):
                        wait_loaded(dve, ph, t, b)
                        v.tensor_tensor(W[b][:, :], st[b][:, :], DEG[b][:, :], ALU.mult)\
                            .then_inc(S["times_degree"], 1)
                        wait(dve, ph, "turned_in", t, b)
                        scan(ph, t, b, 0, AG, SAME, lambda b: PA[b])
                        wait(dve, ph, "turned_edge", t, b)
                        scan(ph, t, b, 1, EF, SAME, lambda b: PB[b])
                    gates(ph, t, nb, r, True)
                    if r == 1:
                        sum_x(ph, t, nb)
                        norm_of(ph, t, nb, 5, X)
                each_batch(dve, ph, body)
            for b in range(B):
                last = v.memset(edges[b][:, :].rearrange("p (s f) -> p s f", f=D)[:, :, 4:5], 1.0)
            last.then_inc(ones_set, 1)
            gru_phase("d4", 0)
            gru_phase("d5", 1)

            def d6(t, nb):
                for b in range(nb):
                    wait_loaded(dve, "d6", t, b)
                    wait(dve, "d6", "message", t, b)
                    scan("d6", t, b, 0, AGS, SAME, lambda b: PA[b])
                    wait_scans(dve, "d6", t, b, 1)
                    v.tensor_tensor(AG[b][:, :], AGS[b][:, :], DEG[b][:, :], ALU.mult).then_inc(S["mean"], 1)
                norm_of("d6", t, nb, 6, X, "6d")
            each_batch(dve, "d6", d6)

        @block.sync
        def _(sp):
            dma = nc.sync.dma_start
            FW = TE * 8 + 1
            sp.wait_ge(fills, 3)
            dma(dst_pad.rearrange("(p c) -> p c", p=P), fill[:, 0, :]).then_inc(pad_filled, 16)
            dma(src_pad.rearrange("(p c) -> p c", p=P), fill[:, 1, 0:FW - 1]).then_inc(pad_filled, 16)
            dma(node_slot.rearrange("(p c) o -> p (c o)", p=80), zero_map[:, :]).then_inc(map_zero, 16)
            sp.wait_ge(zeroed, 1)
            for to, from_ in weight_loads:
                dma(to, from_).then_inc(weights_in, 16)

            def node_rows(n):
                first = min(n * TILE, N - TILE) if isinstance(n, int) else n * TILE
                return bass.ds(first, TILE)

            def load_nodes(t, b):
                dma(rows[b][:, :], a["x"][node_rows(t + b), :].rearrange("(p j) f -> p (j f)", p=P))\
                    .then_inc(loaded[b], 16)
            for b in range(B):
                load_nodes(0, b)

            sp.wait_ge(pad_filled, 32)
            dma(dst_pad[1:1 + E].rearrange("(a c) -> a c", a=8), a["dst"].rearrange("(a c) -> a c", a=8))\
                .then_inc(pad_put, 16)
            dma(src_pad[0:E].rearrange("(a c) -> a c", a=8), a["src"].rearrange("(a c) -> a c", a=8))\
                .then_inc(pad_put, 16)
            sp.wait_ge(pad_put, 32)
            for name, src, off in (("dst_of", dst_pad, 1), ("dst_next", dst_pad, 2), ("src_of", src_pad, 0)):
                v = src[off:off + SLOTS].rearrange("(g h p q) -> h p g q", h=H, p=P, q=Q)
                for h in range(H):
                    dma(ids[name][:, :].rearrange("p (g h q) -> p g h q", h=H, q=Q)[:, :, h, :], v[h]).then_inc(ids_in, 16)
            dma(ids["src_rows"][:, :].rearrange("p (g j) -> p g j", j=8),
                src_pad[0:SLOTS].rearrange("(g p j) -> p g j", p=P, j=8)).then_inc(ids_in, 16)

            def store_nodes(t, b):
                wait(sp, "main", "rows_out7", t, b)
                if isinstance(t, int) and t + b == TM - 1:
                    for c in range(B):
                        sp.wait_ge(stored[c], 16 * (slot_uses("main", c) - (c == b)))
                dma(out[node_rows(t + b), :].rearrange("(p j) f -> p (j f)", p=P), rows_o[b][:, :])\
                    .then_inc(stored[b], 16)

            full = TM // B * B
            with sp.Fori(0, full - 2 * B + 1, B) as t:
                for b in range(B):
                    wait(sp, "main", "turned_in", t, b)
                    load_nodes(t + B, b)
                for b in range(B):
                    store_nodes(t, b)
            for b in range(TM - full):
                wait(sp, "main", "turned_in", full - B, b)
                load_nodes(full, b)
            for b in range(B):
                store_nodes(full - B, b)
            for b in range(TM - full):
                store_nodes(full, b)

            def tile_rows(n):
                return bass.ds(n * P, P)

            def store_level(ph, t, b, level, order):
                wait(sp, ph, f"rows_out{level}", t, b)
                settle(sp)
                if order == "any":
                    to = table[level][bass.ds((t + b) * TILE + SLOTS, TILE), :]
                    dma(to.rearrange("(p j) f -> p (j f)", p=P), rows_o[b][:, :]).then_inc(stored[b], 16)
                else:
                    for h in range(H):
                        to = table[level][bass.ds((t + b) * TILE + h * COLS, COLS), :]
                        dma(to.rearrange("(p q) f -> p q f", q=Q),
                            rows_o[b][:, :].rearrange("p (q h f) -> p q h f", h=H, q=Q)[:, :, h, :]).then_inc(stored[b], 16)

            def src_stores(t, nb):
                for level in range(1, 7):
                    for b in range(nb):
                        store_level("src", t, b, level, "any")
            each_batch(sp, "src", src_stores)

            def load_edges(t, b, attr):
                w = attr.shape[1]
                to = edges[b][:, :].rearrange("p (q h f) -> p q h f", h=H, q=Q)
                short = isinstance(t, int) and t + b == TE - 1
                for h in range(H):
                    if short:
                        from_ = attr[(TE - 1) * TILE:E, :].rearrange("(p q) f -> p q f", q=Q)
                        dma(to[0:LAST_P, :, h, 0:w], from_).then_inc(loaded[b], 16)
                    else:
                        from_ = attr[bass.ds((t + b) * TILE + h * COLS, COLS), :].rearrange("(p q) f -> p q f", q=Q)
                        dma(to[:, :, h, 0:w], from_).then_inc(loaded[b], 16)

            def d0(t, nb):
                for b in range(nb):
                    wait_before(sp, "d0", "turned_out1", t, b)
                    settle(sp)
                    for h in range(H):
                        ids_of = dst_pad[bass.ds((t + b) * TILE + h * COLS, COLS + 1)]
                        dma(IDS[b][h * D:h * D + D, :],
                            ids_of.rearrange("(o c) -> o c", o=1).to_broadcast([D, COLS + 1])).then_inc(loaded[b], 16)
                    load_edges(t, b, a["edge_attr_16"])
                for b in range(nb):
                    for what, buf, stage in ((same_d, SAME, "same"), (degree_d, DEG, "inv_degree"),
                                             (inv_degree_d, MSG, "inv_degree"), (state[1], X, "normed0")):
                        wait(sp, "d0", stage, t, b)
                        settle(sp)
                        dma(what[tile_rows(t + b), :], buf[b][:, :]).then_inc(kept[b], 16)
                    store_level("d0", t, b, 1, "edge")
            wait_phase(sp, "src", "turned_out6")
            sp.wait_ge(prep_dve, 3)
            each_batch(sp, "d0", d0)

            def phase(ph, loads, attr, level, keep):
                after = {2: "added0", 3: "added1", 4: "normed4", 5: "hidden0", 6: "normed5"}.get(level)

                def body(t, nb):
                    for b in range(nb):
                        wait_before(sp, ph, f"turned_out{level}", t, b)
                        if keep is not None:
                            settle(sp)
                            sp.wait_ge(kept[b], t * (4 * KEEPS[ph]) + (1 + before(KEEPS, ph, b)))
                        settle(sp)
                        for from_, buf in loads:
                            dma(buf[b][:, :], from_[tile_rows(t + b), :]).then_inc(loaded[b], 16)
                        if attr is not None:
                            load_edges(t, b, attr)
                    if keep is not None:
                        for b in range(nb):
                            wait(sp, ph, after, t, b)
                            settle(sp)
                            dma(state[level][tile_rows(t + b), :], keep[b][:, :]).then_inc(kept[b], 16)
                            store_level(ph, t, b, level, "edge")
                each_batch(sp, ph, body)

            def phase_over(ph, level):
                wait_phase(sp, ph, f"turned_out{level}")
                for b in range(B):
                    sp.wait_ge(kept[b], 1 + before(KEEPS, ph, b) + 16 * KEEPS[ph] * slot_uses(ph, b))

            phase_over("d0", 1)
            phase("d1", [(state[1], X), (same_d, SAME), (inv_degree_d, DEG)], None, 2, Y)
            phase_over("d1", 2)
            phase("d2", [(state[2], Y), (same_d, SAME), (inv_degree_d, DEG)], None, 3, Y)
            phase_over("d2", 3)
            phase("d3", [(state[1], X), (state[3], Y), (same_d, SAME), (inv_degree_d, DEG)], None, 4, X)
            phase_over("d3", 4)
            phase("d4", [(state[4], X), (same_d, SAME), (degree_d, DEG)], a["edge_attr_4"], 5, Y)
            phase_over("d4", 5)
            phase("d5", [(state[4], X), (state[5], Y), (same_d, SAME), (degree_d, DEG)], a["edge_attr_4"], 6, X)
            phase_over("d5", 6)
            phase("d6", [(state[6], X), (same_d, SAME), (inv_degree_d, DEG)], a["edge_attr_32"], 7, None)
            for b in range(B):
                sp.wait_ge(stored[b], before(STORES, "d6", b))

        @block.gpsimd
        def _(gp):
            g = nc.gpsimd
            for s in kept + [map_copied]:
                gp.sem_inc(s, 1)
            g.memset(fill[:, 0, :], -1).then_inc(fills, 1)
            g.memset(fill[:, 1, :], 0).then_inc(fills, 1)
            g.memset(zero_map[:, :], 0).then_inc(fills, 1)
            g.memset(wraw[:, :, :], 0.0)
            g.memset(bias[:, :], 0.0)
            g.memset(w3e[:, :], 0.0).then_inc(zeroed, 1)
            g.memset(ident[:, :], 0.0).then_inc(ident_zero, 1)
            gp.wait_ge(ident_zero, 1)
            g.affine_select(out=ident[:, :], in_=ident[:, :], compare_op=ALU.not_equal, fill=1.0, base=0,
                            pattern=[[-1, P]], channel_multiplier=1).then_inc(zeroed, 1)
            g.iota(ids["slot1"][:, :], [[TILE, TE], [COLS, H], [1, Q]], base=1, channel_multiplier=Q)\
                .then_inc(iota_done, 1)

            def stage_ids(t, b, first, per, pairs):
                for k, (to, name) in enumerate(pairs):
                    g.tensor_copy(to, ids[name][:, bass.ds((t + b) * 8, 8)]).then_inc(staged, 1)
                gp.wait_ge(staged, t * per + (first + per * (b + 1)))
                settle(gp)

            def at(idx, k):
                return bass.IndirectOffsetOnAxis(ap=idx[:, k:k + 1], axis=0)

            full = TE // B * B

            gp.wait_ge(ids_ready, 2)
            gp.wait_ge(map_zero, 16)

            def put(t, nb):
                for b in range(nb):
                    if not (isinstance(t, int) and t == 0):
                        gp.wait_ge(map_put[b], t * (4 * 8))
                    stage_ids(t, b, 0, 2, [(gi[b][:, 0:8], "put_row"), (gv[b][:, 0:8], "slot1")])
                    for k in range(8):
                        g.indirect_dma_start(node_slot, at(gi[b], k), gv[b][:, k:k + 1], None,
                                             bounds_check=N - 1, oob_is_err=False).then_inc(map_put[b], 16)
            each_batch(gp, "src", put, peel=True)
            for b in range(B):
                gp.wait_ge(map_put[b], 16 * 8 * -(-(TE - b) // B))

            def get(t, nb):
                for b in range(nb):
                    if not (isinstance(t, int) and t == 0):
                        gp.wait_ge(map_copied, t * 2 + 1)
                    stage_ids(t, b, 2 * TE, 2, [(gi[b][:, 0:8], "src_of"), (gi[b][:, 8:16], "dst_row")])
                    for k in range(16):
                        g.indirect_dma_start(gv[b][:, k:k + 1], None, node_slot, at(gi[b], k))\
                            .then_inc(map_got[b], 16)
                for b in range(nb):
                    gp.wait_ge(map_got[b], t * (4 * 16) + 16 * 16)
                    for k, name in enumerate(("src_map", "dst_map")):
                        g.tensor_copy(ids[name][:, bass.ds((t + b) * 8, 8)], gv[b][:, 8 * k:8 * k + 8])\
                            .then_inc(map_copied, 1)
            each_batch(gp, "src", get)

            def gather_tile(ph, sources, first, t, b):
                per = len(sources)
                if not (isinstance(t, int) and t * 4 * GATHERS[ph] + before(GATHERS, ph, b) == 0):
                    gp.wait_ge(gathered[b], t * (4 * GATHERS[ph]) + before(GATHERS, ph, b))
                wait_before(gp, ph, "turned_in", t, b)
                stage_ids(t, b, first, per, [(gi[b][:, 8 * k:8 * k + 8], s[0]) for k, s in enumerate(sources)])
                for k, (name, from_, to, order) in enumerate(sources):
                    for j in range(8):
                        c = j if order == "any" else (j % Q) * H + j // Q
                        g.indirect_dma_start(to[b][:, c * D:c * D + D], None, from_, at(gi[b], 8 * k + j))\
                            .then_inc(gathered[b], 16)

            def gathers(ph, sources, first):
                def body(t, nb):
                    for b in range(nb):
                        gather_tile(ph, sources, first, t, b)
                each_batch(gp, ph, body, peel=(ph == "src"))

            wait_phase(gp, "main", "turned_in")
            gathers("src", [("src_rows", a["x"], rows, "any")], 4 * TE)
            wait_phase(gp, "src", "turned_in")
            gathers("d0", [("src_of", a["x"], rows, "edge"), ("dst_row", a["x"], rows2, "edge")], 5 * TE)
            gp.wait_ge(ids_ready, 5)

            def table_ready(level, ph):
                for b in range(B):
                    gp.wait_ge(stored[b], before(STORES, ph, b) + 16 * STORES[ph] * slot_uses(ph, b))

            for k in range(1, 6):
                table_ready(k, f"d{k - 1}")
                gathers(f"d{k}", [("src_slot", table[k], rows, "edge")], (6 + k) * TE)
            table_ready(6, "d5")

            sources = [("src_slot", table[6], rows, "edge"), ("dst_slot", table[6], rows2, "edge")]
            PER = 3

            def last_gather(t, b, n):
                gp.wait_ge(gathered[b], t * (4 * GATHERS["d6"]) + (before(GATHERS, "d6", b)))
                wait_before(gp, "d6", "turned_in", t, b)
                for k, (name, from_, to, order) in enumerate(sources):
                    g.tensor_copy(gi[b][:, 8 * k:8 * k + 8], ids[name][:, bass.ds((t + b) * 8, 8)]).then_inc(staged, 1)
                gp.wait_ge(staged, n)
                settle(gp)
                for k, (name, from_, to, order) in enumerate(sources):
                    for j in range(8):
                        c = (j % Q) * H + j // Q
                        g.indirect_dma_start(to[b][:, c * D:c * D + D], None, from_, at(gi[b], 8 * k + j))\
                            .then_inc(gathered[b], 16)

            def last_scatter(t, b, n):
                if not (isinstance(t, int) and t == 0):
                    gp.wait_ge(scattered[b], t * (4 * 8))
                g.tensor_copy(gv[b][:, 0:8], ids["put_row"][:, bass.ds((t + b) * 8, 8)]).then_inc(staged, 1)
                gp.wait_ge(staged, n)
                wait(gp, "d6", "rows_out7", t, b)
                settle(gp)
                for j in range(8):
                    c = (j % Q) * H + j // Q
                    g.indirect_dma_start(out, at(gv[b], j), rows_o[b][:, c * D:c * D + D], None,
                                         bounds_check=N - 1, oob_is_err=False).then_inc(scattered[b], 16)

            s0 = 12 * TE
            for b in range(B):
                last_gather(0, b, s0 + 2 * (b + 1))
            s0 += 2 * B

            def last_batch(t):
                for b in range(B):
                    last_gather(t + B, b, t * PER + (s0 + 2 * (b + 1)))
                for b in range(B):
                    last_scatter(t, b, t * PER + (s0 + 2 * B + b + 1))
            last_batch(0)
            with gp.Fori(B, full - 2 * B + 1, B) as t:
                last_batch(t)
            s0 += PER * (full - B)
            rem = TE - full
            for b in range(rem):
                last_gather(full, b, s0 + 2 * (b + 1))
            for b in range(B):
                last_scatter(full - B, b, s0 + 2 * rem + b + 1)
            for b in range(rem):
                last_scatter(full, b, s0 + 2 * rem + B + b + 1)
            for b in range(B):
                gp.wait_ge(scattered[b], 16 * 8 * slot_uses("d6", b))


def kernel(**inputs):
    import numpy as np
    import concourse.bacc as bacc
    from concourse.bass_utils import run_bass_kernel_spmd

    nc = bacc.Bacc("TRN2", target_bir_lowering=False, num_devices=1)
    arrays = {name: np.ascontiguousarray(x) for name, x in inputs.items()}
    aps = {name: nc.dram_tensor(f"in_{name}", x.shape, mybir.dt.from_np(x.dtype), kind="ExternalInput").ap()
           for name, x in arrays.items()}
    out = nc.dram_tensor("out", arrays["x"].shape, mybir.dt.from_np(arrays["x"].dtype), kind="ExternalOutput").ap()
    build(nc, aps, out)
    result = run_bass_kernel_spmd(nc, [{f"in_{name}": x for name, x in arrays.items()}], core_ids=[0])
    return result.results[0]["out"]
```

```python
from contextlib import ExitStack

import concourse.bass as bass
from concourse import mybir

F32 = mybir.dt.float32
I32 = mybir.dt.int32
ALU = mybir.AluOpType
ACT = mybir.ActivationFunctionType

P = 128
D = 64
H = 2
COLS = 512
TILE = H * COLS
Q = COLS // P
B = 4
EPS = 1e-5
BIG = 1e30
OUTSIDE = 1 << 20


def build(nc, a, out):
    N = a["x"].shape[0]
    E = a["src"].shape[0]
    TM = -(-N // TILE)
    TE = -(-E // TILE)
    SLOTS = TE * TILE
    LAST_E = E - (TE - 1) * TILE
    LAST_P = LAST_E // Q
    assert LAST_E % Q == 0 and LAST_E <= COLS and N < OUTSIDE and N % 8 == 0

    norm = lambda l: [f"{s}{l}" for s in ("centred", "squared", "variance", "logvar", "rstd", "normed")]
    sage = lambda i: norm(1 + i) + [f"scaled_norm{i}", f"added{i}"] + (["residual_mm", "relu"] if i == 0 else [])
    gru = lambda r: [f"{s}{r}" for s in ("gate_r", "gate_z", "gate_n", "sig_r", "sig_z", "reset", "tanh",
                                         "diff", "scaled", "hidden")]
    save = lambda l: [f"turned_out{l}", f"rows_out{l}"]
    chain = (["turned_in", "x_in"] + norm(0) + sage(0) + sage(1) + sage(2) + norm(4) + gru(0) + gru(1)
             + ["summed"] + norm(5))
    saves = sum((save(l) for l in range(1, 7)), [])
    gather2 = ["turned_in", "turned_dst", "src_in", "x_in", "turned_edge", "edge_in"]
    PHASES = [
        ("main", TM, chain + norm(6) + save(7)),
        ("src", TE, chain + saves),
        ("d0", TE, gather2 + ["same", "hidden_mm", "small_slope", "leaky", "penalty", "logits", "max_before",
                              "new_weight", "max_step", "max_shift", "log_degree", "inv_degree", "decay_exp", "weight_exp",
                              "weighted", "log_den", "inv_den", "mixed"] + norm(0) + save(1)),
        ("d1", TE, ["turned_in", "mean"] + sage(0) + save(2)),
        ("d2", TE, ["turned_in", "mean"] + sage(1) + save(3)),
        ("d3", TE, ["turned_in", "mean"] + sage(2) + norm(4) + save(4)),
        ("d4", TE, ["turned_in", "turned_edge", "times_degree", "message", "message_in", "reset_sum"] + gru(0)
         + save(5)),
        ("d5", TE, ["turned_in", "turned_edge", "times_degree", "message", "message_in", "reset_sum"] + gru(1)
         + ["summed"] + norm(5) + save(6)),
        ("d6", TE, gather2 + ["hidden_mm", "hidden_relu0", "hidden_relu1", "message", "mean"] + norm(6) + save(7)),
    ]
    tiles_of = {ph: tiles for ph, tiles, _ in PHASES}
    kind = lambda stage: stage.rstrip("0123456789")
    turn, turns, base, count = {}, {}, {}, {}
    for ph, tiles, stages in PHASES:
        for s in stages:
            turn[ph, s] = turns.get((ph, kind(s)), 0)
            turns[ph, kind(s)] = turn[ph, s] + 1
        for k in dict.fromkeys(map(kind, stages)):
            base[ph, k] = count.get(k, 0)
            count[k] = base[ph, k] + turns[ph, k] * tiles
    SCANS = [("d0", 4)] + [(f"d{k}", 1) for k in (1, 2, 3)] + [("d4", 2), ("d5", 2), ("d6", 1)]
    scan_base, n = {}, 0
    for ph, k in SCANS:
        scan_base[ph] = (n, k)
        n += 2 * k * TE

    def slot_uses(ph, b):
        return -(-(tiles_of[ph] - b) // B)

    LOADS = {"main": 1, "d0": 4, "d1": 3, "d2": 3, "d3": 4, "d4": 5, "d5": 6, "d6": 5}
    GATHERS = {"src": 8, "d0": 16, "d1": 8, "d2": 8, "d3": 8, "d4": 8, "d5": 8, "d6": 16}
    STORES = {"main": 1, "src": 6, "d0": 2, "d1": 2, "d2": 2, "d3": 2, "d4": 2, "d5": 2}
    KEEPS = {"d0": 4, "d1": 1, "d2": 1, "d3": 1, "d4": 1, "d5": 1}
    SCATTERS = {"d6": 8}

    def before(table, ph, b):
        v = 0
        for name, _, _ in PHASES:
            if name == ph:
                return v
            v += 16 * table.get(name, 0) * slot_uses(name, b)
        return v

    with ExitStack() as ctx:
        def sb(name, shape, dt=F32):
            return ctx.enter_context(nc.sbuf_tensor(name, shape, dt))

        def dram(name, shape, dt=F32):
            return nc.dram_tensor(name, shape, dt, kind="Internal").ap()

        def sem(name):
            return ctx.enter_context(nc.semaphore(name))

        S = {k: sem(k) for k in count}
        loaded = [sem(f"loaded{b}") for b in range(B)]
        gathered = [sem(f"gathered{b}") for b in range(B)]
        stored = [sem(f"stored{b}") for b in range(B)]
        kept = [sem(f"kept{b}") for b in range(B)]
        scattered = [sem(f"scattered{b}") for b in range(B)]
        carried, scanned = sem("carried"), sem("scanned")
        weights_in, zeroed, consts, prep_pe, prep_dve = (sem(n) for n in (
            "weights_in", "zeroed", "consts", "prep_pe", "prep_dve"))
        pad_filled, pad_put, ids_in, ids_ready, fills, iota_done, id_steps, ident_zero = (
            sem(n) for n in ("pad_filled", "pad_put", "ids_in", "ids_ready", "fills", "iota_done", "id_steps",
                             "ident_zero"))
        map_zero, map_copied, staged, ones_set, passed = (
            sem(n) for n in ("map_zero", "map_copied", "staged", "ones_set", "passed"))
        map_put = [sem(f"map_put{b}") for b in range(B)]
        map_got = [sem(f"map_got{b}") for b in range(B)]

        dst_pad = dram("dst_pad", (P * (TE * 8 + 1),), I32)
        src_pad = dram("src_pad", (SLOTS,), I32)
        node_slot = dram("node_slot", (N, 1), I32)
        table = {l: dram(f"table{l}", (2 * SLOTS, D)) for l in range(1, 7)}
        state = {l: dram(f"state{l}", (TE * P, COLS)) for l in range(1, 7)}
        same_d = dram("same_d", (TE * P, COLS))
        degree_d = dram("degree_d", (TE * P, COLS))
        inv_degree_d = dram("inv_degree_d", (TE * P, COLS))

        def ring(name, cols=COLS, dt=F32):
            return [sb(f"{name}{b}", [P, cols], dt) for b in range(B)]

        rows, rows2, edges, rows_o = ring("rows"), ring("rows2"), ring("edges"), ring("rows_o")
        X, Y, Z, R, W = ring("X"), ring("Y"), ring("Z"), ring("R"), ring("W")
        XS, EF, AG, DN, DC, MSG = ring("XS"), ring("EF"), ring("AG"), ring("DN"), ring("DC"), ring("MSG")
        SAME, DEG = ring("SAME"), ring("DEG")
        MX = ring("MX", COLS + 1)
        IDS = ring("IDS", COLS + 1, I32)
        carry = sb("carry", [P, 1])
        PA = [ctx.enter_context(nc.psum_tensor(f"PA{b}", [P, COLS], F32)) for b in range(B)]
        PB = [ctx.enter_context(nc.psum_tensor(f"PB{b}", [P, COLS], F32)) for b in range(B)]

        NT = 10
        names = (["wr0", "wr1", "wr2", "wfc", "wl0", "wl1", "wl2", "wn", "w1x", "w1e", "w2", "wres"]
                 + [f"{n}{t}" for t in range(2) for n in ("msg_s", "msg_d", "msg_e", "ih_r", "ih_z", "ih_n",
                                                          "hh_r", "hh_z", "hh_n")])
        wraw = sb("wraw", [P, len(names), P])
        wat = {n: wraw[:, i, :] for i, n in enumerate(names)}
        wturned = sb("wturned", [P, NT, P])
        wcentred = sb("wcentred", [P, 9, P])
        wc = {n: wcentred[:, i, :] for i, n in enumerate(names[:8] + ["w2"])}
        w3s, w3d, w3e = sb("w3s", [P, P]), sb("w3d", [P, P]), sb("w3e", [P, P])
        w3o = sb("w3o", [P, D])
        ident, ones_block, mean_block, centre = (sb(n, [P, P]) for n in ("ident", "ones_block", "mean_block", "centre"))
        att_f, att_r = sb("att_f", [P, P]), sb("att_r", [P, P])
        ones = sb("ones", [P, COLS])
        eps = sb("eps", [P, 1])
        cols = ["bias0", "bl0", "bl1", "bl2", "bfc", "zero", "bn", "b3", "g0", "g1", "g2", "be0", "be1", "be2",
                "bres", "att_f", "att_r", "ih_r0", "ih_z0", "ih_n0", "hh_r0", "hh_z0", "hh_n0",
                "ih_r1", "ih_z1", "ih_n1", "hh_r1", "hh_z1", "hh_n1", "b2"]
        bias = sb("bias", [P, 32])
        bcol = {n: bias[:, i:i + 1] for i, n in enumerate(cols)}
        NC = 8
        bcent = sb("bcent", [P, NC])
        b1col = sb("b1col", [P, 1])
        gate_b = sb("gate_b", [P, 4])
        norm_bias = {0: 0, 1: 1, 2: 2, 3: 3, 4: 4, 5: 5, 6: 6, "6d": 7}

        ids = {n: sb(n, [P, TE * 8], I32) for n in
               ("dst_of", "dst_next", "src_of", "src_rows", "dst_row", "put_row", "slot1", "src_map", "dst_map",
                "src_slot", "dst_slot")}
        idf = sb("idf", [P, TE * 8])
        idf2 = sb("idf2", [P, TE * 8])
        fill = sb("fill", [P, 2, TE * 8 + 1], I32)
        zero_map = sb("zero_map", [80, N // 80], I32)
        gi = [sb(f"gi{b}", [P, 16], I32) for b in range(B)]
        gv = [sb(f"gv{b}", [P, 16], I32) for b in range(B)]

        weight_loads = []
        def load_block(name, src, row=0, k=D):
            for h in range(H):
                weight_loads.append((wraw[h * D + row:h * D + row + k, names.index(name), h * D:h * D + src.shape[-1]],
                                     src))
        for i in range(3):
            load_block(f"wr{i}", a["L1_gnn_w_r"][i])
            load_block(f"wl{i}", a["L1_gnn_w_l"][i])
        load_block("wfc", a["L1_gnn_w_fc"])
        load_block("wn", a["L3_gnn_Wn"])
        load_block("w1x", a["L0_gnn_W1"][:, 0:D])
        load_block("w1e", a["L0_gnn_W1"][:, D:])
        load_block("w2", a["L0_gnn_W2"])
        load_block("wres", a["L1_gnn_w_res"])
        for t in range(2):
            m = a["L2_gnn_W_msg"][t]
            load_block(f"msg_s{t}", m[0:D, :])
            load_block(f"msg_d{t}", m[D:2 * D, :])
            load_block(f"msg_e{t}", m[2 * D:, :], 0, 4)
            load_block(f"msg_e{t}", a["L2_gnn_b_msg"][t:t + 1, :], 4, 1)
            for k, g in enumerate("rzn"):
                load_block(f"ih_{g}{t}", a["L2_gnn_W_ih"][t][:, k * D:k * D + D])
                load_block(f"hh_{g}{t}", a["L2_gnn_W_hh"][t][:, k * D:k * D + D])
        w3 = a["L3_gnn_W1"]
        for h in range(H):
            weight_loads += [(w3s[h * D:h * D + D, :], w3[0:D, :]), (w3d[h * D:h * D + D, :], w3[D:2 * D, :]),
                             (w3e[h * D:h * D + 32, :], w3[2 * D:, :])]
        weight_loads.append((w3o[:, :], a["L3_gnn_W2"]))
        column = lambda x: x.rearrange("(f o) -> f o", o=1)
        weight_loads.append((b1col[:, :], column(a["L3_gnn_b1"])))
        vectors = {"bias0": a["L0_gnn_bias"], "bfc": a["L1_gnn_b_fc"], "bres": a["L1_gnn_b_res"],
                   "bn": a["L3_gnn_bn"], "b2": a["L3_gnn_b2"],
                   "att_f": a["L0_gnn_attn"][0:D], "att_r": a["L0_gnn_attn"][D:2 * D]}
        for i in range(3):
            vectors |= {f"bl{i}": a["L1_gnn_b_l"][i], f"g{i}": a["L1_gnn_gamma"][i], f"be{i}": a["L1_gnn_beta"][i]}
        for t in range(2):
            for k, g in enumerate("rzn"):
                vectors |= {f"ih_{g}{t}": a["L2_gnn_b_ih"][t][k * D:k * D + D],
                            f"hh_{g}{t}": a["L2_gnn_b_hh"][t][k * D:k * D + D]}
        for name, vec in vectors.items():
            for h in range(H):
                weight_loads.append((bias[h * D:h * D + D, cols.index(name):cols.index(name) + 1], column(vec)))
        n_weight_dmas = len(weight_loads)

        block = ctx.enter_context(nc.Block())

        def each_batch(eng, ph, body, peel=False):
            full = tiles_of[ph] // B * B
            if peel:
                body(0, B)
            with eng.Fori(B if peel else 0, full - B + 1, B) as t:
                body(t, B)
            if tiles_of[ph] > full:
                body(full, tiles_of[ph] - full)

        def halves(nb):
            cut = (nb + 1) // 2
            return [range(0, cut), range(cut, nb)][:min(nb, 2)]

        def batch_size(ph, t):
            return min(B, tiles_of[ph] - t) if isinstance(t, int) else B

        def wait(eng, ph, stage, t, b):
            k = kind(stage)
            eng.wait_ge(S[k], t * turns[ph, k] + (base[ph, k] + turn[ph, stage] * batch_size(ph, t) + b + 1))

        def wait_before(eng, ph, stage, t, b):
            k = kind(stage)
            v = base[ph, k] + turn[ph, stage] * B + b + 1 - turns[ph, k] * B
            assert v >= 0
            eng.wait_ge(S[k], t * turns[ph, k] + v)

        def wait_phase(eng, ph, stage):
            k = kind(stage)
            eng.wait_ge(S[k], base[ph, k] + turns[ph, k] * tiles_of[ph])

        def settle(eng):
            eng.sem_inc(passed, 1)

        def wait_loaded(eng, ph, t, b, k=None):
            k = LOADS[ph] if k is None else k
            eng.wait_ge(loaded[b], t * (4 * LOADS[ph]) + (before(LOADS, ph, b) + 16 * k))

        def wait_gathered(eng, ph, t, b):
            eng.wait_ge(gathered[b], t * (4 * GATHERS[ph]) + (before(GATHERS, ph, b) + 16 * GATHERS[ph]))

        def wait_stored(eng, ph, t, b, k):
            v = before(STORES, ph, b) + 16 * k
            if not isinstance(t, int) or t * 4 * STORES.get(ph, 0) + v > 0:
                eng.wait_ge(stored[b], t * (4 * STORES.get(ph, 0)) + v)

        def scan_place(ph, t, b, k):
            first, per = scan_base[ph]
            if ph == "d0":
                return first + 4 * (k // 2) * batch_size(ph, t) + 4 * b + 2 * (k % 2)
            return first + 2 * (per * b + k)

        def wait_scans(eng, ph, t, b, k):
            eng.wait_ge(scanned, t * (2 * scan_base[ph][1]) + (scan_place(ph, t, b, k - 1) + 2))

        n_id_loads = 3 * H + 1

        @block.tensor
        def _(pe):
            mm = nc.tensor.matmul

            pe.wait_ge(weights_in, 16 * n_weight_dmas)
            pe.wait_ge(consts, 2)
            for i in range(NT):
                bank = [PA[0], PB[0], PA[1]][i // Q]
                last = nc.tensor.transpose(bank[:, (i % Q) * P:(i % Q + 1) * P], wraw[:, i, :], ident[:, :])
            last.then_inc(prep_pe, 1)
            pe.wait_ge(prep_dve, 1)
            for i in range(8):
                bank = [PB[1], PA[2]][i // Q]
                mm(bank[:, (i % Q) * P:(i % Q + 1) * P], wturned[:, i, :], centre[:, :], start=True, stop=True)
            mm(PB[2][:, 0:P], wat["w2"], centre[:, :], start=True, stop=True)
            mm(PB[2][:, P:P + NC], centre[:, :], bias[:, 0:NC], start=True, stop=True).then_inc(prep_pe, 1)
            pe.wait_ge(prep_dve, 2)

            def turn_in(ph, t, b, src, bank, order, stage):
                for q in range(Q):
                    o = bank[b][:, q * P:(q + 1) * P] if order == "any" else bank[b][:, q::Q]
                    last = nc.tensor.transpose(o, src[b][:, q * P:(q + 1) * P], ident[:, :])
                last.then_inc(S[kind(stage)], 1)

            def turn_out(ph, t, bs, st, order, level, after):
                for b in bs:
                    wait(pe, ph, after, t, b)
                    for q in range(Q):
                        i = st[b][:, q * P:(q + 1) * P] if order == "any" else st[b][:, q::Q]
                        last = nc.tensor.transpose(PB[b][:, q * P:(q + 1) * P], i, ident[:, :])
                    last.then_inc(S["turned_out"], 1)

            def variance(ph, t, bs, l):
                for b in bs:
                    wait(pe, ph, f"squared{l}", t, b)
                    mm(PB[b][:, :], mean_block[:, :], R[b][:, :], start=True, stop=True)\
                        .then_inc(S["variance"], 1)

            def product(ph, t, bs, bank, pairs, stage, waits):
                for b in bs:
                    for w in waits:
                        wait(pe, ph, w, t, b)
                    for k, (w, st) in enumerate(pairs):
                        last = mm(bank[b][:, :], w, st[b][:, :], start=(k == 0), stop=(k == len(pairs) - 1))
                    last.then_inc(S[kind(stage)], 1)

            def norm_of(ph, t, bs, l, pairs, waits):
                product(ph, t, bs, PA, pairs, f"centred{l}", waits)
                variance(ph, t, bs, l)

            def sage_layer(ph, t, bs, i, waits, mean):
                st = X if i == 0 else Y
                pairs = [(wc[f"wr{i}"], st)] + ([(wc[f"wl{i}"], AG)] if mean else [])
                norm_of(ph, t, bs, 1 + i, pairs, waits + (["mean"] if mean else []))

            def residual(ph, t, bs):
                product(ph, t, bs, PB, [(wat["wres"], X)], "residual_mm", ["logvar1"])

            def gates(ph, t, bs, r, st, waits, msg):
                m = lambda g: [(wat[f"ih_{g}{r}"], MSG)] if msg else []
                more = ["message_in"] if msg else []
                product(ph, t, bs, PA, [(wat[f"hh_r{r}"], st)] + m("r"), f"gate_r{r}", waits + more)
                product(ph, t, bs, PB, [(wat[f"hh_z{r}"], st)] + m("z"), f"gate_z{r}", [])

            def gates_n(ph, t, bs, r, st, msg):
                for b in bs:
                    wait(pe, ph, f"sig_r{r}", t, b)
                    last = mm(PA[b][:, :], wat[f"hh_n{r}"], st[b][:, :], start=True, stop=True)
                    if msg:
                        wait(pe, ph, f"sig_z{r}", t, b)
                        last = mm(PB[b][:, :], wat[f"ih_n{r}"], MSG[b][:, :], start=True, stop=True)
                    last.then_inc(S["gate_n"], 1)

            def chain_pe(ph, order, saving):
                def body(t, nb):
                    def out_of(level, bs, st, after):
                        if saving:
                            turn_out(ph, t, bs, st, order, level, after)
                    for bs in halves(nb):
                        for b in bs:
                            if ph == "main":
                                wait_loaded(pe, ph, t, b)
                            else:
                                wait_gathered(pe, ph, t, b)
                            turn_in(ph, t, b, rows, PA, order, "turned_in")
                    for bs in halves(nb):
                        norm_of(ph, t, bs, 0, [(centre[:, :], X)], ["x_in"])
                    for bs in halves(nb):
                        out_of(1, bs, X, "normed0")
                        sage_layer(ph, t, bs, 0, ["normed0"], False)
                    for bs in halves(nb):
                        residual(ph, t, bs)
                    for bs in halves(nb):
                        out_of(2, bs, Y, "added0")
                        sage_layer(ph, t, bs, 1, ["added0"], False)
                    for bs in halves(nb):
                        out_of(3, bs, Y, "added1")
                        sage_layer(ph, t, bs, 2, ["added1"], False)
                    for bs in halves(nb):
                        norm_of(ph, t, bs, 4, [(wc["wfc"], Y), (centre[:, :], X)], ["added2"])
                    for bs in halves(nb):
                        out_of(4, bs, X, "normed4")
                        gates(ph, t, bs, 0, X, ["normed4"] + ["rows_out4"] * saving, False)
                        gates_n(ph, t, bs, 0, X, False)
                    for bs in halves(nb):
                        out_of(5, bs, Y, "hidden0")
                        gates(ph, t, bs, 1, Y, ["hidden0"] + ["rows_out5"] * saving, False)
                        gates_n(ph, t, bs, 1, Y, False)
                    for bs in halves(nb):
                        norm_of(ph, t, bs, 5, [(centre[:, :], Y)], ["summed"])
                    if ph == "main":
                        for bs in halves(nb):
                            norm_of(ph, t, bs, 6, [(wc["wn"], X)], ["normed5"])
                    for bs in halves(nb):
                        out_of(6, bs, X, "normed5")
                        if ph == "main":
                            turn_out(ph, t, bs, X, order, 7, "normed6")
                each_batch(pe, ph, body)

            chain_pe("main", "any", False)
            chain_pe("src", "any", True)

            level = {"d0": 1, "d4": 5, "d5": 6, "d6": 7}

            def pb_free(ph, t, b):
                wait_before(pe, ph, f"rows_out{level[ph]}", t, b)

            def phase_over(ph, lev):
                wait_phase(pe, ph, f"rows_out{lev}")

            def turn_edge_inputs(ph, t, nb):
                for b in range(nb):
                    wait_gathered(pe, ph, t, b)
                    pb_free(ph, t, b)
                    turn_in(ph, t, b, rows2, PB, "edge", "turned_dst")
                    turn_in(ph, t, b, rows, PA, "edge", "turned_in")
                for b in range(nb):
                    wait(pe, ph, "src_in", t, b)
                    wait_loaded(pe, ph, t, b)
                    turn_in(ph, t, b, edges, PA, "edge", "turned_edge")

            def d0(t, nb):
                turn_edge_inputs("d0", t, nb)
                for bs in halves(nb):
                    product("d0", t, bs, PA, [(wturned[:, 8, :], XS), (wturned[:, 9, :], EF)], "hidden_mm", ["edge_in"])
                for bs in halves(nb):
                    product("d0", t, bs, PB, [(att_f[:, :], Z), (att_r[:, :], W)], "logits", ["leaky", "x_in"])
                for bs in halves(nb):
                    norm_of("d0", t, bs, 0, [(centre[:, :], X), (wc["w2"], AG)], ["mixed"])
                for bs in halves(nb):
                    turn_out("d0", t, bs, X, "edge", 1, "normed0")
            phase_over("src", 6)
            each_batch(pe, "d0", d0)

            def turn_src(ph, t, bs):
                for b in bs:
                    wait_gathered(pe, ph, t, b)
                    wait_loaded(pe, ph, t, b)
                    turn_in(ph, t, b, rows, PA, "edge", "turned_in")

            def sage_phase(ph, i):
                def body(t, nb):
                    for bs in halves(nb):
                        turn_src(ph, t, bs)
                    for bs in halves(nb):
                        sage_layer(ph, t, bs, i, [], True)
                    if i == 0:
                        for bs in halves(nb):
                            residual(ph, t, bs)
                    if i == 2:
                        for bs in halves(nb):
                            norm_of(ph, t, bs, 4, [(wc["wfc"], Y), (centre[:, :], X)], ["added2"])
                    for bs in halves(nb):
                        if i == 2:
                            turn_out(ph, t, bs, X, "edge", 4, "normed4")
                        else:
                            turn_out(ph, t, bs, Y, "edge", 2 + i, f"added{i}")
                each_batch(pe, ph, body)
            for i in range(3):
                sage_phase(f"d{1 + i}", i)

            def gru_phase(ph, r):
                st = X if r == 0 else Y
                def body(t, nb):
                    for bs in halves(nb):
                        turn_src(ph, t, bs)
                        for b in bs:
                            pb_free(ph, t, b)
                            turn_in(ph, t, b, edges, PB, "edge", "turned_edge")
                    for bs in halves(nb):
                        for b in bs:
                            wait_scans(pe, ph, t, b, 2)
                        product(ph, t, bs, PA, [(wat[f"msg_s{r}"], AG), (wat[f"msg_d{r}"], W),
                                                (wat[f"msg_e{r}"], EF)], "message", ["times_degree"])
                    for bs in halves(nb):
                        gates(ph, t, bs, r, st, [], True)
                        gates_n(ph, t, bs, r, st, True)
                    if r == 1:
                        for bs in halves(nb):
                            norm_of(ph, t, bs, 5, [(centre[:, :], Y)], ["summed"])
                    for bs in halves(nb):
                        if r == 1:
                            turn_out(ph, t, bs, X, "edge", 6, "normed5")
                        else:
                            turn_out(ph, t, bs, Y, "edge", 5, "hidden0")
                each_batch(pe, ph, body)
            phase_over("d3", 4)
            pe.wait_ge(ones_set, 1)
            gru_phase("d4", 0)
            phase_over("d4", 5)
            gru_phase("d5", 1)
            phase_over("d5", 6)

            def d6(t, nb):
                turn_edge_inputs("d6", t, nb)
                for b in range(nb):
                    wait(pe, "d6", "x_in", t, b)
                    wait(pe, "d6", "edge_in", t, b)
                    for h, bank in enumerate((PA, PB)):
                        r = slice(h * D, h * D + D)
                        mm(bank[b][:, :], w3s[r, :], XS[b][r, :], start=True, stop=False)
                        mm(bank[b][:, :], w3d[r, :], Y[b][r, :], start=False, stop=False)
                        last = mm(bank[b][:, :], w3e[r, :], EF[b][r, :], start=False, stop=True)
                    last.then_inc(S["hidden_mm"], 1)
                for b in range(nb):
                    wait(pe, "d6", "hidden_relu0", t, b)
                    mm(PA[b][0:D, :], w3o[:, :], Z[b][:, :], start=True, stop=True)
                    wait(pe, "d6", "hidden_relu1", t, b)
                    mm(PA[b][D:P, :], w3o[:, :], W[b][:, :], start=True, stop=True).then_inc(S["message"], 1)
                for bs in halves(nb):
                    norm_of("d6", t, bs, 6, [(wc["wn"], X), (centre[:, :], AG)], ["mean"])
                for bs in halves(nb):
                    turn_out("d6", t, bs, X, "edge", 7, "normed6")
            each_batch(pe, "d6", d6)

        @block.scalar
        def _(act):
            fn = nc.scalar.activation

            def per_tile(ph, t, bs, stage, waits, op):
                for b in bs:
                    for w in waits:
                        wait(act, ph, w, t, b)
                    op(b).then_inc(S[kind(stage)], 1)

            def norm_of(ph, t, bs, l, bias_id=None):
                c = norm_bias[l if bias_id is None else bias_id]
                per_tile(ph, t, bs, f"squared{l}", [f"centred{l}"],
                         lambda b: fn(R[b][:, :], PA[b][:, :], ACT.Square, bias=bcent[:, c:c + 1]))
                per_tile(ph, t, bs, f"logvar{l}", [f"variance{l}"],
                         lambda b: fn(R[b][:, :], PB[b][:, :], ACT.Ln, bias=eps[:, :]))
                per_tile(ph, t, bs, f"rstd{l}", [f"logvar{l}"],
                         lambda b: fn(R[b][:, :], R[b][:, :], ACT.Exp, scale=-0.5))

            def sage_layer(ph, t, bs, i):
                norm_of(ph, t, bs, 1 + i)

            def gates(ph, t, bs, r, msg):
                per_tile(ph, t, bs, f"sig_r{r}", [f"gate_r{r}"],
                         lambda b: fn(R[b][:, :], PA[b][:, :], ACT.Sigmoid, bias=gate_b[:, 2 * r:2 * r + 1]))
                per_tile(ph, t, bs, f"sig_z{r}", [f"gate_z{r}"],
                         lambda b: fn(Z[b][:, :], PB[b][:, :], ACT.Sigmoid, bias=gate_b[:, 2 * r + 1:2 * r + 2]))

            def gates_n(ph, t, bs, r, msg):
                per_tile(ph, t, bs, f"tanh{r}", ["reset_sum" if msg else f"reset{r}"],
                         lambda b: fn(R[b][:, :], R[b][:, :], ACT.Tanh, bias=bcol[f"ih_n{r}"]))

            def rows_out(ph, t, bs, level, k):
                for b in bs:
                    wait(act, ph, f"turned_out{level}", t, b)
                    if ph == "d6":
                        if not (isinstance(t, int) and t == 0):
                            act.wait_ge(scattered[b], t * (4 * 8))
                    wait_stored(act, ph, t, b, k)
                    fn(rows_o[b][:, :], PB[b][:, :], ACT.Copy).then_inc(S["rows_out"], 1)

            act.wait_ge(prep_dve, 3)

            def log_exp_tables():
                nc.scalar.preload_act_table_set("natural_log_exp_and_others")

            def chain_act(ph, saving):
                def body(t, nb):
                    def out_of(level, bs):
                        if saving:
                            rows_out(ph, t, bs, level, level - 1)
                    for bs in halves(nb):
                        per_tile(ph, t, bs, "x_in", ["turned_in"], lambda b: fn(X[b][:, :], PA[b][:, :], ACT.Copy))
                    log_exp_tables()
                    for bs in halves(nb):
                        norm_of(ph, t, bs, 0)
                    for i in range(3):
                        for bs in halves(nb):
                            out_of(1 + i, bs)
                            sage_layer(ph, t, bs, i)
                    for bs in halves(nb):
                        norm_of(ph, t, bs, 4)
                    for r in range(2):
                        for bs in halves(nb):
                            out_of(4 + r, bs)
                            gates(ph, t, bs, r, False)
                            gates_n(ph, t, bs, r, False)
                    log_exp_tables()
                    for bs in halves(nb):
                        norm_of(ph, t, bs, 5)
                    if ph == "main":
                        for bs in halves(nb):
                            norm_of(ph, t, bs, 6)
                    for bs in halves(nb):
                        out_of(6, bs)
                        if ph == "main":
                            rows_out(ph, t, bs, 7, 0)
                each_batch(act, ph, body)

            chain_act("main", False)
            chain_act("src", True)

            def edge_inputs(ph, t, nb, dst):
                per_tile(ph, t, range(nb), "src_in", ["turned_in"], lambda b: fn(XS[b][:, :], PA[b][:, :], ACT.Copy))
                for b in range(nb):
                    if ph == "d0" and not (isinstance(t, int) and t == 0):
                        act.wait_ge(kept[b], t * (4 * KEEPS[ph]) + (1 + before(KEEPS, ph, b)))
                    wait(act, ph, "turned_dst", t, b)
                    fn(dst[b][:, :], PB[b][:, :], ACT.Copy).then_inc(S["x_in"], 1)
                per_tile(ph, t, range(nb), "edge_in", ["turned_edge"], lambda b: fn(EF[b][:, :], PA[b][:, :], ACT.Copy))

            def d0(t, nb):
                log_exp_tables()
                edge_inputs("d0", t, nb, X)
                for bs in halves(nb):
                    per_tile("d0", t, bs, "weight_exp", ["new_weight"], lambda b: fn(R[b][:, :], R[b][:, :], ACT.Exp))
                    per_tile("d0", t, bs, "decay_exp", ["max_shift"], lambda b: fn(DC[b][:, :], DC[b][:, :], ACT.Exp))
                for bs in halves(nb):
                    for b in bs:
                        wait_scans(act, "d0", t, b, 2)
                        if not (isinstance(t, int) and t == 0):
                            act.wait_ge(kept[b], t * (4 * KEEPS["d0"]) + 1)
                        fn(MSG[b][:, :], DEG[b][:, :], ACT.Ln).then_inc(S["log_degree"], 1)
                    per_tile("d0", t, bs, "inv_degree", ["log_degree"],
                             lambda b: fn(MSG[b][:, :], MSG[b][:, :], ACT.Exp, scale=-1.0))
                for bs in halves(nb):
                    for b in bs:
                        wait_scans(act, "d0", t, b, 3)
                        wait(act, "d0", "logits", t, b)
                        fn(W[b][:, :], DN[b][:, :], ACT.Ln).then_inc(S["log_den"], 1)
                    per_tile("d0", t, bs, "inv_den", ["log_den"],
                             lambda b: fn(W[b][:, :], W[b][:, :], ACT.Exp, scale=-1.0))
                for bs in halves(nb):
                    norm_of("d0", t, bs, 0)
                for bs in halves(nb):
                    rows_out("d0", t, bs, 1, 0)
            each_batch(act, "d0", d0)

            def sage_phase(ph, i):
                def body(t, nb):
                    log_exp_tables()
                    for bs in halves(nb):
                        sage_layer(ph, t, bs, i)
                    if i == 2:
                        for bs in halves(nb):
                            norm_of(ph, t, bs, 4)
                    for bs in halves(nb):
                        rows_out(ph, t, bs, 4 if i == 2 else 2 + i, 0)
                each_batch(act, ph, body)
            for i in range(3):
                sage_phase(f"d{1 + i}", i)

            def gru_phase(ph, r):
                def body(t, nb):
                    for bs in halves(nb):
                        per_tile(ph, t, bs, "message_in", ["message"],
                                 lambda b: fn(MSG[b][:, :], PA[b][:, :], ACT.Copy))
                    for bs in halves(nb):
                        gates(ph, t, bs, r, True)
                        gates_n(ph, t, bs, r, True)
                    if r == 1:
                        log_exp_tables()
                        for bs in halves(nb):
                            norm_of(ph, t, bs, 5)
                    for bs in halves(nb):
                        rows_out(ph, t, bs, 5 + r, 0)
                each_batch(act, ph, body)
            gru_phase("d4", 0)
            gru_phase("d5", 1)

            def d6(t, nb):
                log_exp_tables()
                edge_inputs("d6", t, nb, Y)
                for h, (bank, hid) in enumerate(((PA, Z), (PB, W))):
                    per_tile("d6", t, range(nb), f"hidden_relu{h}", ["hidden_mm"],
                             lambda b: fn(hid[b][:, :], bank[b][:, :], ACT.Relu, bias=b1col[:, :]))
                for bs in halves(nb):
                    norm_of("d6", t, bs, 6, "6d")
                for bs in halves(nb):
                    rows_out("d6", t, bs, 7, 0)
            each_batch(act, "d6", d6, peel=True)

        @block.vector
        def _(dve):
            v = nc.vector

            dve.wait_ge(zeroed, 1)
            v.memset(ones_block[:, :], 0.0).then_inc(consts, 1)
            v.memset(ones[:, :], 1.0)
            v.memset(eps[:, :], EPS)
            dve.wait_ge(consts, 1)
            for h in range(H):
                last = v.memset(ones_block[h * D:h * D + D, h * D:h * D + D], 1.0)
            last.then_inc(id_steps, 1)
            dve.wait_ge(id_steps, 1)
            v.tensor_scalar(mean_block[:, :], ones_block[:, :], 1.0 / D, None, ALU.mult).then_inc(id_steps, 1)
            dve.wait_ge(id_steps, 2)
            dve.wait_ge(zeroed, 2)
            v.tensor_tensor(centre[:, :], ident[:, :], mean_block[:, :], ALU.subtract).then_inc(consts, 1)
            dve.wait_ge(weights_in, 16 * n_weight_dmas)
            v.tensor_scalar(att_f[:, :], ones_block[:, :], bcol["att_f"], None, ALU.mult)
            v.tensor_scalar(att_r[:, :], ones_block[:, :], bcol["att_r"], None, ALU.mult)
            i = cols.index("b3")
            v.tensor_tensor(bias[:, i:i + 1], bcol["bn"], bcol["b2"], ALU.add)
            for r in range(2):
                for k, g in enumerate("rz"):
                    v.tensor_tensor(gate_b[:, 2 * r + k:2 * r + k + 1], bcol[f"ih_{g}{r}"], bcol[f"hh_{g}{r}"], ALU.add)
            dve.wait_ge(prep_pe, 1)
            v.tensor_copy(wturned[:, 0:Q, :], PA[0][:, :].rearrange("p (a b) -> p a b", a=Q))
            v.tensor_copy(wturned[:, 8:NT, :], PA[1][:, 0:2 * P].rearrange("p (a b) -> p a b", a=2))
            v.tensor_copy(wturned[:, Q:7, :], PB[0][:, 0:3 * P].rearrange("p (a b) -> p a b", a=3))
            v.tensor_tensor(wturned[:, 7, :], PB[0][:, 3 * P:4 * P], ident[:, :], ALU.add).then_inc(prep_dve, 1)
            dve.wait_ge(prep_pe, 2)
            v.tensor_copy(wcentred[:, 0:Q, :], PB[1][:, :].rearrange("p (a b) -> p a b", a=Q))
            v.tensor_copy(wcentred[:, Q:8, :], PA[2][:, :].rearrange("p (a b) -> p a b", a=Q))
            v.tensor_copy(wcentred[:, 8, :], PB[2][:, 0:P])
            v.tensor_copy(bcent[:, :], PB[2][:, P:P + NC]).then_inc(prep_dve, 1)
            for b in range(B):
                v.memset(edges[b][:, :], 0.0)
                v.memset(MX[b][:, :], 0.0)
                v.memset(DN[b][:, :], 0.0)
                v.memset(DEG[b][:, :], 0.0)
                v.memset(AG[b][:, :], 0.0)
                last = v.memset(EF[b][:, :], 0.0)
            last.then_inc(prep_dve, 1)

            g = lambda n: ids[n][:, :]
            dve.wait_ge(ids_in, 16 * n_id_loads)
            dve.wait_ge(iota_done, 1)
            v.tensor_tensor(idf[:, :], g("dst_of"), g("dst_next"), ALU.is_equal)
            v.tensor_scalar(g("dst_row"), g("dst_of"), 0.0, None, ALU.max).then_inc(ids_ready, 1)
            dve.wait_ge(ids_ready, 1)
            v.scalar_tensor_tensor(g("put_row"), idf[:, :], float(OUTSIDE), g("dst_of"), ALU.mult, ALU.add)\
                .then_inc(ids_ready, 1)

            def norm_of(ph, t, bs, l, dst, bias_id=None):
                c = norm_bias[l if bias_id is None else bias_id]
                for b in bs:
                    wait(dve, ph, f"rstd{l}", t, b)
                    v.scalar_tensor_tensor(dst[b][:, :], PA[b][:, :], bcent[:, c:c + 1], R[b][:, :], ALU.add, ALU.mult)\
                        .then_inc(S["normed"], 1)

            def sage_layer(ph, t, bs, i):
                norm_of(ph, t, bs, 1 + i, Z)
                for b in bs:
                    wait(dve, ph, f"normed{1 + i}", t, b)
                    v.tensor_scalar(Z[b][:, :], Z[b][:, :], bcol[f"g{i}"], bcol[f"be{i}"], ALU.mult, ALU.add)\
                        .then_inc(S["scaled_norm"], 1)
                if i == 0:
                    for b in bs:
                        wait(dve, ph, f"scaled_norm{i}", t, b)
                        v.tensor_scalar(Z[b][:, :], Z[b][:, :], 0.0, bcol["bres"], ALU.max, ALU.add)\
                            .then_inc(S["relu"], 1)
                for b in bs:
                    if i == 0:
                        wait(dve, ph, "relu", t, b)
                        wait(dve, ph, "residual_mm", t, b)
                        op = v.tensor_tensor(Y[b][:, :], PB[b][:, :], Z[b][:, :], ALU.add)
                    else:
                        wait(dve, ph, f"scaled_norm{i}", t, b)
                        op = v.scalar_tensor_tensor(Y[b][:, :], Z[b][:, :], 0.0, Y[b][:, :], ALU.max, ALU.add)
                    op.then_inc(S["added"], 1)

            def gates(ph, t, bs, r, msg):
                st = X if r == 0 else Y
                tmp = Y if r == 0 else W
                for b in bs:
                    wait(dve, ph, f"gate_n{r}", t, b)
                    v.scalar_tensor_tensor(R[b][:, :], PA[b][:, :], bcol[f"hh_n{r}"], R[b][:, :], ALU.add, ALU.mult)\
                        .then_inc(S["reset"], 1)
                if msg:
                    for b in bs:
                        wait(dve, ph, f"reset{r}", t, b)
                        v.tensor_tensor(R[b][:, :], PB[b][:, :], R[b][:, :], ALU.add).then_inc(S["reset_sum"], 1)
                for b in bs:
                    wait(dve, ph, f"tanh{r}", t, b)
                    v.tensor_tensor(tmp[b][:, :], st[b][:, :], R[b][:, :], ALU.subtract).then_inc(S["diff"], 1)
                for b in bs:
                    wait(dve, ph, f"diff{r}", t, b)
                    v.tensor_tensor(tmp[b][:, :], tmp[b][:, :], Z[b][:, :], ALU.mult).then_inc(S["scaled"], 1)
                for b in bs:
                    wait(dve, ph, f"scaled{r}", t, b)
                    v.tensor_tensor(Y[b][:, :], tmp[b][:, :], R[b][:, :], ALU.add).then_inc(S["hidden"], 1)

            def sum_x(ph, t, bs):
                for b in bs:
                    wait(dve, ph, "hidden1", t, b)
                    v.tensor_tensor(Y[b][:, :], Y[b][:, :], X[b][:, :], ALU.add).then_inc(S["summed"], 1)

            def chain_dve(ph):
                def body(t, nb):
                    for bs in halves(nb):
                        norm_of(ph, t, bs, 0, X)
                    for i in range(3):
                        for bs in halves(nb):
                            sage_layer(ph, t, bs, i)
                    for bs in halves(nb):
                        norm_of(ph, t, bs, 4, X)
                    for r in range(2):
                        for bs in halves(nb):
                            gates(ph, t, bs, r, False)
                    for bs in halves(nb):
                        sum_x(ph, t, bs)
                    for bs in halves(nb):
                        norm_of(ph, t, bs, 5, X)
                    if ph == "main":
                        for bs in halves(nb):
                            norm_of(ph, t, bs, 6, X)
                each_batch(dve, ph, body)

            chain_dve("main")
            dve.wait_ge(map_copied, 1 + 2 * TE)
            v.tensor_scalar(idf[:, :], g("src_map"), 0.0, None, ALU.is_equal)
            v.tensor_scalar(idf2[:, :], g("slot1"), float(SLOTS), None, ALU.add).then_inc(ids_ready, 1)
            dve.wait_ge(ids_ready, 3)
            v.tensor_tensor(idf2[:, :], idf2[:, :], idf[:, :], ALU.mult).then_inc(ids_ready, 1)
            dve.wait_ge(ids_ready, 4)
            v.scalar_tensor_tensor(g("src_slot"), g("src_map"), -1.0, idf2[:, :], ALU.add, ALU.add)
            v.tensor_scalar(g("dst_slot"), g("dst_map"), -1.0, 0.0, ALU.add, ALU.max).then_inc(ids_ready, 1)
            chain_dve("src")

            def scan(ph, t, b, k, dst, decay, data, op0=ALU.mult, op1=ALU.add, shift=0):
                per = scan_base[ph][1]
                last = COLS - 1 + shift
                for h in range(H):
                    r, other = slice(h * D, h * D + D), slice((1 - h) * D, (1 - h) * D + D)
                    from_ = dst[(b - 1) % B] if h == 0 else dst[b]
                    n = scan_place(ph, t, b, k) + h
                    if not (isinstance(t, int) and t * 2 * per + n == 0):
                        dve.wait_ge(scanned, t * (2 * per) + n)
                    v.tensor_copy(carry[r, :], from_[other, last:last + 1]).then_inc(carried, 1)
                    dve.wait_ge(carried, t * (2 * per) + (n + 1))
                    v.tensor_tensor_scan(dst[b][r, shift:shift + COLS], decay[b][r, :], data(b)[r, :], carry[r, :],
                                         op0, op1).then_inc(scanned, 1)

            def d0(t, nb):
                ph = "d0"
                for b in range(nb):
                    wait_loaded(dve, ph, t, b)
                    if not (isinstance(t, int) and t == 0):
                        dve.wait_ge(kept[b], t * (4 * KEEPS[ph]) + 1)
                    v.tensor_tensor(SAME[b][:, :], IDS[b][:, 0:COLS], IDS[b][:, 1:COLS + 1], ALU.is_equal)\
                        .then_inc(S["same"], 1)
                for b in range(nb):
                    wait(dve, ph, "hidden_mm", t, b)
                    wait(dve, ph, "x_in", t, b)
                    v.tensor_scalar(Z[b][:, :], PA[b][:, :], 0.01, None, ALU.mult).then_inc(S["small_slope"], 1)
                    v.scalar_tensor_tensor(W[b][:, :], X[b][:, :], 0.01, X[b][:, :], ALU.mult, ALU.max)
                    wait(dve, ph, "small_slope", t, b)
                    v.tensor_tensor(Z[b][:, :], PA[b][:, :], Z[b][:, :], ALU.max).then_inc(S["leaky"], 1)
                    wait(dve, ph, "same", t, b)
                    v.tensor_scalar(R[b][:, :], SAME[b][:, :], -1.0, BIG, ALU.add, ALU.mult).then_inc(S["penalty"], 1)
                for b in range(nb):
                    wait(dve, ph, "logits", t, b)
                    wait(dve, ph, "penalty", t, b)
                    scan(ph, t, b, 0, MX, R, lambda b: PB[b], ALU.add, ALU.max, shift=1)
                    wait_scans(dve, ph, t, b, 1)
                    for h in range(H):
                        r, other = slice(h * D, h * D + D), slice((1 - h) * D, (1 - h) * D + D)
                        from_ = MX[(b - 1) % B] if h == 0 else MX[b]
                        last = v.tensor_copy(MX[b][r, 0:1], from_[other, COLS:COLS + 1])
                    last.then_inc(S["max_before"], 1)
                    v.tensor_tensor(R[b][:, :], PB[b][:, :], MX[b][:, 1:COLS + 1], ALU.subtract)\
                        .then_inc(S["new_weight"], 1)
                    wait(dve, ph, "max_before", t, b)
                    v.tensor_tensor(DC[b][:, :], MX[b][:, 0:COLS], MX[b][:, 1:COLS + 1], ALU.subtract)\
                        .then_inc(S["max_step"], 1)
                    wait(dve, ph, "max_step", t, b)
                    v.tensor_scalar(DC[b][:, :], DC[b][:, :], 0.0, None, ALU.min).then_inc(S["max_shift"], 1)
                    scan(ph, t, b, 1, DEG, SAME, lambda b: ones)
                    wait_scans(dve, ph, t, b, 2)
                for b in range(nb):
                    wait(dve, ph, "decay_exp", t, b)
                    v.tensor_tensor(DC[b][:, :], DC[b][:, :], SAME[b][:, :], ALU.mult)
                    wait(dve, ph, "weight_exp", t, b)
                    v.tensor_tensor(Z[b][:, :], R[b][:, :], XS[b][:, :], ALU.mult).then_inc(S["weighted"], 1)
                    wait(dve, ph, "weighted", t, b)
                    scan(ph, t, b, 2, DN, DC, lambda b: R[b])
                    scan(ph, t, b, 3, AG_n, DC, lambda b: Z[b])
                for b in range(nb):
                    wait_scans(dve, ph, t, b, 4)
                    wait(dve, ph, "inv_den", t, b)
                    v.tensor_tensor(AG[b][:, :], AG_n[b][:, :], W[b][:, :], ALU.mult).then_inc(S["mixed"], 1)
                for bs in halves(nb):
                    norm_of(ph, t, bs, 0, X)
            AG_n = Y
            each_batch(dve, "d0", d0)

            def gather_scan(ph, t, bs, invert):
                for b in bs:
                    wait_loaded(dve, ph, t, b)
                    wait(dve, ph, "turned_in", t, b)
                    scan(ph, t, b, 0, AGS, SAME, lambda b: PA[b])
                    if invert:
                        wait_scans(dve, ph, t, b, 1)
                        v.tensor_tensor(AG[b][:, :], AGS[b][:, :], DEG[b][:, :], ALU.mult).then_inc(S["mean"], 1)
            AGS = DN

            def sage_phase(ph, i):
                def body(t, nb):
                    for bs in halves(nb):
                        gather_scan(ph, t, bs, True)
                    for bs in halves(nb):
                        sage_layer(ph, t, bs, i)
                    if i == 2:
                        for bs in halves(nb):
                            norm_of(ph, t, bs, 4, X)
                each_batch(dve, ph, body)
            for i in range(3):
                sage_phase(f"d{1 + i}", i)

            def gru_phase(ph, r):
                st = X if r == 0 else Y
                def body(t, nb):
                    for b in range(nb):
                        wait_loaded(dve, ph, t, b)
                        v.tensor_tensor(W[b][:, :], st[b][:, :], DEG[b][:, :], ALU.mult)\
                            .then_inc(S["times_degree"], 1)
                        wait(dve, ph, "turned_in", t, b)
                        scan(ph, t, b, 0, AG, SAME, lambda b: PA[b])
                        wait(dve, ph, "turned_edge", t, b)
                        scan(ph, t, b, 1, EF, SAME, lambda b: PB[b])
                    for bs in halves(nb):
                        gates(ph, t, bs, r, True)
                    if r == 1:
                        for bs in halves(nb):
                            sum_x(ph, t, bs)
                        for bs in halves(nb):
                            norm_of(ph, t, bs, 5, X)
                each_batch(dve, ph, body)
            for b in range(B):
                last = v.memset(edges[b][:, :].rearrange("p (s f) -> p s f", f=D)[:, :, 4:5], 1.0)
            last.then_inc(ones_set, 1)
            gru_phase("d4", 0)
            gru_phase("d5", 1)

            def d6(t, nb):
                for b in range(nb):
                    wait_loaded(dve, "d6", t, b)
                    wait(dve, "d6", "message", t, b)
                    scan("d6", t, b, 0, AGS, SAME, lambda b: PA[b])
                    wait_scans(dve, "d6", t, b, 1)
                    v.tensor_tensor(AG[b][:, :], AGS[b][:, :], DEG[b][:, :], ALU.mult).then_inc(S["mean"], 1)
                for bs in halves(nb):
                    norm_of("d6", t, bs, 6, X, "6d")
            each_batch(dve, "d6", d6)

        @block.sync
        def _(sp):
            dma = nc.sync.dma_start
            FW = TE * 8 + 1
            sp.wait_ge(fills, 3)
            dma(dst_pad.rearrange("(p c) -> p c", p=P), fill[:, 0, :]).then_inc(pad_filled, 16)
            dma(src_pad.rearrange("(p c) -> p c", p=P), fill[:, 1, 0:FW - 1]).then_inc(pad_filled, 16)
            dma(node_slot.rearrange("(p c) o -> p (c o)", p=80), zero_map[:, :]).then_inc(map_zero, 16)
            sp.wait_ge(zeroed, 1)
            for to, from_ in weight_loads:
                dma(to, from_).then_inc(weights_in, 16)

            def node_rows(n):
                first = min(n * TILE, N - TILE) if isinstance(n, int) else n * TILE
                return bass.ds(first, TILE)

            def load_nodes(t, b):
                dma(rows[b][:, :], a["x"][node_rows(t + b), :].rearrange("(p j) f -> p (j f)", p=P))\
                    .then_inc(loaded[b], 16)
            for b in range(B):
                load_nodes(0, b)

            sp.wait_ge(pad_filled, 32)
            dma(dst_pad[1:1 + E].rearrange("(a c) -> a c", a=8), a["dst"].rearrange("(a c) -> a c", a=8))\
                .then_inc(pad_put, 16)
            dma(src_pad[0:E].rearrange("(a c) -> a c", a=8), a["src"].rearrange("(a c) -> a c", a=8))\
                .then_inc(pad_put, 16)
            sp.wait_ge(pad_put, 32)
            for name, src, off in (("dst_of", dst_pad, 1), ("dst_next", dst_pad, 2), ("src_of", src_pad, 0)):
                v = src[off:off + SLOTS].rearrange("(g h p q) -> h p g q", h=H, p=P, q=Q)
                for h in range(H):
                    dma(ids[name][:, :].rearrange("p (g h q) -> p g h q", h=H, q=Q)[:, :, h, :], v[h]).then_inc(ids_in, 16)
            dma(ids["src_rows"][:, :].rearrange("p (g j) -> p g j", j=8),
                src_pad[0:SLOTS].rearrange("(g p j) -> p g j", p=P, j=8)).then_inc(ids_in, 16)

            def store_nodes(t, b):
                wait(sp, "main", "rows_out7", t, b)
                if isinstance(t, int) and t + b == TM - 1:
                    for c in range(B):
                        sp.wait_ge(stored[c], 16 * (slot_uses("main", c) - (c == b)))
                dma(out[node_rows(t + b), :].rearrange("(p j) f -> p (j f)", p=P), rows_o[b][:, :])\
                    .then_inc(stored[b], 16)

            full = TM // B * B
            with sp.Fori(0, full - 2 * B + 1, B) as t:
                for b in range(B):
                    wait(sp, "main", "turned_in", t, b)
                    load_nodes(t + B, b)
                for b in range(B):
                    store_nodes(t, b)
            for b in range(TM - full):
                wait(sp, "main", "turned_in", full - B, b)
                load_nodes(full, b)
            for b in range(B):
                store_nodes(full - B, b)
            for b in range(TM - full):
                store_nodes(full, b)

            def tile_rows(n):
                return bass.ds(n * P, P)

            def store_level(ph, t, b, level, order):
                wait(sp, ph, f"rows_out{level}", t, b)
                settle(sp)
                if order == "any":
                    to = table[level][bass.ds((t + b) * TILE + SLOTS, TILE), :]
                    dma(to.rearrange("(p j) f -> p (j f)", p=P), rows_o[b][:, :]).then_inc(stored[b], 16)
                else:
                    for h in range(H):
                        to = table[level][bass.ds((t + b) * TILE + h * COLS, COLS), :]
                        dma(to.rearrange("(p q) f -> p q f", q=Q),
                            rows_o[b][:, :].rearrange("p (q h f) -> p q h f", h=H, q=Q)[:, :, h, :]).then_inc(stored[b], 16)

            def src_stores(t, nb):
                for level in range(1, 7):
                    for b in range(nb):
                        store_level("src", t, b, level, "any")
            each_batch(sp, "src", src_stores)

            def load_edges(t, b, attr):
                w = attr.shape[1]
                to = edges[b][:, :].rearrange("p (q h f) -> p q h f", h=H, q=Q)
                short = isinstance(t, int) and t + b == TE - 1
                for h in range(H):
                    if short:
                        from_ = attr[(TE - 1) * TILE:E, :].rearrange("(p q) f -> p q f", q=Q)
                        dma(to[0:LAST_P, :, h, 0:w], from_).then_inc(loaded[b], 16)
                    else:
                        from_ = attr[bass.ds((t + b) * TILE + h * COLS, COLS), :].rearrange("(p q) f -> p q f", q=Q)
                        dma(to[:, :, h, 0:w], from_).then_inc(loaded[b], 16)

            def d0(t, nb):
                for b in range(nb):
                    wait_before(sp, "d0", "turned_out1", t, b)
                    settle(sp)
                    for h in range(H):
                        ids_of = dst_pad[bass.ds((t + b) * TILE + h * COLS, COLS + 1)]
                        dma(IDS[b][h * D:h * D + D, :],
                            ids_of.rearrange("(o c) -> o c", o=1).to_broadcast([D, COLS + 1])).then_inc(loaded[b], 16)
                    load_edges(t, b, a["edge_attr_16"])
                for b in range(nb):
                    for what, buf, stage in ((same_d, SAME, "same"), (degree_d, DEG, "inv_degree"),
                                             (inv_degree_d, MSG, "inv_degree"), (state[1], X, "normed0")):
                        wait(sp, "d0", stage, t, b)
                        settle(sp)
                        dma(what[tile_rows(t + b), :], buf[b][:, :]).then_inc(kept[b], 16)
                    store_level("d0", t, b, 1, "edge")
            wait_phase(sp, "src", "turned_out6")
            sp.wait_ge(prep_dve, 3)
            each_batch(sp, "d0", d0)

            def phase(ph, loads, attr, level, keep):
                after = {2: "added0", 3: "added1", 4: "normed4", 5: "hidden0", 6: "normed5"}.get(level)

                def body(t, nb):
                    for b in range(nb):
                        wait_before(sp, ph, f"turned_out{level}", t, b)
                        if keep is not None:
                            settle(sp)
                            sp.wait_ge(kept[b], t * (4 * KEEPS[ph]) + (1 + before(KEEPS, ph, b)))
                        settle(sp)
                        for from_, buf in loads:
                            dma(buf[b][:, :], from_[tile_rows(t + b), :]).then_inc(loaded[b], 16)
                        if attr is not None:
                            load_edges(t, b, attr)
                    if keep is not None:
                        for b in range(nb):
                            wait(sp, ph, after, t, b)
                            settle(sp)
                            dma(state[level][tile_rows(t + b), :], keep[b][:, :]).then_inc(kept[b], 16)
                            store_level(ph, t, b, level, "edge")
                each_batch(sp, ph, body)

            def phase_over(ph, level):
                wait_phase(sp, ph, f"turned_out{level}")
                for b in range(B):
                    sp.wait_ge(kept[b], 1 + before(KEEPS, ph, b) + 16 * KEEPS[ph] * slot_uses(ph, b))

            phase_over("d0", 1)
            phase("d1", [(state[1], X), (same_d, SAME), (inv_degree_d, DEG)], None, 2, Y)
            phase_over("d1", 2)
            phase("d2", [(state[2], Y), (same_d, SAME), (inv_degree_d, DEG)], None, 3, Y)
            phase_over("d2", 3)
            phase("d3", [(state[1], X), (state[3], Y), (same_d, SAME), (inv_degree_d, DEG)], None, 4, X)
            phase_over("d3", 4)
            phase("d4", [(state[4], X), (same_d, SAME), (degree_d, DEG)], a["edge_attr_4"], 5, Y)
            phase_over("d4", 5)
            phase("d5", [(state[4], X), (state[5], Y), (same_d, SAME), (degree_d, DEG)], a["edge_attr_4"], 6, X)
            phase_over("d5", 6)
            phase("d6", [(state[6], X), (same_d, SAME), (inv_degree_d, DEG)], a["edge_attr_32"], 7, None)
            for b in range(B):
                sp.wait_ge(stored[b], before(STORES, "d6", b))

        @block.gpsimd
        def _(gp):
            g = nc.gpsimd
            for s in kept + [map_copied]:
                gp.sem_inc(s, 1)
            g.memset(fill[:, 0, :], -1).then_inc(fills, 1)
            g.memset(fill[:, 1, :], 0).then_inc(fills, 1)
            g.memset(zero_map[:, :], 0).then_inc(fills, 1)
            g.memset(wraw[:, :, :], 0.0)
            g.memset(bias[:, :], 0.0)
            g.memset(w3e[:, :], 0.0).then_inc(zeroed, 1)
            g.memset(ident[:, :], 0.0).then_inc(ident_zero, 1)
            gp.wait_ge(ident_zero, 1)
            g.affine_select(out=ident[:, :], in_=ident[:, :], compare_op=ALU.not_equal, fill=1.0, base=0,
                            pattern=[[-1, P]], channel_multiplier=1).then_inc(zeroed, 1)
            g.iota(ids["slot1"][:, :], [[TILE, TE], [COLS, H], [1, Q]], base=1, channel_multiplier=Q)\
                .then_inc(iota_done, 1)

            def stage_ids(t, b, first, per, pairs):
                for k, (to, name) in enumerate(pairs):
                    g.tensor_copy(to, ids[name][:, bass.ds((t + b) * 8, 8)]).then_inc(staged, 1)
                gp.wait_ge(staged, t * per + (first + per * (b + 1)))
                settle(gp)

            def at(idx, k):
                return bass.IndirectOffsetOnAxis(ap=idx[:, k:k + 1], axis=0)

            full = TE // B * B

            gp.wait_ge(ids_ready, 2)
            gp.wait_ge(map_zero, 16)

            def put(t, nb):
                for b in range(nb):
                    if not (isinstance(t, int) and t == 0):
                        gp.wait_ge(map_put[b], t * (4 * 8))
                    stage_ids(t, b, 0, 2, [(gi[b][:, 0:8], "put_row"), (gv[b][:, 0:8], "slot1")])
                    for k in range(8):
                        g.indirect_dma_start(node_slot, at(gi[b], k), gv[b][:, k:k + 1], None,
                                             bounds_check=N - 1, oob_is_err=False).then_inc(map_put[b], 16)
            each_batch(gp, "src", put, peel=True)
            for b in range(B):
                gp.wait_ge(map_put[b], 16 * 8 * -(-(TE - b) // B))

            def get(t, nb):
                for b in range(nb):
                    if not (isinstance(t, int) and t == 0):
                        gp.wait_ge(map_copied, t * 2 + 1)
                    stage_ids(t, b, 2 * TE, 2, [(gi[b][:, 0:8], "src_of"), (gi[b][:, 8:16], "dst_row")])
                    for k in range(16):
                        g.indirect_dma_start(gv[b][:, k:k + 1], None, node_slot, at(gi[b], k))\
                            .then_inc(map_got[b], 16)
                for b in range(nb):
                    gp.wait_ge(map_got[b], t * (4 * 16) + 16 * 16)
                    for k, name in enumerate(("src_map", "dst_map")):
                        g.tensor_copy(ids[name][:, bass.ds((t + b) * 8, 8)], gv[b][:, 8 * k:8 * k + 8])\
                            .then_inc(map_copied, 1)
            each_batch(gp, "src", get)

            def gather_tile(ph, sources, first, t, b):
                per = len(sources)
                if not (isinstance(t, int) and t * 4 * GATHERS[ph] + before(GATHERS, ph, b) == 0):
                    gp.wait_ge(gathered[b], t * (4 * GATHERS[ph]) + before(GATHERS, ph, b))
                wait_before(gp, ph, "turned_in", t, b)
                stage_ids(t, b, first, per, [(gi[b][:, 8 * k:8 * k + 8], s[0]) for k, s in enumerate(sources)])
                for k, (name, from_, to, order) in enumerate(sources):
                    for j in range(8):
                        c = j if order == "any" else (j % Q) * H + j // Q
                        g.indirect_dma_start(to[b][:, c * D:c * D + D], None, from_, at(gi[b], 8 * k + j))\
                            .then_inc(gathered[b], 16)

            def gathers(ph, sources, first):
                def body(t, nb):
                    for b in range(nb):
                        gather_tile(ph, sources, first, t, b)
                each_batch(gp, ph, body, peel=(ph == "src"))

            wait_phase(gp, "main", "turned_in")
            gathers("src", [("src_rows", a["x"], rows, "any")], 4 * TE)
            wait_phase(gp, "src", "turned_in")
            gathers("d0", [("src_of", a["x"], rows, "edge"), ("dst_row", a["x"], rows2, "edge")], 5 * TE)
            gp.wait_ge(ids_ready, 5)

            def table_ready(level, ph):
                for b in range(B):
                    gp.wait_ge(stored[b], before(STORES, ph, b) + 16 * STORES[ph] * slot_uses(ph, b))

            for k in range(1, 6):
                table_ready(k, f"d{k - 1}")
                gathers(f"d{k}", [("src_slot", table[k], rows, "edge")], (6 + k) * TE)
            table_ready(6, "d5")

            sources = [("src_slot", table[6], rows, "edge"), ("dst_slot", table[6], rows2, "edge")]
            PER = 3

            def last_gather(t, b, n):
                gp.wait_ge(gathered[b], t * (4 * GATHERS["d6"]) + (before(GATHERS, "d6", b)))
                wait_before(gp, "d6", "turned_in", t, b)
                for k, (name, from_, to, order) in enumerate(sources):
                    g.tensor_copy(gi[b][:, 8 * k:8 * k + 8], ids[name][:, bass.ds((t + b) * 8, 8)]).then_inc(staged, 1)
                gp.wait_ge(staged, n)
                settle(gp)
                for k, (name, from_, to, order) in enumerate(sources):
                    for j in range(8):
                        c = (j % Q) * H + j // Q
                        g.indirect_dma_start(to[b][:, c * D:c * D + D], None, from_, at(gi[b], 8 * k + j))\
                            .then_inc(gathered[b], 16)

            def last_scatter(t, b, n):
                if not (isinstance(t, int) and t == 0):
                    gp.wait_ge(scattered[b], t * (4 * 8))
                g.tensor_copy(gv[b][:, 0:8], ids["put_row"][:, bass.ds((t + b) * 8, 8)]).then_inc(staged, 1)
                gp.wait_ge(staged, n)
                wait(gp, "d6", "rows_out7", t, b)
                settle(gp)
                for j in range(8):
                    c = (j % Q) * H + j // Q
                    g.indirect_dma_start(out, at(gv[b], j), rows_o[b][:, c * D:c * D + D], None,
                                         bounds_check=N - 1, oob_is_err=False).then_inc(scattered[b], 16)

            s0 = 12 * TE
            for b in range(B):
                last_gather(0, b, s0 + 2 * (b + 1))
            s0 += 2 * B

            def last_batch(t):
                for b in range(B):
                    last_gather(t + B, b, t * PER + (s0 + 2 * (b + 1)))
                for b in range(B):
                    last_scatter(t, b, t * PER + (s0 + 2 * B + b + 1))
            last_batch(0)
            with gp.Fori(B, full - 2 * B + 1, B) as t:
                last_batch(t)
            s0 += PER * (full - B)
            rem = TE - full
            for b in range(rem):
                last_gather(full, b, s0 + 2 * (b + 1))
            for b in range(B):
                last_scatter(full - B, b, s0 + 2 * rem + b + 1)
            for b in range(rem):
                last_scatter(full, b, s0 + 2 * rem + B + b + 1)
            for b in range(B):
                gp.wait_ge(scattered[b], 16 * 8 * slot_uses("d6", b))


def kernel(**inputs):
    import numpy as np
    import concourse.bacc as bacc
    from concourse.bass_utils import run_bass_kernel_spmd

    nc = bacc.Bacc("TRN2", target_bir_lowering=False, num_devices=1)
    arrays = {name: np.ascontiguousarray(x) for name, x in inputs.items()}
    aps = {name: nc.dram_tensor(f"in_{name}", x.shape, mybir.dt.from_np(x.dtype), kind="ExternalInput").ap()
           for name, x in arrays.items()}
    out = nc.dram_tensor("out", arrays["x"].shape, mybir.dt.from_np(arrays["x"].dtype), kind="ExternalOutput").ap()
    build(nc, aps, out)
    result = run_bass_kernel_spmd(nc, [{f"in_{name}": x for name, x in arrays.items()}], core_ids=[0])
    return result.results[0]["out"]
```

```python
from contextlib import ExitStack

import concourse.bass as bass
from concourse import mybir

F32 = mybir.dt.float32
I32 = mybir.dt.int32
ALU = mybir.AluOpType
ACT = mybir.ActivationFunctionType

P = 128
D = 64
H = 2
COLS = 512
TILE = H * COLS
Q = COLS // P
B = 4
M = 2
EPS = 1e-5
BIG = 1e30
OUTSIDE = 1 << 20


def build(nc, a, out):
    N = a["x"].shape[0]
    E = a["src"].shape[0]
    TM = -(-N // TILE)
    TE = -(-E // TILE)
    SLOTS = TE * TILE
    LAST_E = E - (TE - 1) * TILE
    LAST_P = LAST_E // Q
    assert LAST_E % Q == 0 and LAST_E <= COLS and N < OUTSIDE and N % 8 == 0

    norm = lambda l: [f"{s}{l}" for s in ("centred", "squared", "variance", "logvar", "rstd", "normed")]
    sage = lambda i: norm(1 + i) + [f"scaled_norm{i}", f"added{i}"] + (["residual_mm", "relu"] if i == 0 else [])
    gru = lambda r: [f"{s}{r}" for s in ("gate_r", "gate_z", "gate_n", "sig_r", "sig_z", "reset", "tanh",
                                         "diff", "scaled", "hidden")]
    save = lambda l: [f"turned_out{l}", f"rows_out{l}"]
    chain = (["turned_in", "x_in"] + norm(0) + sage(0) + sage(1) + sage(2) + norm(4) + gru(0) + gru(1)
             + ["summed"] + norm(5))
    saves = sum((save(l) for l in range(1, 7)), [])
    gather2 = ["turned_in", "turned_dst", "src_in", "x_in", "turned_edge", "edge_in"]
    PHASES = [
        ("src", TE, chain + saves),
        ("d0", TE, gather2 + ["same", "hidden_mm", "small_slope", "leaky", "penalty", "logits", "max_before",
                              "new_weight", "max_step", "max_shift", "log_degree", "inv_degree", "decay_exp",
                              "weight_exp", "weighted", "log_den", "inv_den", "mixed"] + norm(0) + save(1)),
        ("d1", TE, ["turned_in", "mean"] + sage(0) + save(2)),
        ("d2", TE, ["turned_in", "mean"] + sage(1) + save(3)),
        ("d3", TE, ["turned_in", "mean"] + sage(2) + norm(4) + save(4)),
        ("d4", TE, ["turned_in", "turned_edge", "times_degree", "message", "message_in", "reset_sum"] + gru(0)
         + save(5)),
        ("d5", TE, ["turned_in", "turned_edge", "times_degree", "message", "message_in", "reset_sum"] + gru(1)
         + ["summed"] + norm(5) + save(6)),
        ("d6", TE, gather2 + ["hidden_mm", "hidden_relu0", "hidden_relu1", "message", "mean"] + norm(6) + save(7)),
    ]
    STEP = {"src": (1, 2), "d0": (1, 2), "d1": (2, 1), "d2": (2, 1), "d3": (2, 1), "d4": (2, 1), "d5": (1, 1),
            "d6": (1, 0)}
    NODES = {ph: f"nodes_{ph}" for ph, (_, batches) in STEP.items() if batches}
    node_batch, n = {}, 0
    for ph, node_ph in NODES.items():
        fours, batches = STEP[ph]
        assert TE % (fours * B) == 1
        node_batch[node_ph] = n
        n += (TE - 1) // (fours * B) * batches + 1
        PHASES.append((node_ph, M * (n - node_batch[node_ph]), chain + norm(6) + save(7)))
    assert n * M == TM
    is_nodes = lambda ph: ph.startswith("nodes_")
    NODE_INC = 4
    tiles_of = {ph: tiles for ph, tiles, _ in PHASES}
    kind_of = lambda stage: stage.rstrip("0123456789")
    kind = lambda ph, stage: ("node_" if is_nodes(ph) else "") + kind_of(stage)
    turn, turns, base, count = {}, {}, {}, {}
    for ph, tiles, stages in PHASES:
        for s in stages:
            k = kind(ph, s)
            turn[ph, s] = turns.get((ph, k), 0)
            turns[ph, k] = turn[ph, s] + 1
        for k in dict.fromkeys(kind(ph, s) for s in stages):
            base[ph, k] = count.get(k, 0)
            count[k] = base[ph, k] + turns[ph, k] * tiles
    ROUNDS = {"src": 10, "d0": 9, "d1": 3, "d2": 3, "d3": 4, "d4": 4, "d5": 5, "d6": 5, "nodes": 9}
    SCANS = [("d0", 4)] + [(f"d{k}", 1) for k in (1, 2, 3)] + [("d4", 2), ("d5", 2), ("d6", 1)]
    scan_base, n = {}, 0
    for ph, k in SCANS:
        scan_base[ph] = (n, k)
        n += 2 * k * TE

    def slot_uses(ph, b):
        return -(-(tiles_of[ph] - b) // B)

    LOADS = {"d0": 4, "d1": 3, "d2": 3, "d3": 4, "d4": 5, "d5": 6, "d6": 5}
    GATHERS = {"src": 8, "d0": 16, "d1": 8, "d2": 8, "d3": 8, "d4": 8, "d5": 8, "d6": 16}
    STORES = {"src": 6, "d0": 2, "d1": 2, "d2": 2, "d3": 2, "d4": 2, "d5": 2}
    KEEPS = {"d0": 4, "d1": 1, "d2": 1, "d3": 1, "d4": 1, "d5": 1}

    def before(table, ph, b):
        v = 0
        for name, _, _ in PHASES:
            if name == ph:
                return v
            v += 16 * table.get(name, 0) * slot_uses(name, b)
        return v

    with ExitStack() as ctx:
        def sb(name, shape, dt=F32):
            return ctx.enter_context(nc.sbuf_tensor(name, shape, dt))

        def dram(name, shape, dt=F32):
            return nc.dram_tensor(name, shape, dt, kind="Internal").ap()

        def sem(name):
            return ctx.enter_context(nc.semaphore(name))

        S = {k: sem(k) for k in count}
        loaded = [sem(f"loaded{b}") for b in range(B + M)]
        gathered = [sem(f"gathered{b}") for b in range(B)]
        stored = [sem(f"stored{b}") for b in range(B + M)]
        kept = [sem(f"kept{b}") for b in range(B)]
        scattered = [sem(f"scattered{b}") for b in range(B)]
        carried, scanned = sem("carried"), sem("scanned")
        weights_in, zeroed, consts, prep_pe, prep_dve = (sem(n) for n in (
            "weights_in", "zeroed", "consts", "prep_pe", "prep_dve"))
        pad_filled, pad_put, ids_in, ids_ready, fills, iota_done, id_steps, ident_zero = (
            sem(n) for n in ("pad_filled", "pad_put", "ids_in", "ids_ready", "fills", "iota_done", "id_steps",
                             "ident_zero"))
        map_zero, map_copied, staged, ones_set, passed = (
            sem(n) for n in ("map_zero", "map_copied", "staged", "ones_set", "passed"))
        map_put = [sem(f"map_put{b}") for b in range(B)]
        map_got = [sem(f"map_got{b}") for b in range(B)]

        dst_pad = dram("dst_pad", (P * (TE * 8 + 1),), I32)
        src_pad = dram("src_pad", (SLOTS,), I32)
        node_slot = dram("node_slot", (N, 1), I32)
        table = {l: dram(f"table{l}", (2 * SLOTS, D)) for l in range(1, 7)}
        state = {l: dram(f"state{l}", (TE * P, COLS)) for l in range(1, 7)}
        same_d = dram("same_d", (TE * P, COLS))
        degree_d = dram("degree_d", (TE * P, COLS))
        inv_degree_d = dram("inv_degree_d", (TE * P, COLS))

        def ring(name, edge, node=0, cols=COLS, dt=F32):
            tiles = [sb(f"{name}{b}", [P, cols], dt) for b in range(edge + node)]
            return tiles[:edge] * (B // edge) + tiles[edge:]

        rows, rows_o, X, Y = (ring(n, B, M) for n in ("rows", "rows_o", "X", "Y"))
        Z, R, W = (ring(n, M, M) for n in "ZRW")
        rows2, edges, SAME, DEG, MSG = (ring(n, B) for n in ("rows2", "edges", "SAME", "DEG", "MSG"))
        IDS = ring("IDS", B, 0, COLS + 1, I32)
        XS, EF, AG, DN, DC = (ring(n, 2) for n in ("XS", "EF", "AG", "DN", "DC"))
        MX = ring("MX", 2, 0, COLS + 1)
        carry = sb("carry", [P, 1])

        def banks(name):
            b = [ctx.enter_context(nc.psum_tensor(f"{name}{b}", [P, COLS], F32)) for b in range(4)]
            return b[:2] * 2 + b[2:]
        PA, PB = banks("PA"), banks("PB")

        NT = 10
        names = (["wr0", "wr1", "wr2", "wfc", "wl0", "wl1", "wl2", "wn", "w1x", "w1e", "w2", "wres"]
                 + [f"{n}{t}" for t in range(2) for n in ("msg_s", "msg_d", "msg_e", "ih_r", "ih_z", "ih_n",
                                                          "hh_r", "hh_z", "hh_n")])
        wraw = sb("wraw", [P, len(names), P])
        wat = {n: wraw[:, i, :] for i, n in enumerate(names)}
        wturned = sb("wturned", [P, NT, P])
        wcentred = sb("wcentred", [P, 9, P])
        wc = {n: wcentred[:, i, :] for i, n in enumerate(names[:8] + ["w2"])}
        w3s, w3d, w3e = sb("w3s", [P, P]), sb("w3d", [P, P]), sb("w3e", [P, P])
        w3o = sb("w3o", [P, D])
        ident, ones_block, mean_block, centre = (sb(n, [P, P]) for n in ("ident", "ones_block", "mean_block", "centre"))
        att_f, att_r = sb("att_f", [P, P]), sb("att_r", [P, P])
        ones = sb("ones", [P, COLS])
        eps = sb("eps", [P, 1])
        cols = ["bias0", "bl0", "bl1", "bl2", "bfc", "zero", "bn", "b3", "g0", "g1", "g2", "be0", "be1", "be2",
                "bres", "att_f", "att_r", "ih_r0", "ih_z0", "ih_n0", "hh_r0", "hh_z0", "hh_n0",
                "ih_r1", "ih_z1", "ih_n1", "hh_r1", "hh_z1", "hh_n1", "b2"]
        bias = sb("bias", [P, 32])
        bias_rows = sb("bias_rows", [32, P])
        bcol = {n: bias[:, i:i + 1] for i, n in enumerate(cols)}
        NC = 8
        bcent = sb("bcent", [P, NC])
        b1col = sb("b1col", [P, 1])
        gate_b = sb("gate_b", [P, 4])
        norm_bias = {0: 0, 1: 1, 2: 2, 3: 3, 4: 4, 5: 5, 6: 6, "6d": 7}

        ids = {n: sb(n, [P, TE * 8], I32) for n in
               ("dst_of", "dst_next", "src_of", "src_rows", "dst_row", "put_row", "slot1", "src_map", "dst_map",
                "src_slot", "dst_slot")}
        idf = sb("idf", [P, TE * 8])
        idf2 = sb("idf2", [P, TE * 8])
        fill = sb("fill", [P, 2, TE * 8 + 1], I32)
        zero_map = sb("zero_map", [80, N // 80], I32)
        gi = [sb(f"gi{b}", [P, 16], I32) for b in range(B)]
        gv = [sb(f"gv{b}", [P, 16], I32) for b in range(B)]
        mi = [sb(f"mi{b}", [P, 16], I32) for b in range(B)]

        weight_loads = []
        def load_block(name, src, row=0):
            k, n, f = src.shape
            i = names.index(name)
            for h in range(H):
                weight_loads.append((wraw[h * D + row:h * D + row + k, i:i + n, h * D:h * D + f], src))
        one = lambda x: x.rearrange("k (n f) -> k n f", n=1)
        load_block("wr0", a["L1_gnn_w_r"].rearrange("n k f -> k n f"))
        load_block("wl0", a["L1_gnn_w_l"].rearrange("n k f -> k n f"))
        load_block("wfc", one(a["L1_gnn_w_fc"]))
        load_block("wn", one(a["L3_gnn_Wn"]))
        load_block("w1x", one(a["L0_gnn_W1"][:, 0:D]))
        load_block("w1e", one(a["L0_gnn_W1"][:, D:]))
        load_block("w2", one(a["L0_gnn_W2"]))
        load_block("wres", one(a["L1_gnn_w_res"]))
        for t in range(2):
            m = a["L2_gnn_W_msg"][t]
            load_block(f"msg_s{t}", m[0:2 * D, :].rearrange("(n k) f -> k n f", n=2))
            load_block(f"msg_e{t}", one(m[2 * D:, :]))
            load_block(f"msg_e{t}", one(a["L2_gnn_b_msg"][t:t + 1, :]), 4)
            load_block(f"ih_r{t}", a["L2_gnn_W_ih"][t].rearrange("k (n f) -> k n f", n=3))
            load_block(f"hh_r{t}", a["L2_gnn_W_hh"][t].rearrange("k (n f) -> k n f", n=3))
        w3 = a["L3_gnn_W1"]
        for h in range(H):
            weight_loads += [(w3s[h * D:h * D + D, :], w3[0:D, :]), (w3d[h * D:h * D + D, :], w3[D:2 * D, :]),
                             (w3e[h * D:h * D + 32, :], w3[2 * D:, :])]
        weight_loads.append((w3o[:, :], a["L3_gnn_W2"]))
        weight_loads.append((b1col[:, :], a["L3_gnn_b1"].rearrange("(f n) -> f n", n=1)))
        matrix = lambda x, n=1: x.rearrange("(n f) -> n f", n=n)
        vectors = {"bias0": matrix(a["L0_gnn_bias"]), "bfc": matrix(a["L1_gnn_b_fc"]),
                   "bres": matrix(a["L1_gnn_b_res"]), "bn": matrix(a["L3_gnn_bn"]), "b2": matrix(a["L3_gnn_b2"]),
                   "att_f": matrix(a["L0_gnn_attn"], 2), "bl0": a["L1_gnn_b_l"], "g0": a["L1_gnn_gamma"],
                   "be0": a["L1_gnn_beta"]}
        for t in range(2):
            vectors |= {f"ih_r{t}": matrix(a["L2_gnn_b_ih"][t], 3), f"hh_r{t}": matrix(a["L2_gnn_b_hh"][t], 3)}
        for name, rows_of in vectors.items():
            i, n = cols.index(name), rows_of.shape[0]
            for h in range(H):
                weight_loads.append((bias_rows[i:i + n, h * D:h * D + D], rows_of))
        n_weight_dmas = len(weight_loads)

        block = ctx.enter_context(nc.Block())

        def take_turns(ph, t, edge_rounds, node_rounds, fresh, last=False):
            fours, batches = STEP[ph]
            pairs = [(t, range(0, 1))] if last else [(t + i * B, bs) for i in range(fours)
                                                     for bs in (range(0, 2), range(2, B))]
            if last:
                batches = min(batches, 1)
            fresh()
            edge = (None for at, bs in pairs for _ in edge_rounds(at, bs))
            node = (None for j in range(batches) for _ in node_rounds((t, j)))
            n_edge, n_node = (ROUNDS[ph] - 1) * len(pairs) + 1, (ROUNDS["nodes"] - 1) * batches + bool(batches)
            stretch = n_edge if last else n_node
            order = sorted([((i + 0.5) / n_edge, 0, i) for i in range(n_edge)]
                           + [((i + 0.6) / stretch, 1, i) for i in range(n_node)])
            for _, nodes, i in order:
                stream, count, rounds = (node, n_node, ROUNDS["nodes"]) if nodes else (edge, n_edge, ROUNDS[ph])
                next(stream)
                if 0 < i < count - 1 and i % (rounds - 1) == 0:
                    next(stream)
            assert next(edge, "over") == "over" and next(node, "over") == "over"

        def each_step(eng, ph, edge_rounds, node_rounds=None, peel=False, fresh=lambda: None):
            size = STEP[ph][0] * B
            if peel:
                take_turns(ph, 0, edge_rounds, node_rounds, fresh)
            with eng.Fori(size if peel else 0, TE - size, size) as t:
                take_turns(ph, t, edge_rounds, node_rounds, fresh)
            take_turns(ph, TE - 1, edge_rounds, node_rounds, fresh, last=True)

        def pair_size(t):
            return 1 if isinstance(t, int) and t == TE - 1 else 2

        def sem_of(ph, stage):
            return S[kind(ph, stage)]

        def per(ph):
            return NODE_INC if is_nodes(ph) else 1

        def node_place(ph, at, per_batch):
            t, j = at
            fours, batches = next(STEP[p] for p in NODES if NODES[p] == ph)
            assert per_batch * batches % (fours * B) == 0
            return t * (per_batch * batches // (fours * B)) + (node_batch[ph] + j) * per_batch

        def wait(eng, ph, stage, t, b):
            k = kind(ph, stage)
            if is_nodes(ph):
                eng.wait_ge(S[k], node_place(ph, t, NODE_INC * M * turns[ph, k])
                            + NODE_INC * (turn[ph, stage] * M + b - B + 1))
            else:
                eng.wait_ge(S[k], t * turns[ph, k] + (base[ph, k] + turns[ph, k] * (b // 2 * 2)
                                                      + turn[ph, stage] * pair_size(t) + b % 2 + 1))

        def wait_before(eng, ph, stage, t, b, back=B):
            k = kind(ph, stage)
            v = base[ph, k] + turns[ph, k] * (b // 2 * 2 - back) + turn[ph, stage] * 2 + b % 2 + 1
            assert v >= 1
            eng.wait_ge(S[k], t * turns[ph, k] + v)

        def wait_phase(eng, ph, stage):
            k = kind(ph, stage)
            eng.wait_ge(S[k], base[ph, k] + turns[ph, k] * tiles_of[ph])

        def settle(eng):
            eng.sem_inc(passed, 1)

        def wait_loaded(eng, ph, t, b):
            if is_nodes(ph):
                eng.wait_ge(loaded[b], node_place(ph, t, 16) + 16)
            else:
                eng.wait_ge(loaded[b], t * (4 * LOADS[ph]) + (before(LOADS, ph, b) + 16 * LOADS[ph]))

        def wait_gathered(eng, ph, t, b):
            eng.wait_ge(gathered[b], t * (4 * GATHERS[ph]) + (before(GATHERS, ph, b) + 16 * GATHERS[ph]))

        def wait_stored(eng, ph, t, b, k):
            if is_nodes(ph):
                eng.wait_ge(stored[b], node_place(ph, t, 16) + 1)
            else:
                eng.wait_ge(stored[b], t * (4 * STORES.get(ph, 0)) + (before(STORES, ph, b) + 16 * k + 1))

        def scan_place(ph, t, b, k):
            first, per_tile = scan_base[ph]
            if ph == "d0":
                return first + 16 * (b // 2) + 4 * (k // 2) * pair_size(t) + 4 * (b % 2) + 2 * (k % 2)
            return first + 2 * (per_tile * b + k)

        def wait_scans(eng, ph, t, b, k):
            eng.wait_ge(scanned, t * (2 * scan_base[ph][1]) + (scan_place(ph, t, b, k - 1) + 3))

        n_id_loads = 3 * H + 1

        @block.tensor
        def _(pe):
            mm = nc.tensor.matmul

            pe.wait_ge(weights_in, 16 * n_weight_dmas)
            pe.wait_ge(consts, 2)
            for i in range(NT):
                bank = [PA[0], PB[0], PA[1]][i // Q]
                last = nc.tensor.transpose(bank[:, (i % Q) * P:(i % Q + 1) * P], wraw[:, i, :], ident[:, :])
            last = nc.tensor.transpose(PA[B][:, 0:32], bias_rows[:, :], ident[0:32, 0:32])
            last.then_inc(prep_pe, 1)
            pe.wait_ge(prep_dve, 1)
            for i in range(8):
                bank = [PB[1], PA[2]][i // Q]
                mm(bank[:, (i % Q) * P:(i % Q + 1) * P], wturned[:, i, :], centre[:, :], start=True, stop=True)
            mm(PB[2][:, 0:P], wat["w2"], centre[:, :], start=True, stop=True)
            mm(PB[2][:, P:P + NC], centre[:, :], bias[:, 0:NC], start=True, stop=True).then_inc(prep_pe, 1)
            pe.wait_ge(prep_dve, 2)

            def turn_in(ph, t, b, src, bank, order, stage):
                for q in range(Q):
                    o = bank[b][:, q * P:(q + 1) * P] if order == "any" else bank[b][:, q::Q]
                    last = nc.tensor.transpose(o, src[b][:, q * P:(q + 1) * P], ident[:, :])
                last.then_inc(sem_of(ph, stage), per(ph))

            def turn_out(ph, t, bs, st, order, level, after):
                for b in bs:
                    wait(pe, ph, after, t, b)
                    for q in range(Q):
                        i = st[b][:, q * P:(q + 1) * P] if order == "any" else st[b][:, q::Q]
                        last = nc.tensor.transpose(PB[b][:, q * P:(q + 1) * P], i, ident[:, :])
                    last.then_inc(sem_of(ph, "turned_out"), per(ph))

            def variance(ph, t, bs, l):
                for b in bs:
                    wait(pe, ph, f"squared{l}", t, b)
                    mm(PB[b][:, :], mean_block[:, :], R[b][:, :], start=True, stop=True)\
                        .then_inc(sem_of(ph, "variance"), per(ph))

            def product(ph, t, bs, bank, pairs, stage, waits):
                for b in bs:
                    for w in waits:
                        wait(pe, ph, w, t, b)
                    for k, (w, st) in enumerate(pairs):
                        last = mm(bank[b][:, :], w, st[b][:, :], start=(k == 0), stop=(k == len(pairs) - 1))
                    last.then_inc(sem_of(ph, stage), per(ph))

            def norm_of(ph, t, bs, l, pairs, waits):
                product(ph, t, bs, PA, pairs, f"centred{l}", waits)
                variance(ph, t, bs, l)

            def sage_layer(ph, t, bs, i, waits, mean):
                st = X if i == 0 else Y
                pairs = [(wc[f"wr{i}"], st)] + ([(wc[f"wl{i}"], AG)] if mean else [])
                norm_of(ph, t, bs, 1 + i, pairs, waits + (["mean"] if mean else []))

                if i == 0:
                    product(ph, t, bs, PB, [(wat["wres"], X)], "residual_mm", ["logvar1"])

            def gates(ph, t, bs, r, st, waits, msg):
                m = lambda g: [(wat[f"ih_{g}{r}"], MSG)] if msg else []
                more = ["message_in"] if msg else []
                product(ph, t, bs, PA, [(wat[f"hh_r{r}"], st)] + m("r"), f"gate_r{r}", waits + more)
                product(ph, t, bs, PB, [(wat[f"hh_z{r}"], st)] + m("z"), f"gate_z{r}", [])
                for b in bs:
                    wait(pe, ph, f"sig_r{r}", t, b)
                    last = mm(PA[b][:, :], wat[f"hh_n{r}"], st[b][:, :], start=True, stop=True)
                    if msg:
                        wait(pe, ph, f"sig_z{r}", t, b)
                        last = mm(PB[b][:, :], wat[f"ih_n{r}"], MSG[b][:, :], start=True, stop=True)
                    last.then_inc(sem_of(ph, "gate_n"), per(ph))

            def chain(ph, t, bs, order, saving):
                def out_of(level, st, after):
                    if saving:
                        turn_out(ph, t, bs, st, order, level, after)
                for b in bs:
                    (wait_loaded if is_nodes(ph) else wait_gathered)(pe, ph, t, b)
                    turn_in(ph, t, b, rows, PA, order, "turned_in")
                if not is_nodes(ph):
                    yield
                norm_of(ph, t, bs, 0, [(centre[:, :], X)], ["x_in"])
                yield
                out_of(1, X, "normed0")
                sage_layer(ph, t, bs, 0, ["normed0"], False)
                yield
                out_of(2, Y, "added0")
                sage_layer(ph, t, bs, 1, ["added0"], False)
                yield
                out_of(3, Y, "added1")
                sage_layer(ph, t, bs, 2, ["added1"], False)
                yield
                norm_of(ph, t, bs, 4, [(wc["wfc"], Y), (centre[:, :], X)], ["added2"])
                yield
                out_of(4, X, "normed4")
                gates(ph, t, bs, 0, X, ["normed4"] + ["rows_out4"] * saving, False)
                yield
                out_of(5, Y, "hidden0")
                gates(ph, t, bs, 1, Y, ["hidden0"] + ["rows_out5"] * saving, False)
                yield
                norm_of(ph, t, bs, 5, [(centre[:, :], Y)], ["summed"])
                yield
                if is_nodes(ph):
                    norm_of(ph, t, bs, 6, [(wc["wn"], X)], ["normed5"])
                    turn_out(ph, t, bs, X, order, 7, "normed6")
                out_of(6, X, "normed5")
                yield

            def nodes_of(ph):
                return lambda t: chain(NODES[ph], t, range(B, B + M), "any", False)

            each_step(pe, "src", lambda t, bs: chain("src", t, bs, "any", True), nodes_of("src"))

            level = {"d0": 1, "d4": 5, "d5": 6, "d6": 7}

            def pb_free(ph, t, b):
                wait_before(pe, ph, f"rows_out{level[ph]}", t, b, back=2)

            def phase_over(ph, lev):
                wait_phase(pe, ph, f"rows_out{lev}")

            def turn_edge_inputs(ph, t, bs):
                for b in bs:
                    wait_gathered(pe, ph, t, b)
                    pb_free(ph, t, b)
                    turn_in(ph, t, b, rows2, PB, "edge", "turned_dst")
                    turn_in(ph, t, b, rows, PA, "edge", "turned_in")
                for b in bs:
                    wait(pe, ph, "src_in", t, b)
                    wait_loaded(pe, ph, t, b)
                    turn_in(ph, t, b, edges, PA, "edge", "turned_edge")

            def d0(t, bs):
                turn_edge_inputs("d0", t, bs)
                yield
                product("d0", t, bs, PA, [(wturned[:, 8, :], XS), (wturned[:, 9, :], EF)], "hidden_mm", ["edge_in"])
                yield
                product("d0", t, bs, PB, [(att_f[:, :], Z), (att_r[:, :], W)], "logits", ["leaky", "x_in"])
                yield
                yield
                yield
                yield
                yield
                norm_of("d0", t, bs, 0, [(centre[:, :], X), (wc["w2"], AG)], ["mixed"])
                yield
                turn_out("d0", t, bs, X, "edge", 1, "normed0")
                yield
            phase_over("src", 6)
            each_step(pe, "d0", d0, nodes_of("d0"))

            def turn_src(ph, t, bs):
                for b in bs:
                    wait_gathered(pe, ph, t, b)
                    wait_loaded(pe, ph, t, b)
                    turn_in(ph, t, b, rows, PA, "edge", "turned_in")

            def sage_phase(ph, i):
                def rounds(t, bs):
                    turn_src(ph, t, bs)
                    yield
                    sage_layer(ph, t, bs, i, [], True)
                    yield
                    if i == 2:
                        norm_of(ph, t, bs, 4, [(wc["wfc"], Y), (centre[:, :], X)], ["added2"])
                        yield
                        turn_out(ph, t, bs, X, "edge", 4, "normed4")
                    else:
                        turn_out(ph, t, bs, Y, "edge", 2 + i, f"added{i}")
                    yield
                each_step(pe, ph, rounds, nodes_of(ph))
            for i in range(3):
                sage_phase(f"d{1 + i}", i)

            def gru_phase(ph, r):
                st = X if r == 0 else Y
                def rounds(t, bs):
                    turn_src(ph, t, bs)
                    for b in bs:
                        pb_free(ph, t, b)
                        turn_in(ph, t, b, edges, PB, "edge", "turned_edge")
                    yield
                    for b in bs:
                        wait_scans(pe, ph, t, b, 2)
                    product(ph, t, bs, PA, [(wat[f"msg_s{r}"], AG), (wat[f"msg_d{r}"], W), (wat[f"msg_e{r}"], EF)],
                            "message", ["times_degree"])
                    yield
                    gates(ph, t, bs, r, st, [], True)
                    yield
                    if r == 1:
                        norm_of(ph, t, bs, 5, [(centre[:, :], Y)], ["summed"])
                        yield
                        turn_out(ph, t, bs, X, "edge", 6, "normed5")
                    else:
                        turn_out(ph, t, bs, Y, "edge", 5, "hidden0")
                    yield
                each_step(pe, ph, rounds, nodes_of(ph))
            phase_over("d3", 4)
            pe.wait_ge(ones_set, 1)
            gru_phase("d4", 0)
            phase_over("d4", 5)
            gru_phase("d5", 1)
            phase_over("d5", 6)

            def d6(t, bs):
                turn_edge_inputs("d6", t, bs)
                yield
                for b in bs:
                    wait(pe, "d6", "x_in", t, b)
                    wait(pe, "d6", "edge_in", t, b)
                    for h, bank in enumerate((PA, PB)):
                        r = slice(h * D, h * D + D)
                        mm(bank[b][:, :], w3s[r, :], XS[b][r, :], start=True, stop=False)
                        mm(bank[b][:, :], w3d[r, :], Y[b][r, :], start=False, stop=False)
                        last = mm(bank[b][:, :], w3e[r, :], EF[b][r, :], start=False, stop=True)
                    last.then_inc(S["hidden_mm"], 1)
                yield
                for b in bs:
                    wait(pe, "d6", "hidden_relu0", t, b)
                    mm(PA[b][0:D, :], w3o[:, :], Z[b][:, :], start=True, stop=True)
                    wait(pe, "d6", "hidden_relu1", t, b)
                    mm(PA[b][D:P, :], w3o[:, :], W[b][:, :], start=True, stop=True).then_inc(S["message"], 1)
                yield
                norm_of("d6", t, bs, 6, [(wc["wn"], X), (centre[:, :], AG)], ["mean"])
                yield
                turn_out("d6", t, bs, X, "edge", 7, "normed6")
                yield
            each_step(pe, "d6", d6)

        @block.scalar
        def _(act):
            fn = nc.scalar.activation

            def per_tile(ph, t, bs, stage, waits, op):
                for b in bs:
                    for w in waits:
                        wait(act, ph, w, t, b)
                    op(b).then_inc(sem_of(ph, stage), per(ph))

            tables = {"log_exp": False}

            def log_exp_tables():
                if not tables["log_exp"]:
                    nc.scalar.preload_act_table_set("natural_log_exp_and_others")
                tables["log_exp"] = True

            def norm_of(ph, t, bs, l, bias_id=None):
                log_exp_tables()
                c = norm_bias[l if bias_id is None else bias_id]
                per_tile(ph, t, bs, f"squared{l}", [f"centred{l}"],
                         lambda b: fn(R[b][:, :], PA[b][:, :], ACT.Square, bias=bcent[:, c:c + 1]))
                for b in bs:
                    one = range(b, b + 1)
                    per_tile(ph, t, one, f"logvar{l}", [f"variance{l}"],
                             lambda b: fn(R[b][:, :], PB[b][:, :], ACT.Ln, bias=eps[:, :]))
                    per_tile(ph, t, one, f"rstd{l}", [f"logvar{l}"],
                             lambda b: fn(R[b][:, :], R[b][:, :], ACT.Exp, scale=-0.5))

            def gates(ph, t, bs, r, msg):
                tables["log_exp"] = False
                per_tile(ph, t, bs, f"sig_r{r}", [f"gate_r{r}"],
                         lambda b: fn(R[b][:, :], PA[b][:, :], ACT.Sigmoid, bias=gate_b[:, 2 * r:2 * r + 1]))
                per_tile(ph, t, bs, f"sig_z{r}", [f"gate_z{r}"],
                         lambda b: fn(Z[b][:, :], PB[b][:, :], ACT.Sigmoid, bias=gate_b[:, 2 * r + 1:2 * r + 2]))
                per_tile(ph, t, bs, f"tanh{r}", ["reset_sum" if msg else f"reset{r}"],
                         lambda b: fn(R[b][:, :], R[b][:, :], ACT.Tanh, bias=bcol[f"ih_n{r}"]))

            def rows_out(ph, t, bs, level, k):
                for b in bs:
                    wait(act, ph, f"turned_out{level}", t, b)
                    if ph == "d6":
                        if not (isinstance(t, int) and t == 0):
                            act.wait_ge(scattered[b], t * (4 * 8))
                    wait_stored(act, ph, t, b, k)
                    fn(rows_o[b][:, :], PB[b][:, :], ACT.Copy).then_inc(sem_of(ph, "rows_out"), per(ph))

            act.wait_ge(zeroed, 1)
            for to, from_ in weight_loads[1::2]:
                nc.scalar.dma_start(to, from_).then_inc(weights_in, 16)
            act.wait_ge(prep_dve, 3)

            def chain(ph, t, bs, saving):
                def out_of(level):
                    if saving:
                        rows_out(ph, t, bs, level, level - 1)
                per_tile(ph, t, bs, "x_in", ["turned_in"], lambda b: fn(X[b][:, :], PA[b][:, :], ACT.Copy))
                if not is_nodes(ph):
                    yield
                norm_of(ph, t, bs, 0)
                yield
                for i in range(3):
                    out_of(1 + i)
                    norm_of(ph, t, bs, 1 + i)
                    yield
                norm_of(ph, t, bs, 4)
                yield
                for r in range(2):
                    out_of(4 + r)
                    gates(ph, t, bs, r, False)
                    yield
                norm_of(ph, t, bs, 5)
                yield
                if is_nodes(ph):
                    norm_of(ph, t, bs, 6)
                    rows_out(ph, t, bs, 7, 0)
                out_of(6)
                yield

            def nodes_of(ph):
                return lambda t: chain(NODES[ph], t, range(B, B + M), False)

            def fresh():
                tables["log_exp"] = False

            each_step(act, "src", lambda t, bs: chain("src", t, bs, True), nodes_of("src"), fresh=fresh)

            def edge_inputs(ph, t, bs, dst):
                per_tile(ph, t, bs, "src_in", ["turned_in"], lambda b: fn(XS[b][:, :], PA[b][:, :], ACT.Copy))
                for b in bs:
                    if ph == "d0" and not (isinstance(t, int) and t == 0):
                        act.wait_ge(kept[b], t * (4 * KEEPS[ph]) + (1 + before(KEEPS, ph, b)))
                    wait(act, ph, "turned_dst", t, b)
                    fn(dst[b][:, :], PB[b][:, :], ACT.Copy).then_inc(S["x_in"], 1)
                per_tile(ph, t, bs, "edge_in", ["turned_edge"], lambda b: fn(EF[b][:, :], PA[b][:, :], ACT.Copy))

            def d0(t, bs):
                edge_inputs("d0", t, bs, X)
                yield
                yield
                yield
                yield
                log_exp_tables()
                per_tile("d0", t, bs, "weight_exp", ["new_weight"], lambda b: fn(R[b][:, :], R[b][:, :], ACT.Exp))
                per_tile("d0", t, bs, "decay_exp", ["max_shift"], lambda b: fn(DC[b][:, :], DC[b][:, :], ACT.Exp))
                for b in bs:
                    wait_scans(act, "d0", t, b, 2)
                    act.wait_ge(kept[b], t * (4 * KEEPS["d0"]) + 1)
                    fn(MSG[b][:, :], DEG[b][:, :], ACT.Ln).then_inc(S["log_degree"], 1)
                per_tile("d0", t, bs, "inv_degree", ["log_degree"],
                         lambda b: fn(MSG[b][:, :], MSG[b][:, :], ACT.Exp, scale=-1.0))
                yield
                yield
                log_exp_tables()
                for b in bs:
                    wait_scans(act, "d0", t, b, 3)
                    wait(act, "d0", "logits", t, b)
                    fn(W[b][:, :], DN[b][:, :], ACT.Ln).then_inc(S["log_den"], 1)
                per_tile("d0", t, bs, "inv_den", ["log_den"],
                         lambda b: fn(W[b][:, :], W[b][:, :], ACT.Exp, scale=-1.0))
                yield
                norm_of("d0", t, bs, 0)
                yield
                rows_out("d0", t, bs, 1, 0)
                yield
            each_step(act, "d0", d0, nodes_of("d0"), fresh=fresh)

            def sage_phase(ph, i):
                def rounds(t, bs):
                    yield
                    norm_of(ph, t, bs, 1 + i)
                    yield
                    if i == 2:
                        norm_of(ph, t, bs, 4)
                        yield
                    rows_out(ph, t, bs, 4 if i == 2 else 2 + i, 0)
                    yield
                each_step(act, ph, rounds, nodes_of(ph), fresh=fresh)
            for i in range(3):
                sage_phase(f"d{1 + i}", i)

            def gru_phase(ph, r):
                def rounds(t, bs):
                    yield
                    per_tile(ph, t, bs, "message_in", ["message"], lambda b: fn(MSG[b][:, :], PA[b][:, :], ACT.Copy))
                    yield
                    gates(ph, t, bs, r, True)
                    yield
                    if r == 1:
                        norm_of(ph, t, bs, 5)
                        yield
                    rows_out(ph, t, bs, 5 + r, 0)
                    yield
                each_step(act, ph, rounds, nodes_of(ph), fresh=fresh)
            gru_phase("d4", 0)
            gru_phase("d5", 1)

            def d6(t, bs):
                edge_inputs("d6", t, bs, Y)
                yield
                for h, (bank, hid) in enumerate(((PA, Z), (PB, W))):
                    per_tile("d6", t, bs, f"hidden_relu{h}", ["hidden_mm"],
                             lambda b: fn(hid[b][:, :], bank[b][:, :], ACT.Relu, bias=b1col[:, :]))
                yield
                yield
                norm_of("d6", t, bs, 6, "6d")
                yield
                rows_out("d6", t, bs, 7, 0)
                yield
            each_step(act, "d6", d6, peel=True, fresh=fresh)

        @block.vector
        def _(dve):
            v = nc.vector

            dve.wait_ge(zeroed, 1)
            v.memset(ones_block[:, :], 0.0).then_inc(consts, 1)
            v.memset(ones[:, :], 1.0)
            v.memset(eps[:, :], EPS)
            dve.wait_ge(consts, 1)
            for h in range(H):
                last = v.memset(ones_block[h * D:h * D + D, h * D:h * D + D], 1.0)
            last.then_inc(id_steps, 1)
            dve.wait_ge(id_steps, 1)
            v.tensor_scalar(mean_block[:, :], ones_block[:, :], 1.0 / D, None, ALU.mult).then_inc(id_steps, 1)
            dve.wait_ge(id_steps, 2)
            dve.wait_ge(zeroed, 2)
            v.tensor_tensor(centre[:, :], ident[:, :], mean_block[:, :], ALU.subtract).then_inc(consts, 1)
            dve.wait_ge(prep_pe, 1)
            v.tensor_copy(bias[:, :], PA[B][:, 0:32]).then_inc(id_steps, 1)
            dve.wait_ge(id_steps, 3)
            v.tensor_scalar(att_f[:, :], ones_block[:, :], bcol["att_f"], None, ALU.mult)
            v.tensor_scalar(att_r[:, :], ones_block[:, :], bcol["att_r"], None, ALU.mult)
            i = cols.index("b3")
            v.tensor_tensor(bias[:, i:i + 1], bcol["bn"], bcol["b2"], ALU.add)
            for r in range(2):
                for k, g in enumerate("rz"):
                    v.tensor_tensor(gate_b[:, 2 * r + k:2 * r + k + 1], bcol[f"ih_{g}{r}"], bcol[f"hh_{g}{r}"], ALU.add)
            v.tensor_copy(wturned[:, 0:Q, :], PA[0][:, :].rearrange("p (a b) -> p a b", a=Q))
            v.tensor_copy(wturned[:, 8:NT, :], PA[1][:, 0:2 * P].rearrange("p (a b) -> p a b", a=2))
            v.tensor_copy(wturned[:, Q:7, :], PB[0][:, 0:3 * P].rearrange("p (a b) -> p a b", a=3))
            v.tensor_tensor(wturned[:, 7, :], PB[0][:, 3 * P:4 * P], ident[:, :], ALU.add).then_inc(prep_dve, 1)
            dve.wait_ge(prep_pe, 2)
            v.tensor_copy(wcentred[:, 0:Q, :], PB[1][:, :].rearrange("p (a b) -> p a b", a=Q))
            v.tensor_copy(wcentred[:, Q:8, :], PA[2][:, :].rearrange("p (a b) -> p a b", a=Q))
            v.tensor_copy(wcentred[:, 8, :], PB[2][:, 0:P])
            v.tensor_copy(bcent[:, :], PB[2][:, P:P + NC]).then_inc(prep_dve, 1)
            for b in range(2):
                for buf in (MX, DN, AG, EF):
                    v.memset(buf[b][:, :], 0.0)
            for b in range(B):
                v.memset(DEG[b][:, :], 0.0)
                last = v.memset(edges[b][:, :], 0.0)
            last.then_inc(prep_dve, 1)

            g = lambda n: ids[n][:, :]
            dve.wait_ge(ids_in, 16 * n_id_loads)
            dve.wait_ge(iota_done, 1)
            v.tensor_tensor(idf[:, :], g("dst_of"), g("dst_next"), ALU.is_equal)
            v.tensor_scalar(g("dst_row"), g("dst_of"), 0.0, None, ALU.max).then_inc(ids_ready, 1)
            dve.wait_ge(ids_ready, 1)
            v.scalar_tensor_tensor(g("put_row"), idf[:, :], float(OUTSIDE), g("dst_of"), ALU.mult, ALU.add)\
                .then_inc(ids_ready, 1)

            def norm_of(ph, t, bs, l, dst, bias_id=None):
                c = norm_bias[l if bias_id is None else bias_id]
                for b in bs:
                    wait(dve, ph, f"rstd{l}", t, b)
                    v.scalar_tensor_tensor(dst[b][:, :], PA[b][:, :], bcent[:, c:c + 1], R[b][:, :], ALU.add, ALU.mult)\
                        .then_inc(sem_of(ph, "normed"), per(ph))

            def sage_layer(ph, t, bs, i):
                for b in bs:
                    norm_of(ph, t, [b], 1 + i, Z)
                    wait(dve, ph, f"normed{1 + i}", t, b)
                    v.tensor_scalar(Z[b][:, :], Z[b][:, :], bcol[f"g{i}"], bcol[f"be{i}"], ALU.mult, ALU.add)\
                        .then_inc(sem_of(ph, "scaled_norm"), per(ph))
                    wait(dve, ph, f"scaled_norm{i}", t, b)
                    if i == 0:
                        v.tensor_scalar(Z[b][:, :], Z[b][:, :], 0.0, bcol["bres"], ALU.max, ALU.add)\
                            .then_inc(sem_of(ph, "relu"), per(ph))
                        wait(dve, ph, "relu", t, b)
                        wait(dve, ph, "residual_mm", t, b)
                        op = v.tensor_tensor(Y[b][:, :], PB[b][:, :], Z[b][:, :], ALU.add)
                    else:
                        op = v.scalar_tensor_tensor(Y[b][:, :], Z[b][:, :], 0.0, Y[b][:, :], ALU.max, ALU.add)
                    op.then_inc(sem_of(ph, "added"), per(ph))

            def gates(ph, t, bs, r, msg):
                st = X if r == 0 else Y
                tmp = Y if r == 0 else W
                for b in bs:
                    wait(dve, ph, f"gate_n{r}", t, b)
                    v.scalar_tensor_tensor(R[b][:, :], PA[b][:, :], bcol[f"hh_n{r}"], R[b][:, :], ALU.add, ALU.mult)\
                        .then_inc(sem_of(ph, "reset"), per(ph))
                    if msg:
                        wait(dve, ph, f"reset{r}", t, b)
                        v.tensor_tensor(R[b][:, :], PB[b][:, :], R[b][:, :], ALU.add)\
                            .then_inc(sem_of(ph, "reset_sum"), per(ph))
                for b in bs:
                    wait(dve, ph, f"tanh{r}", t, b)
                    v.tensor_tensor(tmp[b][:, :], st[b][:, :], R[b][:, :], ALU.subtract)\
                        .then_inc(sem_of(ph, "diff"), per(ph))
                for b in bs:
                    wait(dve, ph, f"diff{r}", t, b)
                    v.tensor_tensor(tmp[b][:, :], tmp[b][:, :], Z[b][:, :], ALU.mult)\
                        .then_inc(sem_of(ph, "scaled"), per(ph))
                for b in bs:
                    wait(dve, ph, f"scaled{r}", t, b)
                    v.tensor_tensor(Y[b][:, :], tmp[b][:, :], R[b][:, :], ALU.add)\
                        .then_inc(sem_of(ph, "hidden"), per(ph))
                if r == 1:
                    for b in bs:
                        wait(dve, ph, "hidden1", t, b)
                        v.tensor_tensor(Y[b][:, :], Y[b][:, :], X[b][:, :], ALU.add)\
                            .then_inc(sem_of(ph, "summed"), per(ph))

            def chain(ph, t, bs):
                if not is_nodes(ph):
                    yield
                norm_of(ph, t, bs, 0, X)
                yield
                for i in range(3):
                    sage_layer(ph, t, bs, i)
                    yield
                norm_of(ph, t, bs, 4, X)
                yield
                for r in range(2):
                    gates(ph, t, bs, r, False)
                    yield
                norm_of(ph, t, bs, 5, X)
                yield
                if is_nodes(ph):
                    norm_of(ph, t, bs, 6, X)
                yield

            def nodes_of(ph):
                return lambda t: chain(NODES[ph], t, range(B, B + M))

            each_step(dve, "src", lambda t, bs: chain("src", t, bs), nodes_of("src"))

            def scan(ph, t, b, k, dst, decay, data, op0=ALU.mult, op1=ALU.add, shift=0):
                scans = scan_base[ph][1]
                last = COLS - 1 + shift
                for h in range(H):
                    r, other = slice(h * D, h * D + D), slice((1 - h) * D, (1 - h) * D + D)
                    from_ = dst[(b - 1) % B] if h == 0 else dst[b]
                    n = scan_place(ph, t, b, k) + h
                    dve.wait_ge(scanned, t * (2 * scans) + (n + 1))
                    v.tensor_copy(carry[r, :], from_[other, last:last + 1]).then_inc(carried, 1)
                    dve.wait_ge(carried, t * (2 * scans) + (n + 1))
                    v.tensor_tensor_scan(dst[b][r, shift:shift + COLS], decay[b][r, :], data(b)[r, :], carry[r, :],
                                         op0, op1).then_inc(scanned, 1)

            def d0(t, bs):
                ph = "d0"
                for b in bs:
                    wait_loaded(dve, ph, t, b)
                    if not (isinstance(t, int) and t == 0):
                        dve.wait_ge(kept[b], t * (4 * KEEPS[ph]) + 1)
                    v.tensor_tensor(SAME[b][:, :], IDS[b][:, 0:COLS], IDS[b][:, 1:COLS + 1], ALU.is_equal)\
                        .then_inc(S["same"], 1)
                yield
                for b in bs:
                    wait(dve, ph, "hidden_mm", t, b)
                    wait(dve, ph, "x_in", t, b)
                    v.tensor_scalar(Z[b][:, :], PA[b][:, :], 0.01, None, ALU.mult).then_inc(S["small_slope"], 1)
                    v.scalar_tensor_tensor(W[b][:, :], X[b][:, :], 0.01, X[b][:, :], ALU.mult, ALU.max)
                    wait(dve, ph, "small_slope", t, b)
                    v.tensor_tensor(Z[b][:, :], PA[b][:, :], Z[b][:, :], ALU.max).then_inc(S["leaky"], 1)
                    wait(dve, ph, "same", t, b)
                    v.tensor_scalar(R[b][:, :], SAME[b][:, :], -1.0, BIG, ALU.add, ALU.mult).then_inc(S["penalty"], 1)
                yield
                for i in range(2):
                    if i < len(bs):
                        b = bs[i]
                        wait(dve, ph, "logits", t, b)
                        wait(dve, ph, "penalty", t, b)
                        scan(ph, t, b, 0, MX, R, lambda b: PB[b], ALU.add, ALU.max, shift=1)
                        wait_scans(dve, ph, t, b, 1)
                        for h in range(H):
                            r, other = slice(h * D, h * D + D), slice((1 - h) * D, (1 - h) * D + D)
                            from_ = MX[(b - 1) % B] if h == 0 else MX[b]
                            last = v.tensor_copy(MX[b][r, 0:1], from_[other, COLS:COLS + 1])
                        last.then_inc(S["max_before"], 1)
                        v.tensor_tensor(R[b][:, :], PB[b][:, :], MX[b][:, 1:COLS + 1], ALU.subtract)\
                            .then_inc(S["new_weight"], 1)
                        wait(dve, ph, "max_before", t, b)
                        v.tensor_tensor(DC[b][:, :], MX[b][:, 0:COLS], MX[b][:, 1:COLS + 1], ALU.subtract)\
                            .then_inc(S["max_step"], 1)
                        wait(dve, ph, "max_step", t, b)
                        v.tensor_scalar(DC[b][:, :], DC[b][:, :], 0.0, None, ALU.min).then_inc(S["max_shift"], 1)
                        scan(ph, t, b, 1, DEG, SAME, lambda b: ones)
                    yield
                for i in range(2):
                    if i < len(bs):
                        b = bs[i]
                        wait(dve, ph, "decay_exp", t, b)
                        v.tensor_tensor(DC[b][:, :], DC[b][:, :], SAME[b][:, :], ALU.mult)
                        wait(dve, ph, "weight_exp", t, b)
                        v.tensor_tensor(Z[b][:, :], R[b][:, :], XS[b][:, :], ALU.mult).then_inc(S["weighted"], 1)
                        wait(dve, ph, "weighted", t, b)
                        scan(ph, t, b, 2, DN, DC, lambda b: R[b])
                        scan(ph, t, b, 3, AG_n, DC, lambda b: Z[b])
                    yield
                for b in bs:
                    wait_scans(dve, ph, t, b, 4)
                    wait(dve, ph, "inv_den", t, b)
                    v.tensor_tensor(AG[b][:, :], AG_n[b][:, :], W[b][:, :], ALU.mult).then_inc(S["mixed"], 1)
                yield
                norm_of(ph, t, bs, 0, X)
                yield
                yield
            AG_n = Y
            each_step(dve, "d0", d0, nodes_of("d0"))

            dve.wait_ge(map_copied, 1 + 2 * TE)
            v.tensor_scalar(idf[:, :], g("src_map"), 0.0, None, ALU.is_equal)
            v.tensor_scalar(idf2[:, :], g("slot1"), float(SLOTS), None, ALU.add).then_inc(ids_ready, 1)
            dve.wait_ge(ids_ready, 3)
            v.tensor_tensor(idf2[:, :], idf2[:, :], idf[:, :], ALU.mult).then_inc(ids_ready, 1)
            dve.wait_ge(ids_ready, 4)
            v.scalar_tensor_tensor(g("src_slot"), g("src_map"), -1.0, idf2[:, :], ALU.add, ALU.add)
            v.tensor_scalar(g("dst_slot"), g("dst_map"), -1.0, 0.0, ALU.add, ALU.max).then_inc(ids_ready, 1)

            def gather_scan(ph, t, bs, invert):
                for b in bs:
                    wait_loaded(dve, ph, t, b)
                    wait(dve, ph, "turned_in", t, b)
                    scan(ph, t, b, 0, AGS, SAME, lambda b: PA[b])
                    if invert:
                        wait_scans(dve, ph, t, b, 1)
                        v.tensor_tensor(AG[b][:, :], AGS[b][:, :], DEG[b][:, :], ALU.mult).then_inc(S["mean"], 1)
            AGS = DN

            def sage_phase(ph, i):
                def rounds(t, bs):
                    gather_scan(ph, t, bs, True)
                    yield
                    sage_layer(ph, t, bs, i)
                    yield
                    if i == 2:
                        norm_of(ph, t, bs, 4, X)
                        yield
                    yield
                each_step(dve, ph, rounds, nodes_of(ph))
            for i in range(3):
                sage_phase(f"d{1 + i}", i)

            def gru_phase(ph, r):
                st = X if r == 0 else Y
                def rounds(t, bs):
                    for b in bs:
                        wait_loaded(dve, ph, t, b)
                        v.tensor_tensor(W[b][:, :], st[b][:, :], DEG[b][:, :], ALU.mult)\
                            .then_inc(S["times_degree"], 1)
                        wait(dve, ph, "turned_in", t, b)
                        scan(ph, t, b, 0, AG, SAME, lambda b: PA[b])
                        wait(dve, ph, "turned_edge", t, b)
                        scan(ph, t, b, 1, EF, SAME, lambda b: PB[b])
                    yield
                    yield
                    gates(ph, t, bs, r, True)
                    yield
                    if r == 1:
                        norm_of(ph, t, bs, 5, X)
                        yield
                    yield
                each_step(dve, ph, rounds, nodes_of(ph))
            for b in range(B):
                last = v.memset(edges[b][:, :].rearrange("p (s f) -> p s f", f=D)[:, :, 4:5], 1.0)
            last.then_inc(ones_set, 1)
            gru_phase("d4", 0)
            gru_phase("d5", 1)

            def d6(t, bs):
                yield
                yield
                for b in bs:
                    wait_loaded(dve, "d6", t, b)
                    wait(dve, "d6", "message", t, b)
                    scan("d6", t, b, 0, AGS, SAME, lambda b: PA[b])
                    wait_scans(dve, "d6", t, b, 1)
                    v.tensor_tensor(AG[b][:, :], AGS[b][:, :], DEG[b][:, :], ALU.mult).then_inc(S["mean"], 1)
                yield
                norm_of("d6", t, bs, 6, X, "6d")
                yield
                yield
            each_step(dve, "d6", d6)

        @block.sync
        def _(sp):
            dma = nc.sync.dma_start
            FW = TE * 8 + 1
            sp.wait_ge(fills, 3)
            dma(dst_pad.rearrange("(p c) -> p c", p=P), fill[:, 0, :]).then_inc(pad_filled, 16)
            dma(src_pad.rearrange("(p c) -> p c", p=P), fill[:, 1, 0:FW - 1]).then_inc(pad_filled, 16)
            dma(node_slot.rearrange("(p c) o -> p (c o)", p=80), zero_map[:, :]).then_inc(map_zero, 16)

            def node_rows(first, m):
                if isinstance(first, int):
                    first = min(first + m * TILE, N - TILE)
                    return bass.ds(first, TILE)
                return bass.ds(first + m * TILE, TILE)

            def first_node(ph, at):
                return node_place(ph, at, M * TILE)

            def is_last(ph, at):
                return isinstance(at[0], int) and first_node(ph, at) == (TM - M) * TILE

            def load_nodes(first):
                for m in range(M):
                    dma(rows[B + m][:, :], a["x"][node_rows(first, m), :].rearrange("(p j) f -> p (j f)", p=P))\
                        .then_inc(loaded[B + m], 16)

            sp.wait_ge(pad_filled, 32)
            dma(dst_pad[1:1 + E].rearrange("(a c) -> a c", a=8), a["dst"].rearrange("(a c) -> a c", a=8))\
                .then_inc(pad_put, 16)
            dma(src_pad[0:E].rearrange("(a c) -> a c", a=8), a["src"].rearrange("(a c) -> a c", a=8))\
                .then_inc(pad_put, 16)
            sp.wait_ge(pad_put, 32)
            for name, src, off in (("dst_of", dst_pad, 1), ("dst_next", dst_pad, 2), ("src_of", src_pad, 0)):
                v = src[off:off + SLOTS].rearrange("(g h p q) -> h p g q", h=H, p=P, q=Q)
                for h in range(H):
                    dma(ids[name][:, :].rearrange("p (g h q) -> p g h q", h=H, q=Q)[:, :, h, :], v[h]).then_inc(ids_in, 16)
            dma(ids["src_rows"][:, :].rearrange("p (g j) -> p g j", j=8),
                src_pad[0:SLOTS].rearrange("(g p j) -> p g j", p=P, j=8)).then_inc(ids_in, 16)
            sp.wait_ge(zeroed, 1)
            for to, from_ in weight_loads[::2]:
                dma(to, from_).then_inc(weights_in, 16)

            load_nodes(0)

            def next_nodes(ph, at):
                ph = NODES[ph]
                if not is_last(ph, at):
                    wait(sp, ph, "turned_in", at, B + M - 1)
                    settle(sp)
                    load_nodes(first_node(ph, (at[0], at[1] + 1)))

            def store_nodes(ph, at):
                ph = NODES[ph]
                for m in range(M):
                    b = B + m
                    wait(sp, ph, "rows_out7", at, b)
                    settle(sp)
                    if is_last(ph, at) and m == M - 1:
                        for c in range(M):
                            sp.wait_ge(stored[B + c], 16 * (TM // M - (c == m)) + 1)
                    dma(out[node_rows(first_node(ph, at), m), :].rearrange("(p j) f -> p (j f)", p=P), rows_o[b][:, :])\
                        .then_inc(stored[b], 16)

            def each_step_of_sp(ph, load, store, ready, stores_before):
                ready()
                load(0, range(0, 2))
                if stores_before is not None:
                    store_nodes(stores_before, (TE - 1, 0))
                fours, batches = STEP[ph]

                def step(t):
                    for i in range(fours):
                        at = t + i * B
                        load(at, range(2, B))
                        if i == 0 and batches:
                            next_nodes(ph, (t, 0))
                        store(at, range(0, 2))
                        if batches == 2:
                            store_nodes(ph, (t, 0))
                            next_nodes(ph, (t, 1))
                        last = isinstance(at, int) and at == TE - 1 - B
                        load(at + B, range(0, 1 if last else 2))
                        store(at, range(2, B))
                    if batches:
                        store_nodes(ph, (t, batches - 1))
                with sp.Fori(0, TE - 2 * fours * B, fours * B) as t:
                    step(t)
                step(TE - 1 - fours * B)
                if batches:
                    next_nodes(ph, (TE - 1, 0))
                store(TE - 1, range(0, 1))

            def tile_rows(n):
                return bass.ds(n * P, P)

            def store_level(ph, t, b, level, order):
                wait(sp, ph, f"rows_out{level}", t, b)
                settle(sp)
                if order == "any":
                    to = table[level][bass.ds((t + b) * TILE + SLOTS, TILE), :]
                    dma(to.rearrange("(p j) f -> p (j f)", p=P), rows_o[b][:, :]).then_inc(stored[b], 16)
                else:
                    for h in range(H):
                        to = table[level][bass.ds((t + b) * TILE + h * COLS, COLS), :]
                        dma(to.rearrange("(p q) f -> p q f", q=Q),
                            rows_o[b][:, :].rearrange("p (q h f) -> p q h f", h=H, q=Q)[:, :, h, :]).then_inc(stored[b], 16)

            def src_stores(t, bs):
                for level in range(1, 7):
                    for b in bs:
                        store_level("src", t, b, level, "any")
            each_step_of_sp("src", lambda t, bs: None, src_stores, lambda: None, None)

            def load_edges(t, b, attr):
                w = attr.shape[1]
                to = edges[b][:, :].rearrange("p (q h f) -> p q h f", h=H, q=Q)
                short = isinstance(t, int) and t + b == TE - 1
                for h in range(H):
                    if short:
                        from_ = attr[(TE - 1) * TILE:E, :].rearrange("(p q) f -> p q f", q=Q)
                        dma(to[0:LAST_P, :, h, 0:w], from_).then_inc(loaded[b], 16)
                    else:
                        from_ = attr[bass.ds((t + b) * TILE + h * COLS, COLS), :].rearrange("(p q) f -> p q f", q=Q)
                        dma(to[:, :, h, 0:w], from_).then_inc(loaded[b], 16)

            def load_d0(t, bs):
                for b in bs:
                    wait_before(sp, "d0", "turned_out1", t, b)
                    settle(sp)
                    for h in range(H):
                        ids_of = dst_pad[bass.ds((t + b) * TILE + h * COLS, COLS + 1)]
                        dma(IDS[b][h * D:h * D + D, :],
                            ids_of.rearrange("(o c) -> o c", o=1).to_broadcast([D, COLS + 1])).then_inc(loaded[b], 16)
                    load_edges(t, b, a["edge_attr_16"])

            def store_d0(t, bs):
                for b in bs:
                    for what, buf, stage in ((same_d, SAME, "same"), (degree_d, DEG, "inv_degree"),
                                             (inv_degree_d, MSG, "inv_degree"), (state[1], X, "normed0")):
                        wait(sp, "d0", stage, t, b)
                        settle(sp)
                        dma(what[tile_rows(t + b), :], buf[b][:, :]).then_inc(kept[b], 16)
                    store_level("d0", t, b, 1, "edge")
            wait_phase(sp, "src", "turned_out6")
            sp.wait_ge(prep_dve, 3)
            each_step_of_sp("d0", load_d0, store_d0, lambda: None, "src")

            def phase(ph, ready, loads, attr, level, keep):
                after = {2: "added0", 3: "added1", 4: "normed4", 5: "hidden0", 6: "normed5"}.get(level)

                def load(t, bs):
                    for b in bs:
                        wait_before(sp, ph, f"turned_out{level}", t, b)
                        settle(sp)
                        if keep is not None:
                            sp.wait_ge(kept[b], t * (4 * KEEPS[ph]) + (1 + before(KEEPS, ph, b)))
                            settle(sp)
                        for from_, buf in loads:
                            dma(buf[b][:, :], from_[tile_rows(t + b), :]).then_inc(loaded[b], 16)
                        if attr is not None:
                            load_edges(t, b, attr)

                def store(t, bs):
                    if keep is not None:
                        for b in bs:
                            wait(sp, ph, after, t, b)
                            settle(sp)
                            dma(state[level][tile_rows(t + b), :], keep[b][:, :]).then_inc(kept[b], 16)
                            store_level(ph, t, b, level, "edge")
                each_step_of_sp(ph, load, store, lambda: phase_over(*ready), ready[0])

            def phase_over(ph, level):
                wait_phase(sp, ph, f"turned_out{level}")
                for b in range(B):
                    sp.wait_ge(kept[b], 1 + before(KEEPS, ph, b) + 16 * KEEPS[ph] * slot_uses(ph, b))

            phase("d1", ("d0", 1), [(state[1], X), (same_d, SAME), (inv_degree_d, DEG)], None, 2, Y)
            phase("d2", ("d1", 2), [(state[2], Y), (same_d, SAME), (inv_degree_d, DEG)], None, 3, Y)
            phase("d3", ("d2", 3), [(state[1], X), (state[3], Y), (same_d, SAME), (inv_degree_d, DEG)], None, 4, X)
            phase("d4", ("d3", 4), [(state[4], X), (same_d, SAME), (degree_d, DEG)], a["edge_attr_4"], 5, Y)
            phase("d5", ("d4", 5), [(state[4], X), (state[5], Y), (same_d, SAME), (degree_d, DEG)],
                  a["edge_attr_4"], 6, X)
            phase("d6", ("d5", 6), [(state[6], X), (same_d, SAME), (inv_degree_d, DEG)], a["edge_attr_32"], 7, None)
            for b in range(B):
                sp.wait_ge(stored[b], before(STORES, "d6", b) + 1)
            for b in range(B, B + M):
                sp.wait_ge(stored[b], 16 * (TM // M) + 1)

        @block.gpsimd
        def _(gp):
            g = nc.gpsimd
            for s in kept + stored + [map_copied, scanned]:
                gp.sem_inc(s, 1)
            g.memset(fill[:, 0, :], -1).then_inc(fills, 1)
            g.memset(fill[:, 1, :], 0).then_inc(fills, 1)
            g.memset(zero_map[:, :], 0).then_inc(fills, 1)
            g.memset(wraw[:, :, :], 0.0)
            g.memset(bias_rows[:, :], 0.0)
            g.memset(w3e[:, :], 0.0).then_inc(zeroed, 1)
            g.memset(ident[:, :], 0.0).then_inc(ident_zero, 1)
            gp.wait_ge(ident_zero, 1)
            g.affine_select(out=ident[:, :], in_=ident[:, :], compare_op=ALU.not_equal, fill=1.0, base=0,
                            pattern=[[-1, P]], channel_multiplier=1).then_inc(zeroed, 1)
            g.iota(ids["slot1"][:, :], [[TILE, TE], [COLS, H], [1, Q]], base=1, channel_multiplier=Q)\
                .then_inc(iota_done, 1)

            def stage_ids(at, b, t, per_tile, done, pairs):
                settle(gp)
                for to, name in pairs:
                    g.tensor_copy(to, ids[name][:, bass.ds((at + b) * 8, 8)]).then_inc(staged, 1)
                gp.wait_ge(staged, t * per_tile + done)
                settle(gp)

            def column_of(idx, k):
                return bass.IndirectOffsetOnAxis(ap=idx[:, k:k + 1], axis=0)

            def each_batch(body):
                with gp.Fori(0, TE - B, B) as t:
                    body(t, B)
                body(TE - 1, 1)

            def put_tile(at, j, staged_then):
                b = j % B
                if not (isinstance(at, int) and at + j < B):
                    gp.wait_ge(map_put[b], at * (16 * 8 // B) + 16 * 8 * (j // B))
                stage_ids(at, j, *staged_then, [(mi[b][:, 0:8], "put_row"), (gv[b][:, 0:8], "slot1")])
                for k in range(8):
                    g.indirect_dma_start(node_slot, column_of(mi[b], k), gv[b][:, k:k + 1], None,
                                         bounds_check=N - 1, oob_is_err=False).then_inc(map_put[b], 16)

            def get_tile(at, j, staged_then):
                b = j % B
                gp.wait_ge(map_copied, at * 2 + (2 * B * (j // B) + 1))
                stage_ids(at, j, *staged_then, [(mi[b][:, 0:8], "src_of"), (mi[b][:, 8:16], "dst_row")])
                for k in range(16):
                    g.indirect_dma_start(gv[b][:, k:k + 1], None, node_slot, column_of(mi[b], k))\
                        .then_inc(map_got[b], 16)

            def copy_tile(at, j):
                b = j % B
                gp.wait_ge(map_got[b], at * (16 * 16 // B) + 16 * 16 * (j // B + 1))
                settle(gp)
                for k, name in enumerate(("src_map", "dst_map")):
                    g.tensor_copy(ids[name][:, bass.ds((at + j) * 8, 8)], gv[b][:, 8 * k:8 * k + 8])\
                        .then_inc(map_copied, 1)

            def gather_tile(ph, sources, t, b, per_tile, done):
                if not (isinstance(t, int) and ph == "src" and t == 0):
                    gp.wait_ge(gathered[b], t * (4 * GATHERS[ph]) + before(GATHERS, ph, b))
                    if ph == "src":
                        gp.wait_ge(S["turned_in"], t + (b // 2 * 2 - B + b % 2 + 1))
                    else:
                        wait_before(gp, ph, "turned_in", t, b)
                stage_ids(t, b, t, per_tile, done, [(gi[b][:, 8 * k:8 * k + 8], s[0]) for k, s in enumerate(sources)])
                for k, (name, from_, to, order) in enumerate(sources):
                    for j in range(8):
                        c = j if order == "any" else (j % Q) * H + j // Q
                        g.indirect_dma_start(to[b][:, c * D:c * D + D], None, from_, column_of(gi[b], 8 * k + j))\
                            .then_inc(gathered[b], 16)

            HALF = (TE - 1) // 2
            def src_tile(t, b, done):
                gather_tile("src", [("src_rows", a["x"], rows, "any")], t, b, 5, done)

            def put_step(t):
                for b in range(B):
                    src_tile(t, b, b + 1)
                for j in range(2 * B):
                    put_tile(t * 2, j, (t, 5, B + 2 * (j + 1)))

            def get_step(t):
                for b in range(B):
                    src_tile(t, b, 5 * b + 3)
                    for j in (2 * b, 2 * b + 1):
                        get_tile(t * 2 - 2 * HALF, j, (t, 5, 5 * b + 3 + 2 * (j % 2 + 1)))
                    if b % 2 == 1:
                        for j in range(2 * b - 2, 2 * b + 2):
                            copy_tile(t * 2 - 2 * HALF, j)
            assert HALF % B == 0
            gp.wait_ge(ids_ready, 2)
            gp.wait_ge(map_zero, 16)
            put_step(0)
            with gp.Fori(B, HALF - B + 1, B) as t:
                put_step(t)
            put_tile(2 * HALF, 0, (HALF, 5, 2))
            for b in range(B):
                gp.wait_ge(map_put[b], 16 * 8 * slot_uses("src", b))
            with gp.Fori(HALF, TE - B, B) as t:
                get_step(t)
            src_tile(TE - 1, 0, 3)
            get_tile(TE - 1, 0, (TE - 1, 5, 5))
            copy_tile(TE - 1, 0)

            def d0_step(t, nb):
                for b in range(nb):
                    gather_tile("d0", [("src_of", a["x"], rows, "edge"), ("dst_row", a["x"], rows2, "edge")], t, b,
                                2, 5 * TE + 2 * (b + 1))
            wait_phase(gp, "src", "turned_in")
            each_batch(d0_step)
            gp.wait_ge(ids_ready, 5)

            def table_ready(level, ph):
                for b in range(B):
                    gp.wait_ge(stored[b], before(STORES, ph, b) + 16 * STORES[ph] * slot_uses(ph, b) + 1)

            for k in range(1, 6):
                def step(t, nb):
                    for b in range(nb):
                        gather_tile(f"d{k}", [("src_slot", table[k], rows, "edge")], t, b, 1, (6 + k) * TE + b + 1)
                table_ready(k, f"d{k - 1}")
                each_batch(step)
            table_ready(6, "d5")

            sources = [("src_slot", table[6], rows, "edge"), ("dst_slot", table[6], rows2, "edge")]
            PER = 3

            def last_gather(t, b, n):
                gp.wait_ge(gathered[b], t * (4 * GATHERS["d6"]) + (before(GATHERS, "d6", b)))
                wait_before(gp, "d6", "turned_in", t, b)
                for k, (name, from_, to, order) in enumerate(sources):
                    g.tensor_copy(gi[b][:, 8 * k:8 * k + 8], ids[name][:, bass.ds((t + b) * 8, 8)]).then_inc(staged, 1)
                gp.wait_ge(staged, n)
                settle(gp)
                for k, (name, from_, to, order) in enumerate(sources):
                    for j in range(8):
                        c = (j % Q) * H + j // Q
                        g.indirect_dma_start(to[b][:, c * D:c * D + D], None, from_, column_of(gi[b], 8 * k + j))\
                            .then_inc(gathered[b], 16)

            def last_scatter(t, b, n):
                if not (isinstance(t, int) and t == 0):
                    gp.wait_ge(scattered[b], t * (4 * 8))
                g.tensor_copy(gv[b][:, 0:8], ids["put_row"][:, bass.ds((t + b) * 8, 8)]).then_inc(staged, 1)
                gp.wait_ge(staged, n)
                wait(gp, "d6", "rows_out7", t, b)
                settle(gp)
                for j in range(8):
                    c = (j % Q) * H + j // Q
                    g.indirect_dma_start(out, column_of(gv[b], j), rows_o[b][:, c * D:c * D + D], None,
                                         bounds_check=N - 1, oob_is_err=False).then_inc(scattered[b], 16)

            s0 = 12 * TE
            full = TE - 1
            for b in range(B):
                last_gather(0, b, s0 + 2 * (b + 1))
            s0 += 2 * B

            for b in range(B, B + M):
                gp.wait_ge(stored[b], 16 * (TM // M) + 1)

            def last_batch(t):
                for b in range(B):
                    last_gather(t + B, b, t * PER + (s0 + 2 * (b + 1)))
                for b in range(B):
                    last_scatter(t, b, t * PER + (s0 + 2 * B + b + 1))
            last_batch(0)
            with gp.Fori(B, full - 2 * B + 1, B) as t:
                last_batch(t)
            s0 += PER * (full - B)
            rem = TE - full
            for b in range(rem):
                last_gather(full, b, s0 + 2 * (b + 1))
            for b in range(B):
                last_scatter(full - B, b, s0 + 2 * rem + b + 1)
            for b in range(rem):
                last_scatter(full, b, s0 + 2 * rem + B + b + 1)
            for b in range(B):
                gp.wait_ge(scattered[b], 16 * 8 * slot_uses("d6", b))


def kernel(**inputs):
    import numpy as np
    import concourse.bacc as bacc
    from concourse.bass_utils import run_bass_kernel_spmd

    nc = bacc.Bacc("TRN2", target_bir_lowering=False, num_devices=1)
    arrays = {name: np.ascontiguousarray(x) for name, x in inputs.items()}
    aps = {name: nc.dram_tensor(f"in_{name}", x.shape, mybir.dt.from_np(x.dtype), kind="ExternalInput").ap()
           for name, x in arrays.items()}
    out = nc.dram_tensor("out", arrays["x"].shape, mybir.dt.from_np(arrays["x"].dtype), kind="ExternalOutput").ap()
    build(nc, aps, out)
    result = run_bass_kernel_spmd(nc, [{f"in_{name}": x for name, x in arrays.items()}], core_ids=[0])
    return result.results[0]["out"]
```
